# Optimizing a Trainium2 kernel written in Bass

```python
import numpy as np
import jax
import jax.numpy as jnp

def _softmax(x, axis=-1):
    return jax.nn.softmax(x, axis=axis)

def _gelu(x):
    return jax.nn.gelu(x, approximate=True)

def _silu(x):
    return jax.nn.silu(x)

def _sigmoid(x):
    return jax.nn.sigmoid(x)

def _layernorm(x, axis=-1, eps=1e-05):
    m = jnp.mean(x, axis=axis, keepdims=True)
    v = jnp.var(x, axis=axis, keepdims=True)
    return (x - m) / jnp.sqrt(v + eps)

def _scatter_add(tgt, idx, src, axis=0):
    return tgt.at[idx].add(src)

def _segment_sum(src, seg, n):
    return jax.ops.segment_sum(src, seg, n)
kernel_name = 'mk_gnn_ffn_d1_gnn_r8_ab1101'

def setup_inputs(seed: int=0):
    np.random.seed(seed)
    _w = jnp.asarray

    def _rec_inputs():
        import jax
        import jax.numpy as jnp
        _gk = jax.random.key(seed)
        x = -6.415e-05 + 1 * jax.random.normal(jax.random.fold_in(_gk, 1), (1250, 1024), jnp.float32)
        _s = jax.random.randint(jax.random.fold_in(_gk, 2), (10000,), 0, 1250, jnp.int32)
        _d = jax.random.randint(jax.random.fold_in(_gk, 3), (10000,), 0, 1250, jnp.int32)
        _loop = jnp.arange(1250, dtype=jnp.int32)
        src = jnp.concatenate([_s, _d, _loop])
        dst = jnp.concatenate([_d, _s, _loop])
        _o = jnp.argsort(dst, stable=True)
        src = src[_o]
        dst = dst[_o]
        return (x, src, dst)
    x, src, dst = _rec_inputs()

    def _L0_gnn_setup():
        import jax, jax.numpy as jnp
        import numpy as np
        NEG_SLOPE = 0.1
        EPS = 1e-05
        key = jax.random.key(seed)
        k1, k2, k3, k4, k5 = jax.random.split(key, 5)
        N, E, DIN, DOUT = (1250, 20000, 1024, 1024)
        x = jax.random.normal(k1, (N, DIN), dtype=jnp.float32)
        W = jax.random.normal(k2, (DIN, DOUT), dtype=jnp.float32) * 0.02
        a = jax.random.normal(k3, (1, 2 * DOUT), dtype=jnp.float32) * 0.02
        src = jax.random.randint(k4, (E,), 0, N, dtype=jnp.int64)
        dst = jax.random.randint(k5, (E,), 0, N, dtype=jnp.int64)
        return {'x': x, 'W': W, 'a': a, 'src': src, 'dst': dst}
    _L0_gnn_all = _L0_gnn_setup()
    _L0_gnn_in = {k: v for k, v in _L0_gnn_all.items() if k in ('W', 'a')}
    del _L0_gnn_all

    def _L0_ffn_setup():
        import jax, jax.numpy as jnp
        import numpy as np
        E, H, I = (8, 1024, 512)
        NG, TKG, TOPK = (4, 2, 4)
        SCALE = 2.5

        def _mlp(x, wg, wu, wd):
            return jax.nn.silu(x @ wg) * (x @ wu) @ wd
        key = jax.random.key(seed)
        ks = jax.random.split(key, 8)
        s = 0.02
        return {'hidden_states': jax.random.normal(ks[0], (32, 256, H), jnp.float32), 'gate_w': jax.random.normal(ks[1], (E, H), jnp.float32) * np.float32(np.sqrt(2.0 / H)), 'correction_bias': jnp.zeros((E,), jnp.float32), 'Wg': jax.random.normal(ks[2], (E, H, I), jnp.float32) * s, 'Wu': jax.random.normal(ks[3], (E, H, I), jnp.float32) * s, 'Wd': jax.random.normal(ks[4], (E, I, H), jnp.float32) * s, 'Wg_s': jax.random.normal(ks[5], (H, I), jnp.float32) * s, 'Wu_s': jax.random.normal(ks[6], (H, I), jnp.float32) * s, 'Wd_s': jax.random.normal(ks[7], (I, H), jnp.float32) * s}
    _L0_ffn_all = _L0_ffn_setup()
    _L0_ffn_in = {k: v for k, v in _L0_ffn_all.items() if k in ('gate_w', 'correction_bias', 'Wg', 'Wu', 'Wd', 'Wg_s', 'Wu_s', 'Wd_s')}
    del _L0_ffn_all
    return {'x': x, 'src': src, 'dst': dst, 'L0_gnn_W': _L0_gnn_in['W'], 'L0_gnn_a': _L0_gnn_in['a'], 'L0_ffn_gate_w': _L0_ffn_in['gate_w'], 'L0_ffn_correction_bias': _L0_ffn_in['correction_bias'], 'L0_ffn_Wg': _L0_ffn_in['Wg'], 'L0_ffn_Wu': _L0_ffn_in['Wu'], 'L0_ffn_Wd': _L0_ffn_in['Wd'], 'L0_ffn_Wg_s': _L0_ffn_in['Wg_s'], 'L0_ffn_Wu_s': _L0_ffn_in['Wu_s'], 'L0_ffn_Wd_s': _L0_ffn_in['Wd_s']}

def reference(x, src, dst, L0_gnn_W, L0_gnn_a, L0_ffn_gate_w, L0_ffn_correction_bias, L0_ffn_Wg, L0_ffn_Wu, L0_ffn_Wd, L0_ffn_Wg_s, L0_ffn_Wu_s, L0_ffn_Wd_s):
    import jax
    import jax.numpy as jnp

    def _L0_gnn_ref(x, W, a, src, dst):
        import jax, jax.numpy as jnp
        import numpy as np
        NEG_SLOPE = 0.1
        EPS = 1e-05
        N = x.shape[0]
        d = W.shape[1]
        h = x @ W
        a_l, a_r = (a[0, :d], a[0, d:])
        al = h @ a_l
        ar = h @ a_r
        e = jnp.exp(-jax.nn.leaky_relu(al[src] + ar[dst], negative_slope=NEG_SLOPE))
        rowsum = jax.ops.segment_sum(e, src, num_segments=N)
        h_prime = jax.ops.segment_sum(e[:, None] * h[dst], src, num_segments=N)
        h_prime = h_prime / (rowsum[:, None] + EPS)
        return jax.nn.elu(h_prime)

    def _L0_ffn_ref(hidden_states, gate_w, correction_bias, Wg, Wu, Wd, Wg_s, Wu_s, Wd_s):
        import jax, jax.numpy as jnp
        import numpy as np
        E, H, I = (8, 1024, 512)
        NG, TKG, TOPK = (4, 2, 4)
        SCALE = 2.5

        def _mlp(x, wg, wu, wd):
            return jax.nn.silu(x @ wg) * (x @ wu) @ wd
        B, T, _ = hidden_states.shape
        x = hidden_states.reshape(-1, H)
        N = x.shape[0]
        logits = x @ gate_w.T
        scores = jax.nn.sigmoid(logits)
        scores_c = scores + correction_bias
        grp = scores_c.reshape(N, NG, E // NG)
        group_scores = jnp.sum(jax.lax.top_k(grp, 2)[0], axis=-1)
        grp_idx = jax.lax.top_k(group_scores, TKG)[1]
        group_mask = jnp.zeros_like(group_scores).at[jnp.arange(N)[:, None], grp_idx].set(1.0)
        score_mask = jnp.repeat(group_mask, E // NG, axis=-1) > 0.5
        scores_for_choice = jnp.where(score_mask, scores_c, 0.0)
        topk_idx = jax.lax.top_k(scores_for_choice, TOPK)[1]
        topk_w = jnp.take_along_axis(scores, topk_idx, axis=-1)
        topk_w = topk_w / (jnp.sum(topk_w, axis=-1, keepdims=True) + 1e-20)
        topk_w = topk_w * SCALE
        cw = jnp.sum(jax.nn.one_hot(topk_idx, E, dtype=topk_w.dtype) * topk_w[..., None], axis=1)
        g = jnp.einsum('nh,ehi->eni', x, Wg)
        u = jnp.einsum('nh,ehi->eni', x, Wu)
        y = jnp.einsum('eni,eih->enh', jax.nn.silu(g) * u, Wd)
        routed = jnp.einsum('enh,ne->nh', y, cw)
        out = routed + _mlp(x, Wg_s, Wu_s, Wd_s)
        return out.reshape(B, T, H)
    x = x + _L0_gnn_ref(_layernorm(x, axis=-1), L0_gnn_W, L0_gnn_a, src, dst)
    x = x + _L0_ffn_ref(_layernorm(x, axis=-1)[None], L0_ffn_gate_w, L0_ffn_correction_bias, L0_ffn_Wg, L0_ffn_Wu, L0_ffn_Wd, L0_ffn_Wg_s, L0_ffn_Wu_s, L0_ffn_Wd_s)[0]
    return x

_drawn_inputs = setup_inputs


def setup_inputs(seed=0):
    import zlib

    import numpy as np

    out = dict(_drawn_inputs(seed))
    spreads = {'L0_ffn_correction_bias': (0.0, 0.1)}
    factors = {}
    for name, (base, spread) in spreads.items():
        noise = np.random.default_rng([zlib.crc32(name.encode()), seed]).standard_normal(out[name].shape)
        drawn = base * np.exp(spread * noise) if base else spread * noise
        out[name] = jnp.asarray(drawn.astype(out[name].dtype))
    for name, factor in factors.items():
        out[name] = (out[name] * factor).astype(out[name].dtype)
    return out
```

```python
import concourse.bass as bass
from concourse import mybir

F32 = mybir.dt.float32
F16 = mybir.dt.float16
I32 = mybir.dt.int32
ALU = mybir.AluOpType
ACT = mybir.ActivationFunctionType
X = mybir.AxisListType.X

P = 128
WS = 256.0
AS = 64.0
LN_EPS = 1e-5
SUM_EPS = 1e-5
SLOPE = 0.1
ROUTED_SCALE = 2.5
TOPK = 4
GROUPS = 4
TOP_GROUPS = 2


def build(nc, x_in, src_in, dst_in, w_in, a_in, gate_in, bias_in, wg_in, wu_in, wd_in,
          wgs_in, wus_in, wds_in, out):
    N, D = x_in.shape
    NE = src_in.shape[0]
    E, _, FI = wg_in.shape
    T = -(-N // P)
    NP = T * P
    TAIL = N - (T - 1) * P
    K = D // P
    KI = FI // P
    C = -(-NE // P)
    CB = C - P
    FULL = NE // P
    REST = NE - FULL * P
    HALF = 512
    EG = E // GROUPS
    assert T % 2 == 0 and 0 < CB <= P and D == 2 * HALF and FI == HALF and NP == 2 * HALF + 256
    CH = [(0, HALF), (HALF, HALF), (2 * HALF, NP - 2 * HALF)]
    GRP = len(CH) * KI

    base = nc.sbuf_base + (-nc.sbuf_base) % 64
    cursor = [base]

    def at(name, offset, shape, dt):
        return nc.alloc_sbuf_tensor_at(name, shape, dt, offset=offset)

    def region(nbytes):
        start = cursor[0]
        cursor[0] += nbytes + (-nbytes) % 32
        assert cursor[0] <= nc.sbuf_usable_end, (cursor[0], nc.sbuf_usable_end)
        return start

    R_X = region(T * D * 4)
    R_A = region(T * NP * 4)
    R_B = region(T * D * 4)
    R_C = region(T * D * 4)
    R_D = region(2 * K * FI * 4)
    R_T = region(12288)

    xs = at("xs", R_X, [P, T, D], F32)
    x1T = [at(f"x1T{i}", R_A + i * K * NP * 2, [P, K, NP], F16) for i in range(2)]
    xn1 = at("xn1", R_A + K * NP * 4, [P, 2, D], F32)
    att = [at(f"att{i}", R_A + i * T * NP * 2, [P, T, NP], F16) for i in range(2)]
    hs = [at(f"hs{i}", R_B + i * T * D * 2, [P, T, D], F16) for i in range(2)]
    ws = [at(f"ws{i}", R_C + i * K * D * 2, [P, K, D], F16) for i in range(2)]
    x2T = [at(f"x2T{i}", R_C + i * K * NP * 2, [P, K, NP], F16) for i in range(2)]
    w_stage = at("w_stage", R_D, [P, 2, 2, D], F32)
    h_row = at("h_row", R_D + 16384, [P, D], F32)
    a_rows = at("a_rows", R_D + 20480, [P, 2, D], F32)
    al_row = at("al_row", R_D, [P, NP], F32)
    e_low = at("e_low", R_D + 5120, [P, NP], F32)
    e_high = at("e_high", R_D + 10240, [P, NP], F32)
    att_row = at("att_row", R_D + 15360, [P, NP], F32)
    hot_src = at("hot_src", R_D + 20480, [P, 2, NP], F16)
    hot_dst = at("hot_dst", R_D + 25600, [P, 2, P], F16)
    gu_stage = [at(f"gu_stage{m}", R_D + m * K * FI * 4, [P, K, FI], F32) for m in range(2)]
    gu_w = [[at(f"gu_w{m}{i}", R_A + (2 * m + i) * K * FI * 2, [P, K, FI], F16) for i in range(2)] for m in range(2)]
    d_stage = at("d_stage", R_A + 4 * K * FI * 2, [P, KI, D], F32)
    d_w = [at(f"d_w{i}", R_B + i * KI * D * 2, [P, KI, D], F16) for i in range(2)]
    actT = [at(f"actT{i}", R_B + 2 * KI * D * 2 + i * KI * NP * 2, [P, KI, NP], F16) for i in range(2)]
    elu_neg = at("elu_neg", R_T, [P, D], F32)
    elu_pos = at("elu_pos", R_T + 4096, [P, D], F32)
    xn2 = at("xn2", R_T + 8192, [P, D], F32)
    sig = at("sig", R_T, [P, HALF], F32)
    gated = at("gated", R_T + 2048, [P, HALF], F32)
    act_row = at("act_row", R_T + 4096, [P, HALF], F32)

    def small(name, shape, dt):
        n = 1
        for s in shape[1:]:
            n *= s
        return at(name, region(n * mybir.dt.size(dt)), shape, dt)

    ident = small("ident", [P, P], F32)
    ones = small("ones", [P, P], F32)
    ones16 = small("ones16", [P, 1], F16)
    zero16 = small("zero16", [P, P], F16)
    iota_i = at("iota_i", R_B, [P, NP], I32)
    nodes16 = small("nodes16", [P, NP], F16)
    edges_i = at("edges_i", R_B + 5120, [P, 4, P], I32)
    edges_f = at("edges_f", R_B + 8192, [P, 4, P], F32)
    edgeT = small("edgeT", [P, 4, P], F32)
    gate_rows = at("gate_rows", R_B + 12288, [E, D], F32)
    gateT = [small(f"gateT{i}", [P, K, E], F16) for i in range(2)]
    bias_row = small("bias_row", [P, E], F32)
    stats = small("stats", [P, 2, 2, 6], F32)
    mv = small("mv", [P, 2, 2], F32)
    rs = small("rs", [P, 2, 4], F32)
    mhalf = small("mhalf", [P, 1], F32)
    alr = small("alr", [P, 2, T], F32)
    nar = small("nar", [P, 2, T], F32)
    diag = small("diag", [P, P], F32)
    rsum = small("rsum", [P, 2, 2], F32)
    span = small("span", [P, 2, 2], F32)
    pads = at("pads", R_B + 16384, [P, 2, P], F32)
    pair_i = small("pair_i", [P, 2], I32)
    pair_f = small("pair_f", [P, 2], F32)
    first_i = small("first_i", [P, T], I32)
    first_f = small("first_f", [P, 2, T], F32)
    need = at("need", R_B + 17408, [P, 2, 2, T], F32)
    cand = at("cand", R_B + 18432, [P, 2, 2, T], F32)
    cmax = small("cmax", [P, 1], F32)
    crow = small("crow", [1, 2, T], F32)
    lens = small("lens", [1, T], F32)
    bounds_f = small("bounds_f", [1, 3, T], F32)
    bounds = small("bounds", [1, 3, T], I32)
    R_R = R_B + 2 * KI * D * 2
    rank_a = at("rank_a", R_R, [P, T, E, E], F32)
    rank_b = at("rank_b", R_R + 4 * T * E * E, [P, T, E, E], F32)
    lower = at("lower", R_R + 8 * T * E * E, [P, E, E], F32)
    score = small("score", [P, T, E], F32)
    choice = at("choice", R_R + 8 * T * E * E + 4 * T * E * 4, [P, T, E], F32)
    r1 = at("r1", R_R + 8 * T * E * E + 5 * T * E * 4, [P, T, E], F32)
    r2 = at("r2", R_R + 8 * T * E * E + 6 * T * E * 4, [P, T, E], F32)
    rg = small("rg", [P, T, GROUPS], F32)
    rg2 = small("rg2", [P, T, GROUPS], F32)
    rt = small("rt", [P, T], F32)
    rt2 = small("rt2", [P, T], F32)
    comb = small("comb", [P, T, E + 1], F32)

    bank = nc.alloc_psum_tensor("bank", [P, 8, HALF], F32)
    trans = [bank[:, 2 * b:2 * b + 2, :].rearrange("p a (k n) -> p (a k) n", n=P) for b in range(2)]
    h_acc = [bank[:, 4 + 2 * b:6 + 2 * b, :].rearrange("p a n -> p (a n)") for b in range(2)]
    count_acc = [bank[:, 3 * b:3 * b + 3, :].rearrange("p a n -> p (a n)")[:, 0:NP] for b in range(2)]
    al_acc = count_acc[0]
    prep = bank[:, 7, :]
    agg_acc = [bank[:, 2 * b:2 * b + 2, :].rearrange("p a n -> p (a n)") for b in range(2)]
    sum_acc = bank[:, 4, 0:1]
    logit_acc = bank[:, 5, 0:T * E].rearrange("p (t e) -> p t e", e=E)
    trans2 = bank[:, 6:8, :].rearrange("p a (k n) -> p (a k) n", n=P)
    g_acc = [bank[:, 2 * b, :] for b in range(2)]
    u_acc = [bank[:, 2 * b + 1, :] for b in range(2)]
    y_acc = [bank[:, 4 + 2 * b:6 + 2 * b, :].rearrange("p a n -> p (a n)") for b in range(2)]

    x_tail_zeroed = nc.alloc_semaphore("x_tail_zeroed")
    edges_padded = nc.alloc_semaphore("edges_padded")
    small_loaded = nc.alloc_semaphore("small_loaded")
    edges_loaded = nc.alloc_semaphore("edges_loaded")
    consts_set = nc.alloc_semaphore("consts_set")
    iota_set = nc.alloc_semaphore("iota_set")
    pool_step = nc.alloc_semaphore("pool_step")
    stats_set = nc.alloc_semaphore("stats_set")
    rstd_set = nc.alloc_semaphore("rstd_set")
    norm_set = nc.alloc_semaphore("norm_set")
    trans_set = nc.alloc_semaphore("trans_set")
    hi_set = nc.alloc_semaphore("hi_set")
    lo_set = nc.alloc_semaphore("lo_set")
    w_hi = nc.alloc_semaphore("w_hi")
    w_lo = nc.alloc_semaphore("w_lo")
    h_set = nc.alloc_semaphore("h_set")
    h_hi = nc.alloc_semaphore("h_hi")
    h_lo = nc.alloc_semaphore("h_lo")
    h_rowed = nc.alloc_semaphore("h_rowed")
    al_dotted = nc.alloc_semaphore("al_dotted")
    diag_set = nc.alloc_semaphore("diag_set")
    diag_used = nc.alloc_semaphore("diag_used")
    al_copied = nc.alloc_semaphore("al_copied")
    edges_floated = nc.alloc_semaphore("edges_floated")
    edges_turned = nc.alloc_semaphore("edges_turned")
    edgeT_set = nc.alloc_semaphore("edgeT_set")
    cand_set = nc.alloc_semaphore("cand_set")
    cand_turned = nc.alloc_semaphore("cand_turned")
    cmax_set = nc.alloc_semaphore("cmax_set")
    cmax_turned = nc.alloc_semaphore("cmax_turned")
    bounds_set = nc.alloc_semaphore("bounds_set")
    gate_turned = nc.alloc_semaphore("gate_turned")
    gate_hi = nc.alloc_semaphore("gate_hi")
    gate_lo = nc.alloc_semaphore("gate_lo")
    dve_step = nc.alloc_semaphore("dve_step")
    hot_ready = nc.alloc_semaphore("hot_ready")
    hot_free = nc.alloc_semaphore("hot_free")
    count_set = nc.alloc_semaphore("count_set")
    e_low_set = nc.alloc_semaphore("e_low_set")
    e_high_set = nc.alloc_semaphore("e_high_set")
    att_set = nc.alloc_semaphore("att_set")
    att_hi = nc.alloc_semaphore("att_hi")
    att_lo = nc.alloc_semaphore("att_lo")
    sum_set = nc.alloc_semaphore("sum_set")
    sum_read = nc.alloc_semaphore("sum_read")
    agg_set = nc.alloc_semaphore("agg_set")
    agg_free = nc.alloc_semaphore("agg_free")
    neg_set = nc.alloc_semaphore("neg_set")
    exp_set = nc.alloc_semaphore("exp_set")
    stats2_set = nc.alloc_semaphore("stats2_set")
    rstd2_set = nc.alloc_semaphore("rstd2_set")
    norm2_set = nc.alloc_semaphore("norm2_set")
    trans2_set = nc.alloc_semaphore("trans2_set")
    trans2_hi = nc.alloc_semaphore("trans2_hi")
    trans2_lo = nc.alloc_semaphore("trans2_lo")
    logits_set = nc.alloc_semaphore("logits_set")
    logit_exp = nc.alloc_semaphore("logit_exp")
    agg_done = nc.alloc_semaphore("agg_done")
    gu_loaded0 = nc.alloc_semaphore("gu_loaded0")
    gu_loaded1 = nc.alloc_semaphore("gu_loaded1")
    d_loaded = nc.alloc_semaphore("d_loaded")
    gu_hi = nc.alloc_semaphore("gu_hi")
    gu_lo = nc.alloc_semaphore("gu_lo")
    d_hi = nc.alloc_semaphore("d_hi")
    d_lo = nc.alloc_semaphore("d_lo")
    gu_set = nc.alloc_semaphore("gu_set")
    sig_set = nc.alloc_semaphore("sig_set")
    gated_set = nc.alloc_semaphore("gated_set")
    act_set = nc.alloc_semaphore("act_set")
    act_hi = nc.alloc_semaphore("act_hi")
    act_lo = nc.alloc_semaphore("act_lo")
    y_set = nc.alloc_semaphore("y_set")
    y_banks_free = nc.alloc_semaphore("y_banks_free")
    stored = nc.alloc_semaphore("stored")
    ln_chain = nc.alloc_semaphore("ln_chain")
    acc_chain = nc.alloc_semaphore("acc_chain")
    x_loaded = [nc.alloc_semaphore(f"x_loaded{t}") for t in range(T)]
    w_loaded = [nc.alloc_semaphore(f"w_loaded{b}") for b in range(2)]

    with nc.Block() as block:

        @block.sync
        def _(sp):
            sp.wait_ge(edges_padded, 1)
            for i, e in enumerate((src_in, dst_in)):
                sp.dma_start(edges_i[:, 2 * i, :], e[0:P * P].rearrange("(c e) -> c e", e=P)).then_inc(edges_loaded, 16)
                sp.dma_start(edges_i[0:FULL - P, 2 * i + 1, :],
                             e[P * P:FULL * P].rearrange("(c e) -> c e", e=P)).then_inc(edges_loaded, 16)
                if REST:
                    sp.dma_start(edges_i[FULL - P:FULL - P + 1, 2 * i + 1, 0:REST],
                                 e[FULL * P:NE].rearrange("(c e) -> c e", c=1)).then_inc(edges_loaded, 16)
            for t in range(T):
                if t == T - 1:
                    sp.wait_ge(x_tail_zeroed, 1)
                rows = P if t < T - 1 else TAIL
                sp.dma_start(xs[0:rows, t, :], x_in[t * P:t * P + rows, :]).then_inc(x_loaded[t], 16)
                if t == 1:
                    sp.dma_start(gate_rows[:, :], gate_in).then_inc(small_loaded, 16)
                    sp.dma_start(bias_row[:, :], bias_in.rearrange("(a e) -> a e", a=1).to_broadcast([P, E])).then_inc(small_loaded, 16)
                    sp.dma_start(a_rows[:, :, :].rearrange("p a d -> p (a d)"),
                                 a_in.to_broadcast([P, 2 * D])).then_inc(small_loaded, 16)
                if t % 2 and t // 2 < K // 2:
                    q = t // 2
                    if q >= 2:
                        sp.wait_ge(w_hi, q - 1)
                        sp.wait_ge(w_lo, q - 1)
                    sp.dma_start(w_stage[:, q % 2, :, :],
                                 w_in[2 * q * P:(2 * q + 2) * P, :].rearrange("(k p) n -> p k n", p=P)).then_inc(w_loaded[q % 2], 16)
            sp.wait_ge(att_lo, T)
            for m, (w, loaded) in enumerate(((wg_in, gu_loaded0), (wu_in, gu_loaded1))):
                sp.dma_start(gu_stage[m][:, :, :], w[0].rearrange("(k p) n -> p k n", p=P)).then_inc(loaded, 16)
            sp.wait_ge(agg_done, 1)
            sp.dma_start(d_stage[:, :, :], wd_in[0].rearrange("(k p) n -> p k n", p=P)).then_inc(d_loaded, 16)

            def load_expert(e, g, u, d):
                sp.wait_ge(gu_hi, 2 * e)
                sp.wait_ge(gu_lo, 2 * e)
                sp.dma_start(gu_stage[0][:, :, :], g.rearrange("(k p) n -> p k n", p=P)).then_inc(gu_loaded0, 16)
                sp.dma_start(gu_stage[1][:, :, :], u.rearrange("(k p) n -> p k n", p=P)).then_inc(gu_loaded1, 16)
                sp.wait_ge(d_hi, e)
                sp.wait_ge(d_lo, e)
                sp.dma_start(d_stage[:, :, :], d.rearrange("(k p) n -> p k n", p=P)).then_inc(d_loaded, 16)

            with sp.Fori(1, E) as e:
                load_expert(e, wg_in[bass.ds(e, 1)].rearrange("a h i -> (a h) i"),
                            wu_in[bass.ds(e, 1)].rearrange("a h i -> (a h) i"),
                            wd_in[bass.ds(e, 1)].rearrange("a h i -> (a h) i"))
            load_expert(E, wgs_in, wus_in, wds_in)
            for t in range(T):
                rows = P if t < T - 1 else TAIL
                sp.wait_ge(y_banks_free, 2 + E * T + t + 1)
                sp.dma_start(out[t * P:t * P + rows, :], xs[0:rows, t, :]).then_inc(stored, 16)
            sp.wait_ge(stored, 16 * T)

        @block.gpsimd
        def _(pool):
            pool.memset(xs[96:P, T - 1, :], 0.0).then_inc(x_tail_zeroed, 1)
            pool.wait_ge(x_tail_zeroed, 1)
            pool.memset(edges_i[:, :, :], -1).then_inc(edges_padded, 1)
            pool.memset(ident[:, :], 0.0).then_inc(pool_step, 1)
            pool.wait_ge(pool_step, 1)
            pool.affine_select(out=ident[:, :], in_=ident[:, :], compare_op=ALU.not_equal, fill=1.0, base=0,
                               pattern=[[-1, P]], channel_multiplier=1).then_inc(consts_set, 1)
            pool.memset(ones[:, :], 1.0).then_inc(consts_set, 1)
            pool.memset(ones16[:, :], 1.0).then_inc(consts_set, 1)
            pool.memset(zero16[:, :], 0.0).then_inc(consts_set, 1)
            pool.memset(mhalf[:, :], -0.5).then_inc(consts_set, 1)
            pool.wait_ge(consts_set, 5)
            pool.iota(iota_i[:, :], [[1, NP]], base=0, channel_multiplier=0).then_inc(iota_set, 1)
            pool.iota(pair_i[:, :], [[P, 2]], base=0, channel_multiplier=1).then_inc(iota_set, 1)
            pool.iota(first_i[:, :], [[P, T]], base=0, channel_multiplier=0).then_inc(iota_set, 1)

            pool_steps = [1]

            def chain(ins):
                pool_steps[0] += 1
                ins.then_inc(pool_step, 1)
                pool.wait_ge(pool_step, pool_steps[0])

            def rstd(n, stats_ready, ready):
                b = n % 2
                v, y, q, r = (rs[:, b, i:i + 1] for i in range(4))
                pool.wait_ge(stats_ready, n + 1)
                if n >= 2:
                    pool.wait_ge(norm_set if ready is rstd_set else norm2_set, n - 1)
                elif ready is rstd2_set:
                    pool.wait_ge(norm_set, T)
                chain(pool.tensor_scalar(v, mv[:, b, 1:2], LN_EPS, None, ALU.add))
                chain(pool.tensor_tensor(y, v, mhalf[:, :], ALU.pow))
                chain(pool.tensor_tensor(q, y, y, ALU.mult))
                chain(pool.tensor_tensor(q, q, v, ALU.mult))
                chain(pool.tensor_scalar(q, q, -0.5, 1.5, ALU.mult, ALU.add))
                pool.tensor_tensor(r, y, q, ALU.mult).then_inc(ready, 1)

            for n in range(T):
                rstd(n, stats_set, rstd_set)
            for n in range(T):
                rstd(n, stats2_set, rstd2_set)

        @block.scalar
        def _(act):
            act.wait_ge(edges_turned, 1)
            act.copy(edgeT[:, :, :].rearrange("p a c -> p (a c)"), prep[:, 0:4 * P]).then_inc(edgeT_set, 1)
            act.wait_ge(gate_turned, 1)
            act.activation(gateT[0][:, :, :].rearrange("p k e -> p (k e)"), prep[:, 0:K * E], ACT.Copy, scale=WS).then_inc(gate_hi, 1)

            def w_part(q):
                act.wait_ge(w_loaded[q % 2], 16 * (q // 2 + 1))
                act.activation(ws[0][:, 2 * q:2 * q + 2, :], w_stage[:, q % 2, :, :], ACT.Copy, scale=WS).then_inc(w_hi, 1)

            def turned_hi(n):
                act.wait_ge(trans_set, n + 1)
                act.copy(x1T[0][:, :, n * P:(n + 1) * P], trans[n % 2]).then_inc(hi_set, 1)

            def h_out(n):
                act.wait_ge(h_set, n + 1)
                if n == 0:
                    act.wait_ge(bounds_set, 1)
                act.activation(hs[0][:, n, :], h_acc[n % 2], ACT.Copy, scale=1 / WS).then_inc(h_hi, 1)
                if n >= 1:
                    act.wait_ge(al_dotted, n)
                else:
                    act.wait_ge(small_loaded, 48)
                act.activation(h_row[:, :], h_acc[n % 2], ACT.Copy, scale=1 / WS).then_inc(h_rowed, 1)

            for n in range(2):
                turned_hi(n)
                w_part(2 * n)
                w_part(2 * n + 1)
            for n in range(T):
                h_out(n)
                if n + 2 < T:
                    turned_hi(n + 2)
            act.wait_ge(diag_used, T)
            act.wait_ge(h_lo, T)
            act.wait_ge(w_lo, K // 2)
            act.copy(al_row[:, :], al_acc).then_inc(al_copied, 1)
            for j in range(T):
                act.wait_ge(al_copied, 1)
                if j >= 1:
                    act.wait_ge(att_set, j)
                else:
                    act.wait_ge(diag_set, T)
                act.activation(e_low[:, :], al_row[:, :], ACT.Exp, bias=nar[:, 0, j:j + 1], scale=-1.0).then_inc(e_low_set, 1)
                act.activation(e_high[:, :], al_row[:, :], ACT.Exp, bias=nar[:, 1, j:j + 1], scale=-SLOPE).then_inc(e_high_set, 1)
                act.wait_ge(att_set, j + 1)
                act.copy(att[0][:, j, :], att_row[:, :]).then_inc(att_hi, 1)

            def gate_up_hi(e):
                for m, loaded in ((0, gu_loaded0), (1, gu_loaded1)):
                    act.wait_ge(loaded, 16 * (e + 1))
                    act.activation(gu_w[m][0][:, :, :], gu_stage[m][:, :, :], ACT.Copy, scale=WS).then_inc(gu_hi, 1)

            def down_hi(e):
                act.wait_ge(d_loaded, 16 * (e + 1))
                act.activation(d_w[0][:, :, :], d_stage[:, :, :], ACT.Copy, scale=WS).then_inc(d_hi, 1)

            for n in range(T):
                act.wait_ge(neg_set, n + 1)
                act.activation(elu_neg[:, :], elu_neg[:, :], ACT.Exp).then_inc(exp_set, 1)
                act.wait_ge(trans2_set, n + 1)
                act.copy(x2T[0][:, :, n * P:(n + 1) * P], trans2).then_inc(trans2_hi, 1)
            act.wait_ge(agg_done, 1)
            gate_up_hi(0)
            down_hi(0)
            act.wait_ge(logits_set, T)
            act.activation(score[:, :, :], logit_acc, ACT.Exp, scale=-1 / WS).then_inc(logit_exp, 1)

            def expert(e, last):
                for m in range(GRP):
                    (c0, w), i = CH[m // KI], m % KI
                    act.wait_ge(gu_set, GRP * e + m + 1)
                    act.activation(sig[:, 0:w], g_acc[m % 2][:, 0:w], ACT.Sigmoid, scale=1 / WS).then_inc(sig_set, 1)
                    act.wait_ge(act_set, GRP * e + m + 1)
                    act.copy(actT[0][:, i, c0:c0 + w], act_row[:, 0:w]).then_inc(act_hi, 1)
                if not last:
                    act.wait_ge(gu_set, GRP * (e + 1))
                    gate_up_hi(e + 1)
                    act.wait_ge(y_set, T * (e + 1))
                    down_hi(e + 1)

            with act.Fori(0, E) as e:
                expert(e, False)
            expert(E, True)

        @block.vector
        def _(dve):
            steps = [0]

            def chain(ins):
                steps[0] += 1
                ins.then_inc(dve_step, 1)
                dve.wait_ge(dve_step, steps[0])

            def norm_stats(n, ready):
                b = n % 2
                dve.bn_stats(stats[:, b, 0, :], xs[:, n, 0:HALF])
                chain(dve.bn_stats(stats[:, b, 1, :], xs[:, n, HALF:D]))
                dve.bn_aggr(mv[:, b, :], stats[:, b, :, :].rearrange("p a s -> p (a s)")).then_inc(ready, 1)

            dve.wait_ge(iota_set, 3)
            dve.tensor_copy(nodes16[:, :], iota_i[:, :])
            dve.tensor_copy(first_f[:, 0, :], first_i[:, :])
            chain(dve.tensor_scalar(pair_i[:, :], pair_i[:, :], 1, None, ALU.arith_shift_right))
            chain(dve.tensor_copy(pair_f[:, :], pair_i[:, :]))
            dve.tensor_scalar(first_f[:, 1, :], first_f[:, 0, :], float(P - 1), None, ALU.add)
            dve.wait_ge(edges_loaded, 16 * (6 if REST else 4))
            dve.tensor_copy(edges_f[:, :, :], edges_i[:, :, :]).then_inc(edges_floated, 1)
            dve.wait_ge(edges_floated, 1)
            chain(dve.tensor_scalar(pads[:, :, :], edges_f[:, 2:4, :], 0.0, 4.0 * NP, ALU.is_lt, ALU.mult))
            chain(dve.tensor_tensor(pads[:, :, :], pads[:, :, :], edges_f[:, 2:4, :], ALU.add))
            dve.tensor_reduce(span[:, 0, :], pads[:, :, :], X, ALU.min)
            chain(dve.tensor_reduce(span[:, 1, :], edges_f[:, 2:4, :], X, ALU.max))
            for g in range(2):
                dve.tensor_scalar(need[:, 0, g, :], first_f[:, 1, :], span[:, 0, g:g + 1], None, ALU.is_ge)
                chain(dve.tensor_scalar(need[:, 1, g, :], first_f[:, 0, :], span[:, 1, g:g + 1], None, ALU.is_le))
            chain(dve.tensor_tensor(need[:, 0, :, :], need[:, 0, :, :], need[:, 1, :, :], ALU.mult))
            for g in range(2):
                dve.tensor_scalar(cand[:, 0, g, :], need[:, 0, g, :], pair_f[:, g:g + 1], None, ALU.mult)
                chain(dve.tensor_scalar(cand[:, 1, g, :], need[:, 0, g, :], float(P), None, ALU.mult))
            chain(dve.tensor_tensor(cand[:, 1, :, :], cand[:, 1, :, :], cand[:, 0, :, :], ALU.subtract))
            dve.tensor_tensor(cand[:, 0, :, :], cand[:, 0, :, :], need[:, 0, :, :], ALU.add).then_inc(cand_set, 1)
            dve.wait_ge(edgeT_set, 1)
            dve.wait_ge(cand_turned, 1)
            chain(dve.tensor_reduce(cmax[0:4 * T, :], prep[0:4 * T, 0:P], X, ALU.max))
            dve.tensor_scalar(diag[0:4 * T, 0:4 * T], ident[0:4 * T, 0:4 * T], cmax[0:4 * T, :], None, ALU.mult).then_inc(cmax_set, 1)
            dve.wait_ge(cmax_turned, 1)
            row = prep[0:1, 0:4 * T].rearrange("p (w g t) -> p w g t", w=2, g=2)
            chain(dve.tensor_copy(crow[:, :, :], row[:, :, 0, :]))
            chain(dve.tensor_tensor(crow[:, :, :], crow[:, :, :], row[:, :, 1, :], ALU.max))
            chain(dve.tensor_scalar(crow[:, 0, :], crow[:, 0, :], 1.0, None, ALU.max))
            chain(dve.tensor_scalar(crow[:, 1, :], crow[:, 1, :], -1.0, float(P), ALU.mult, ALU.add))
            chain(dve.tensor_scalar(lens[:, :], crow[:, 0, :], -1.0, None, ALU.add))
            chain(dve.tensor_tensor(crow[:, 1, :], crow[:, 1, :], lens[:, :], ALU.min))
            chain(dve.tensor_tensor(lens[:, :], crow[:, 0, :], crow[:, 1, :], ALU.subtract))
            chain(dve.memset(bounds_f[:, 0, 0:1], 0.0))
            for j in range(T):
                chain(dve.tensor_tensor(bounds_f[:, 1, j:j + 1], bounds_f[:, 0, j:j + 1], lens[:, j:j + 1], ALU.add))
                if j + 1 < T:
                    chain(dve.tensor_copy(bounds_f[:, 0, j + 1:j + 2], bounds_f[:, 1, j:j + 1]))
            chain(dve.tensor_tensor(bounds_f[:, 2, :], crow[:, 1, :], bounds_f[:, 0, :], ALU.subtract))
            chain(dve.tensor_scalar(bounds_f[:, 2, :], bounds_f[:, 2, :], float(P * T), None, ALU.add))
            dve.tensor_copy(bounds[:, :, :], bounds_f[:, :, :]).then_inc(bounds_set, 1)
            dve.wait_ge(gate_hi, 1)
            dve.scalar_tensor_tensor(out=gateT[1][:, :, :].rearrange("p k e -> p (k e)"), in0=prep[:, 0:K * E], scalar=WS,
                                     in1=gateT[0][:, :, :].rearrange("p k e -> p (k e)"), op0=ALU.mult,
                                     op1=ALU.subtract).then_inc(gate_lo, 1)

            def normalise(n):
                dve.wait_ge(rstd_set, n + 1)
                if n >= 2:
                    dve.wait_ge(trans_set, n - 1)
                b = n % 2
                dve.tensor_scalar(xn1[:, b, :], xs[:, n, :], mv[:, b, 0:1], rs[:, b, 3:4], ALU.subtract,
                                  ALU.mult).then_inc(norm_set, 1)

            def turned_lo(n):
                dve.wait_ge(hi_set, n + 1)
                dve.tensor_tensor(x1T[1][:, :, n * P:(n + 1) * P], trans[n % 2], x1T[0][:, :, n * P:(n + 1) * P],
                                  ALU.subtract).then_inc(lo_set, 1)

            def w_part(q):
                dve.wait_ge(w_hi, q + 1)
                dve.scalar_tensor_tensor(out=ws[1][:, 2 * q:2 * q + 2, :], in0=w_stage[:, q % 2, :, :], scalar=WS,
                                         in1=ws[0][:, 2 * q:2 * q + 2, :], op0=ALU.mult, op1=ALU.subtract).then_inc(w_lo, 1)

            def stats1(n):
                dve.wait_ge(x_loaded[n], 16)
                if n >= 2:
                    dve.wait_ge(norm_set, n - 1)
                norm_stats(n, stats_set)

            def h_out(n):
                dve.wait_ge(h_rowed, n + 1)
                dve.tensor_tensor(hs[1][:, n, :], h_row[:, :], hs[0][:, n, :], ALU.subtract).then_inc(h_lo, 1)
                if n >= 1:
                    dve.wait_ge(al_dotted, n)
                for i in range(2):
                    last = dve.tensor_tensor_reduce(dots[i][:, :], h_row[:, :], a_rows[:, i, :], 1.0, 0.0, ALU.mult, ALU.add,
                                                    alr[:, i, n:n + 1])
                last.then_inc(al_dotted, 1)

            dots = [elu_neg, elu_pos]
            stats1(0)
            stats1(1)
            for n in range(2):
                normalise(n)
                w_part(2 * n) if n == 0 else turned_lo(n)
                w_part(2 * n + 1) if n == 0 else w_part(2)
                turned_lo(0) if n == 0 else w_part(3)
            for n in range(T):
                if n + 2 < T:
                    stats1(n + 2)
                    normalise(n + 2)
                h_out(n)
                if n + 2 < T:
                    turned_lo(n + 2)

            dve.wait_ge(al_dotted, T)
            dve.tensor_scalar(nar[:, 0, :], alr[:, 1, :], -1.0, None, ALU.mult)
            dve.tensor_scalar(nar[:, 1, :], alr[:, 1, :], -SLOPE, None, ALU.mult)
            for n in range(T):
                if n >= 1:
                    dve.wait_ge(diag_used, n)
                dve.tensor_scalar(diag[:, :], ident[:, :], alr[:, 0, n:n + 1], None, ALU.mult).then_inc(diag_set, 1)

            def one_hots(j):
                begin = dve.value_load(bounds[0:1, 0, j:j + 1], min_val=0, max_val=P * T)
                end = dve.value_load(bounds[0:1, 1, j:j + 1], min_val=1, max_val=P * T)
                back = dve.value_load(bounds[0:1, 2, j:j + 1], min_val=0, max_val=P * T + P)
                with dve.Fori(begin, end) as q:
                    pair = nc.s_assert_within(
                        dve.snap(q + back - P * T), 0, P - 1,
                        skip_runtime_bounds_check_because="a tile's first and last pairs are pairs of chunks")
                    for b in range(2):
                        dve.wait_ge(hot_free, q * 2 + (b + 1))
                        dve.tensor_scalar(hot_src[:, b, :], nodes16[:, :], edge_src[:, bass.ds(pair * 2 + b, 1)], None, ALU.is_equal)
                        dve.tensor_scalar(hot_dst[:, b, :], nodes16[:, j * P:(j + 1) * P], edge_dst[:, bass.ds(pair * 2 + b, 1)],
                                          None, ALU.is_equal).then_inc(hot_ready, 1)

            def attention(j):
                dve.wait_ge(e_low_set, j + 1)
                dve.wait_ge(e_high_set, j + 1)
                dve.tensor_tensor(e_low[:, :], e_low[:, :], e_high[:, :], ALU.min).then_inc(acc_chain, 1)
                dve.wait_ge(acc_chain, j + 1)
                dve.wait_ge(count_set, j + 1)
                if j >= 1:
                    dve.wait_ge(att_hi, j)
                dve.scalar_tensor_tensor(out=att_row[:, :], in0=count_acc[j % 2], scalar=AS, in1=e_low[:, :], op0=ALU.mult,
                                         op1=ALU.mult).then_inc(att_set, 1)
                dve.wait_ge(att_set, j + 1)
                dve.wait_ge(att_hi, j + 1)
                dve.tensor_tensor(att[1][:, j, :], att_row[:, :], att[0][:, j, :], ALU.subtract).then_inc(att_lo, 1)

            edge_src = edgeT[:, 0:2, :].rearrange("p a c -> p (a c)")
            edge_dst = edgeT[:, 2:4, :].rearrange("p a c -> p (a c)")
            dve.wait_ge(bounds_set, 1)
            for j in range(T):
                one_hots(j)
                if j >= 1:
                    attention(j - 1)
            attention(T - 1)

            lns = [0]

            def link(ins):
                lns[0] += 1
                ins.then_inc(ln_chain, 1)
                dve.wait_ge(ln_chain, lns[0])

            def node_out(n):
                b = n % 2
                dve.wait_ge(sum_set, n + 1)
                dve.tensor_scalar(rsum[:, b, 0:1], sum_acc, AS * SUM_EPS, None, ALU.add).then_inc(sum_read, 1)
                dve.wait_ge(sum_read, n + 1)
                link(dve.reciprocal(rsum[:, b, 1:2], rsum[:, b, 0:1]))
                dve.wait_ge(agg_set, n + 1)
                dve.tensor_scalar(elu_neg[:, :], agg_acc[b], rsum[:, b, 1:2], 0.0, ALU.mult, ALU.min).then_inc(neg_set, 1)
                last = dve.tensor_scalar(elu_pos[:, :], agg_acc[b], rsum[:, b, 1:2], 0.0, ALU.mult, ALU.max)
                last.then_inc(agg_free, 1)
                dve.wait_ge(agg_free, n + 1)
                link(dve.tensor_tensor(elu_pos[:, :], elu_pos[:, :], xs[:, n, :], ALU.add))
                dve.wait_ge(exp_set, n + 1)
                link(dve.scalar_tensor_tensor(out=xs[:, n, :], in0=elu_neg[:, :], scalar=-1.0, in1=elu_pos[:, :], op0=ALU.add,
                                              op1=ALU.add))
                norm_stats(n, stats2_set)
                dve.wait_ge(rstd2_set, n + 1)
                if n >= 1:
                    dve.wait_ge(trans2_set, n)
                dve.tensor_scalar(xn2[:, :], xs[:, n, :], mv[:, b, 0:1], rs[:, b, 3:4], ALU.subtract,
                                  ALU.mult).then_inc(norm2_set, 1)
                if n >= 1:
                    turned2_lo(n - 1)

            def turned2_lo(n):
                dve.wait_ge(trans2_hi, n + 1)
                dve.tensor_tensor(x2T[1][:, :, n * P:(n + 1) * P], trans2, x2T[0][:, :, n * P:(n + 1) * P],
                                  ALU.subtract).then_inc(trans2_lo, 1)

            for n in range(T):
                node_out(n)
            turned2_lo(T - 1)

            def gate_up_lo(e):
                for m in range(2):
                    dve.wait_ge(gu_hi, 2 * e + (m + 1))
                    dve.scalar_tensor_tensor(out=gu_w[m][1][:, :, :], in0=gu_stage[m][:, :, :], scalar=WS, in1=gu_w[m][0][:, :, :],
                                             op0=ALU.mult, op1=ALU.subtract).then_inc(gu_lo, 1)

            def down_lo(e):
                dve.wait_ge(d_hi, e + 1)
                dve.scalar_tensor_tensor(out=d_w[1][:, :, :], in0=d_stage[:, :, :], scalar=WS, in1=d_w[0][:, :, :],
                                         op0=ALU.mult, op1=ALU.subtract).then_inc(d_lo, 1)

            gate_up_lo(0)
            down_lo(0)

            def bc(ap, shape):
                return ap.to_broadcast(shape)

            def ranks(v, n, out_rank, ra, rb):
                mine = bc(v.unsqueeze(3), [P, T, n, n])
                other = bc(v.unsqueeze(2), [P, T, n, n])
                chain(dve.tensor_tensor(ra, other, mine, ALU.is_equal))
                chain(dve.tensor_tensor(ra, ra, bc(lower[:, 0:n, 0:n].unsqueeze(1), [P, T, n, n]), ALU.mult))
                chain(dve.tensor_tensor(rb, other, mine, ALU.is_gt))
                chain(dve.tensor_tensor(ra, ra, rb, ALU.add))
                chain(dve.tensor_reduce(out_rank, ra, X, ALU.add))

            dve.wait_ge(logit_exp, 1)
            chain(dve.memset(lower[:, :, :], 0.0))
            for e in range(1, E):
                last = dve.memset(lower[:, e, 0:e], 1.0)
            chain(last)
            chain(dve.tensor_scalar(score[:, :, :], score[:, :, :], 1.0, None, ALU.add))
            chain(dve.reciprocal(score[:, :, :], score[:, :, :]))
            chain(dve.tensor_tensor(choice[:, :, :], score[:, :, :], bc(bias_row[:, :].unsqueeze(1), [P, T, E]), ALU.add))
            pairs = choice[:, :, :].rearrange("p t (g m) -> p t g m", m=EG)
            chain(dve.tensor_tensor(rg[:, :, :], pairs[:, :, :, 0], pairs[:, :, :, 1], ALU.add))
            nn = GROUPS * GROUPS
            ga = rank_a[:, :, :, :].rearrange("p t a b -> p (t a b)")[:, 0:T * nn].rearrange("p (t a b) -> p t a b", a=GROUPS, b=GROUPS)
            gb = rank_b[:, :, :, :].rearrange("p t a b -> p (t a b)")[:, 0:T * nn].rearrange("p (t a b) -> p t a b", a=GROUPS, b=GROUPS)
            ranks(rg[:, :, :], GROUPS, rg2[:, :, :], ga, gb)
            chain(dve.tensor_scalar(rg[:, :, :], rg2[:, :, :], TOP_GROUPS - 0.5, None, ALU.is_lt))
            chain(dve.tensor_tensor(pairs, pairs, bc(rg[:, :, :].unsqueeze(3), [P, T, GROUPS, EG]), ALU.mult))
            ranks(choice[:, :, :], E, r1[:, :, :], rank_a[:, :, :, :], rank_b[:, :, :, :])
            chain(dve.tensor_scalar(r2[:, :, :], r1[:, :, :], TOPK - 0.5, None, ALU.is_lt))
            chain(dve.tensor_tensor(r2[:, :, :], r2[:, :, :], score[:, :, :], ALU.mult))
            chain(dve.tensor_reduce(rt[:, :], r2[:, :, :], X, ALU.add))
            chain(dve.tensor_scalar(rt[:, :], rt[:, :], 1e-20, None, ALU.add))
            chain(dve.reciprocal(rt2[:, :], rt[:, :]))
            chain(dve.tensor_scalar(rt2[:, :], rt2[:, :], ROUTED_SCALE / WS, None, ALU.mult))
            chain(dve.tensor_tensor(comb[:, :, 0:E], r2[:, :, :], bc(rt2[:, :].unsqueeze(2), [P, T, E]), ALU.mult))
            chain(dve.memset(comb[:, :, E:E + 1], 1 / WS))

            def add_out(e, n):
                dve.wait_ge(y_set, T * e + (n + 1))
                weight = comb[:, n, E:E + 1] if isinstance(e, int) else comb[:, n, bass.ds(e, 1)]
                dve.scalar_tensor_tensor(out=xs[:, n, :], in0=y_acc[n % 2], scalar=weight, in1=xs[:, n, :], op0=ALU.mult,
                                         op1=ALU.add).then_inc(y_banks_free, 1)

            def expert(e, last):
                for m in range(GRP):
                    (c0, w), i, done = CH[m // KI], m % KI, GRP * e + (m + 1)
                    dve.wait_ge(sig_set, done)
                    dve.scalar_tensor_tensor(out=gated[:, 0:w], in0=g_acc[m % 2][:, 0:w], scalar=1 / WS, in1=sig[:, 0:w],
                                             op0=ALU.mult, op1=ALU.mult).then_inc(gated_set, 1)
                    dve.wait_ge(gated_set, done)
                    dve.scalar_tensor_tensor(out=act_row[:, 0:w], in0=u_acc[m % 2][:, 0:w], scalar=1 / WS, in1=gated[:, 0:w],
                                             op0=ALU.mult, op1=ALU.mult).then_inc(act_set, 1)
                    dve.wait_ge(act_hi, done)
                    dve.tensor_tensor(actT[1][:, i, c0:c0 + w], act_row[:, 0:w], actT[0][:, i, c0:c0 + w],
                                      ALU.subtract).then_inc(act_lo, 1)
                for n in range(T):
                    add_out(e, n)
                    if n == 1 and not last:
                        gate_up_lo(e + 1)
                if not last:
                    down_lo(e + 1)

            with dve.Fori(0, E) as e:
                expert(e, False)
            expert(E, True)

        @block.tensor
        def _(pe):
            pe.wait_ge(consts_set, 5)
            pe.wait_ge(edges_floated, 1)
            for i in range(4):
                last = pe.transpose(prep[:, i * P:(i + 1) * P], edges_f[:, i, :], ident[:, :])
            last.then_inc(edges_turned, 1)
            pe.wait_ge(edgeT_set, 1)
            pe.wait_ge(cand_set, 1)
            pe.transpose(prep[0:4 * T, 0:P], cand[:, :, :, :].rearrange("p a g t -> p (a g t)"), ident[:, :]).then_inc(cand_turned, 1)
            pe.wait_ge(cmax_set, 1)
            pe.matmul(prep[0:1, 0:4 * T], ones[0:4 * T, 0:1], diag[0:4 * T, 0:4 * T], start=True, stop=True).then_inc(cmax_turned, 1)
            pe.wait_ge(bounds_set, 1)
            pe.wait_ge(small_loaded, 48)
            for k in range(K):
                last = pe.transpose(prep[:, k * E:(k + 1) * E], gate_rows[:, k * P:(k + 1) * P], ident[0:E, 0:E])
            last.then_inc(gate_turned, 1)

            def turn(n):
                pe.wait_ge(norm_set, n + 1)
                if n >= 2:
                    pe.wait_ge(lo_set, n - 1)
                for k in range(K):
                    last = pe.transpose(trans[n % 2][:, k, :], xn1[:, n % 2, k * P:(k + 1) * P], ident[:, :])
                last.then_inc(trans_set, 1)

            def three_pass(out_ap, lhs, rhs, k, nk, cols, closes=True):
                for li, ri in ((0, 0), (0, 1), (1, 0)):
                    for c0, c1 in cols:
                        last = pe.matmul(out_ap[:, c0:c1], lhs(li), rhs(ri)[:, c0:c1], start=(k == 0 and li == ri),
                                         stop=(closes and k == nk - 1 and li == 1))
                return last

            HALVES = [(0, HALF), (HALF, D)]

            def h_product(n):
                pe.wait_ge(lo_set, n + 1)
                if n >= 2:
                    pe.wait_ge(h_rowed, n - 1)
                elif n == 0:
                    pe.wait_ge(gate_lo, 1)
                for k in range(K):
                    if n == 0 and k % 2 == 0:
                        pe.wait_ge(w_lo, k // 2 + 1)
                    last = three_pass(h_acc[n % 2], lambda i: x1T[i][:, k, n * P:(n + 1) * P], lambda i: ws[i][:, k, :], k, K, HALVES)
                last.then_inc(h_set, 1)

            turn(0)
            turn(1)
            for n in range(T):
                h_product(n)
                if n + 2 < T:
                    turn(n + 2)

            pe.wait_ge(lo_set, T)
            for n in range(T):
                pe.wait_ge(diag_set, n + 1)
                last = pe.matmul(al_acc[:, n * P:(n + 1) * P], ones[:, :], diag[:, :], start=True, stop=True)
                last.then_inc(diag_used, 1)

            def counts(j):
                acc = count_acc[j % 2]
                if j == 0:
                    pe.wait_ge(al_copied, 1)
                    pe.wait_ge(bounds_set, 1)
                elif j == 1:
                    pe.wait_ge(h_lo, T)
                    pe.wait_ge(h_rowed, T)
                else:
                    pe.wait_ge(att_set, j - 1)
                for c0, w in CH:
                    pe.matmul(acc[:, c0:c0 + 1], zero16[:, :], zero16[:, 0:1], start=True, stop=False, skip_group_check=True)
                begin = pe.value_load(bounds[0:1, 0, j:j + 1], min_val=0, max_val=P * T)
                end = pe.value_load(bounds[0:1, 1, j:j + 1], min_val=1, max_val=P * T)
                with pe.Fori(begin, end) as q:
                    for b in range(2):
                        pe.wait_ge(hot_ready, q * 2 + (b + 1))
                        for c0, w in CH:
                            last = pe.matmul(acc[:, c0:c0 + w], hot_dst[:, b, :], hot_src[:, b, c0:c0 + w], start=False,
                                             stop=False, skip_group_check=True)
                        last.then_inc(hot_free, 1)
                for c0, w in CH:
                    last = pe.matmul(acc[:, c0:c0 + 1], zero16[:, :], zero16[:, 0:1], start=False, stop=True, skip_group_check=True)
                last.then_inc(count_set, 1)

            pe.sem_inc(hot_free, 2)
            for j in range(T):
                counts(j)

            def aggregate(n):
                b = n % 2
                if n == 0:
                    pe.wait_ge(att_lo, T)
                if n >= 2:
                    pe.wait_ge(agg_free, n - 1)
                if n >= 1:
                    pe.wait_ge(sum_read, n)
                for j in range(T):
                    for i in range(2):
                        last = pe.matmul(sum_acc, att[i][:, j, n * P:(n + 1) * P], ones16[:, :], start=(j == 0 and i == 0),
                                         stop=(j == T - 1 and i == 1))
                last.then_inc(sum_set, 1)
                for j in range(T):
                    last = three_pass(agg_acc[b], lambda i: att[i][:, j, n * P:(n + 1) * P], lambda i: hs[i][:, j, :], j, T, HALVES)
                last.then_inc(agg_set, 1)

            def turn2(n):
                pe.wait_ge(norm2_set, n + 1)
                if n >= 1:
                    pe.wait_ge(trans2_lo, n)
                for k in range(K):
                    last = pe.transpose(trans2[:, k, :], xn2[:, k * P:(k + 1) * P], ident[:, :])
                last.then_inc(trans2_set, 1)

            def logits(n):
                pe.wait_ge(trans2_lo, n + 1)
                for k in range(K):
                    for li, ri in ((0, 0), (0, 1), (1, 0)):
                        last = pe.matmul(logit_acc[:, n, :], x2T[li][:, k, n * P:(n + 1) * P], gateT[ri][:, k, :],
                                         start=(k == 0 and li == ri), stop=(k == K - 1 and li == 1))
                last.then_inc(logits_set, 1)

            for n in range(T):
                aggregate(n)
                if n == T - 1:
                    last = pe.matmul(bank[0:1, 5, 511:512], zero16[:, 0:1], zero16[:, 0:1], start=True, stop=True)
                    last.then_inc(agg_done, 1)
                if n >= 1:
                    turn2(n - 1)
                if n >= 2:
                    logits(n - 2)
            turn2(T - 1)
            logits(T - 2)
            logits(T - 1)

            pe.wait_ge(agg_free, T)
            pe.sem_inc(act_lo, 2)
            pe.wait_ge(logit_exp, 1)
            pe.sem_inc(y_banks_free, 2)
            with pe.Fori(0, E + 1) as e:
                for m in range(GRP):
                    (c0, w), i = CH[m // KI], m % KI
                    if m == 0:
                        pe.wait_ge(gu_lo, 2 * e + 2)
                    pe.wait_ge(act_lo, GRP * e + (m + 1))
                    for mat, acc in ((0, g_acc), (1, u_acc)):
                        for k in range(K):
                            last = three_pass(acc[m % 2], lambda q: gu_w[mat][q][:, k, i * P:(i + 1) * P],
                                              lambda q: x2T[q][:, k, c0:c0 + w], k, K, [(0, w)])
                    last.then_inc(gu_set, 1)
                pe.wait_ge(d_lo, e + 1)
                for n in range(T):
                    if n * P in (0, HALF, 2 * HALF):
                        pe.wait_ge(act_lo, GRP * e + (2 + KI * (n * P // HALF + 1)))
                    pe.wait_ge(y_banks_free, T * e + (n + 1))
                    for k in range(KI):
                        last = three_pass(y_acc[n % 2], lambda q: actT[q][:, k, n * P:(n + 1) * P], lambda q: d_w[q][:, k, :],
                                          k, KI, HALVES)
                    last.then_inc(y_set, 1)


_INS = ["x", "src", "dst", "L0_gnn_W", "L0_gnn_a", "L0_ffn_gate_w", "L0_ffn_correction_bias", "L0_ffn_Wg", "L0_ffn_Wu",
        "L0_ffn_Wd", "L0_ffn_Wg_s", "L0_ffn_Wu_s", "L0_ffn_Wd_s"]


def kernel(**inputs):
    import numpy as np
    import concourse.bacc as bacc
    from concourse.bass_utils import run_bass_kernel_spmd

    nc = bacc.Bacc("TRN2", target_bir_lowering=False, num_devices=1, dynamic_dma_scratch_size=1024)
    arrays, args = {}, []
    for name in _INS:
        a = np.ascontiguousarray(inputs[name])
        arrays[f"in_{name}"] = a
        args.append(nc.dram_tensor(f"in_{name}", a.shape, mybir.dt.from_np(a.dtype), kind="ExternalInput").ap())
    shape = inputs["x"].shape
    args.append(nc.dram_tensor("out", shape, F32, kind="ExternalOutput").ap())
    build(nc, *args)
    r = run_bass_kernel_spmd(nc, [arrays], core_ids=[0])
    return r.results[0]["out"]
```

```python
import concourse.bass as bass
from concourse import mybir

F32 = mybir.dt.float32
F16 = mybir.dt.float16
I32 = mybir.dt.int32
ALU = mybir.AluOpType
ACT = mybir.ActivationFunctionType
X = mybir.AxisListType.X

P = 128
WS = 256.0
AS = 64.0
LN_EPS = 1e-5
SUM_EPS = 1e-5
SLOPE = 0.1
ROUTED_SCALE = 2.5
MIN_TILES = 3
TOPK = 4
GROUPS = 4
TOP_GROUPS = 2


def build(nc, x_in, src_in, dst_in, w_in, a_in, gate_in, bias_in, wg_in, wu_in, wd_in,
          wgs_in, wus_in, wds_in, out):
    N, D = x_in.shape
    NE = src_in.shape[0]
    E, _, FI = wg_in.shape
    T = -(-N // P)
    NP = T * P
    TAIL = N - (T - 1) * P
    K = D // P
    KI = FI // P
    C = -(-NE // P)
    CB = C - P
    FULL = NE // P
    REST = NE - FULL * P
    HALF = 512
    EG = E // GROUPS
    assert T % 2 == 0 and 0 < CB <= P and D == 2 * HALF and FI == HALF and NP == 2 * HALF + 256
    CH = [(0, HALF), (HALF, HALF), (2 * HALF, NP - 2 * HALF)]
    T0 = T // 2
    TE = N * TOPK // P + E * MIN_TILES
    KT = 64
    assert TE <= KT and FI == HALF and T0 == 5

    x_rows = nc.dram_tensor("x_rows", [NP, 2 * D], F16, kind="Internal").ap()
    y_rows = nc.dram_tensor("y_rows", [NP * TOPK, D], F32, kind="Internal").ap()

    base = nc.sbuf_base + (-nc.sbuf_base) % 64
    cursor = [base]

    def at(name, offset, shape, dt):
        return nc.alloc_sbuf_tensor_at(name, shape, dt, offset=offset)

    def region(nbytes):
        start = cursor[0]
        cursor[0] += nbytes + (-nbytes) % 32
        assert cursor[0] <= nc.sbuf_usable_end, (cursor[0], nc.sbuf_usable_end)
        return start

    R_X = region(T * D * 4)
    R_A = region(T * NP * 4)
    R_B = region(T * D * 4)
    R_C = region(T * D * 4)
    R_D = region(2 * K * FI * 4)
    R_T = region(12288)

    xs = at("xs", R_X, [P, T, D], F32)
    x1T = [at(f"x1T{i}", R_A + i * K * NP * 2, [P, K, NP], F16) for i in range(2)]
    xn1 = at("xn1", R_A + K * NP * 4, [P, 2, D], F32)
    att = [at(f"att{i}", R_A + i * T * NP * 2, [P, T, NP], F16) for i in range(2)]
    hs = [at(f"hs{i}", R_B + i * T * D * 2, [P, T, D], F16) for i in range(2)]
    ws = [at(f"ws{i}", R_C + i * K * D * 2, [P, K, D], F16) for i in range(2)]
    w_stage = at("w_stage", R_D, [P, 2, 2, D], F32)
    h_row = at("h_row", R_D + 16384, [P, D], F32)
    a_rows = at("a_rows", R_D + 20480, [P, 2, D], F32)
    al_row = at("al_row", R_D, [P, NP], F32)
    e_low = at("e_low", R_D + 5120, [P, NP], F32)
    e_high = at("e_high", R_D + 10240, [P, NP], F32)
    att_row = at("att_row", R_D + 15360, [P, NP], F32)
    hot_src = at("hot_src", R_D + 20480, [P, 2, NP], F16)
    hot_dst = at("hot_dst", R_D + 25600, [P, 2, P], F16)
    MAT = K * FI * 4
    MATS = 3
    slot_at = [R_C, R_A]
    weights = [[[at(f"w{sl}{m}{i}", slot_at[sl] + m * MAT + i * MAT // 2, [P, KI if m == 2 else K, D if m == 2 else FI], F16)
                 for i in range(2)] for m in range(MATS)] for sl in range(2)]
    stage_at = [R_C + MATS * MAT, R_A + MATS * MAT, R_A + (MATS + 1) * MAT]
    stage = [at(f"stage{m}", stage_at[m], [P, KI if m == 2 else K, D if m == 2 else FI], F32) for m in range(MATS)]
    stage0 = [stage[0], stage[0], at("stage_first_down", stage_at[0], [P, KI, D], F32)]
    x_row = at("x_row", R_D + 24576, [P, 2, D], F16)
    xT = at("xT", R_D + 28672, [P, 2, K, P], F16)
    y_row = at("y_row", R_A + (MATS + 2) * MAT, [P, D], F32)
    y_in = [at(f"y_in{b}", stage_at[1 + b], [P, TOPK, D], F32) for b in range(2)]
    act_hl = at("act_hl", R_T + 6144, [P, 2, FI], F16)
    actT = at("actT", R_T + 8192, [P, 2, KI, P], F16)
    elu_neg = at("elu_neg", R_T, [P, D], F32)
    elu_pos = at("elu_pos", R_T + 4096, [P, D], F32)
    xn2 = at("xn2", R_T + 8192, [P, D], F32)
    sig = at("sig", R_T, [P, HALF], F32)
    gated = at("gated", R_T + 2048, [P, HALF], F32)
    act_row = at("act_row", R_T + 4096, [P, HALF], F32)

    early_at = [R_T + 8192]
    late_at = [R_A + 5 * MAT + 4096]

    def early(name, shape, dt):
        n = mybir.dt.size(dt)
        for d in shape[1:]:
            n *= d
        n += -n % 32
        early_at[0] += n
        assert early_at[0] <= R_T + 12288
        return at(name, early_at[0] - n, shape, dt)

    def late(name, shape, dt):
        n = mybir.dt.size(dt)
        for d in shape[1:]:
            n *= d
        n += -n % 32
        late_at[0] += n
        assert late_at[0] <= R_C
        return at(name, late_at[0] - n, shape, dt)

    def small(name, shape, dt):
        n = 1
        for s in shape[1:]:
            n *= s
        return at(name, region(n * mybir.dt.size(dt)), shape, dt)

    ident = small("ident", [P, P], F32)
    ident16 = small("ident16", [P, P], F16)
    before16 = small("before16", [P, P], F16)
    ones = early("ones", [P, P], F32)
    ones16w = small("ones16", [P, P], F16)
    ones16 = ones16w[:, 0:1]
    zero16 = small("zero16", [P, P], F16)
    iota_i = at("iota_i", R_B, [P, NP], I32)
    nodes16 = small("nodes16", [P, NP], F16)
    edges_i = at("edges_i", R_B + 5120, [P, 4, P], I32)
    edges_f = at("edges_f", R_B + 8192, [P, 4, P], F32)
    edgeT = early("edgeT", [P, 4, P], F32)
    gate_rows = at("gate_rows", R_B + 12288, [E, D], F32)
    gateT = [small(f"gateT{i}", [P, K, E], F16) for i in range(2)]
    bias_row = small("bias_row", [P, E], F32)
    stats = small("stats", [P, 2, 2, 6], F32)
    mv = small("mv", [P, 2, 2], F32)
    rs = small("rs", [P, 2, 4], F32)
    mhalf = small("mhalf", [P, 1], F32)
    alr = early("alr", [P, 2, T], F32)
    nar = early("nar", [P, 2, T], F32)
    diag = early("diag", [P, P], F32)
    rsum = small("rsum", [P, 2, 2], F32)
    span = small("span", [P, 2, 2], F32)
    pads = at("pads", R_B + 16384, [P, 2, P], F32)
    pair_i = small("pair_i", [P, 2], I32)
    pair_f = small("pair_f", [P, 2], F32)
    first_i = small("first_i", [P, T], I32)
    first_f = small("first_f", [P, 2, T], F32)
    need = at("need", R_B + 17408, [P, 2, 2, T], F32)
    cand = at("cand", R_B + 18432, [P, 2, 2, T], F32)
    cmax = small("cmax", [P, 1], F32)
    crow = small("crow", [1, 2, T], F32)
    lens = small("lens", [1, T], F32)
    bounds_f = small("bounds_f", [1, 3, T], F32)
    bounds = small("bounds", [1, 3, T], I32)
    PAIRS = T * E
    hot_slot = at("hot_slot", R_A, [P, PAIRS, P], F16)
    hot_tile = at("hot_tile", R_A + PAIRS * P * 2, [P, PAIRS, 2, KT], F16)
    r_at = [R_A + PAIRS * (P + 2 * KT) * 2]

    def routing(name, shape, dt=F32):
        n = 4
        for d in shape[1:]:
            n *= d
        n += -n % 32
        r_at[0] += n
        assert r_at[0] <= R_A + MATS * MAT
        return at(name, r_at[0] - n, shape, dt)

    rank_a = routing("rank_a", [P, T, E, E])
    rank_b = routing("rank_b", [P, T, E, E])
    lower = routing("lower", [P, E, E])
    choice, r1, r2, sel, cw, ranked, kglob, slot = (
        late(n, [P, T, E], F32) for n in ("choice", "r1", "r2", "sel", "cw", "ranked", "kglob", "slot"))
    pos_i = late("pos_i", [P, T, E], I32)
    tile_i = late("tile_i", [P, T, E], I32)
    slot_i = late("slot_i", [P, T, E], I32)
    offs = late("offs", [P, T + 1, E], F32)
    tiles_f = routing("tiles_f", [P, E])
    tiles_i = routing("tiles_i", [P, E], I32)
    begin_f = routing("begin_f", [P, E + 1])
    sel16 = routing("sel16", [P, T, E], F16)
    valid = routing("valid", [P, T])
    rg = routing("rg", [P, T, GROUPS])
    rg2 = routing("rg2", [P, T, GROUPS])
    rt = routing("rt", [P, T])
    rt2 = routing("rt2", [P, T])
    dest_a = routing("dest_a", [P, KT])
    dest_b = routing("dest_b", [P, KT])
    token_i = small("token_i", [P, T], I32)
    token = late("token", [P, T], F32)
    score = late("score", [P, T, E], F32)
    rank_w = late("rank_w", [P, T, TOPK], F32)
    gather_at = late("gather_at", [P, KT], I32)
    scatter_at = late("scatter_at", [P, KT], I32)
    gather_now = small("gather_now", [P, 1], mybir.dt.uint32)
    scatter_now = small("scatter_now", [P, 1], mybir.dt.uint32)
    spans = small("spans", [1, E + 1], I32)

    bank = nc.alloc_psum_tensor("bank", [P, 8, HALF], F32)
    trans = [bank[:, 2 * b:2 * b + 2, :].rearrange("p a (k n) -> p (a k) n", n=P) for b in range(2)]
    h_acc = [bank[:, 4 + 2 * b:6 + 2 * b, :].rearrange("p a n -> p (a n)") for b in range(2)]
    count_acc = [bank[:, 3 * b:3 * b + 3, :].rearrange("p a n -> p (a n)")[:, 0:NP] for b in range(2)]
    al_acc = count_acc[0]
    prep = bank[:, 7, :]
    agg_acc = [bank[:, 2 * b:2 * b + 2, :].rearrange("p a n -> p (a n)") for b in range(2)]
    sum_acc = bank[:, 4, 0:1]
    logit_acc = bank[:, 5, 0:T * E].rearrange("p (t e) -> p t e", e=E)
    trans2 = [bank[:, 6 + i, :].bitcast(F16).rearrange("p (k n) -> p k n", n=P) for i in range(2)]
    g_acc, u_acc = bank[:, 0, :], bank[:, 1, :]
    y_acc = bank[:, 2:4, :].rearrange("p a n -> p (a n)")
    xT_acc = [bank[:, 4 + i, :].bitcast(F16).rearrange("p (k n) -> p k n", n=P) for i in range(2)]
    actT_acc = bank[:, 6, :].bitcast(F16).rearrange("p (i k n) -> p i k n", i=2, n=P)
    route_acc = bank[:, 7, :]

    x_tail_zeroed = nc.alloc_semaphore("x_tail_zeroed")
    edges_padded = nc.alloc_semaphore("edges_padded")
    small_loaded = nc.alloc_semaphore("small_loaded")
    edges_loaded = nc.alloc_semaphore("edges_loaded")
    consts_set = nc.alloc_semaphore("consts_set")
    iota_set = nc.alloc_semaphore("iota_set")
    pool_step = nc.alloc_semaphore("pool_step")
    stats_set = nc.alloc_semaphore("stats_set")
    rstd_set = nc.alloc_semaphore("rstd_set")
    norm_set = nc.alloc_semaphore("norm_set")
    trans_set = nc.alloc_semaphore("trans_set")
    hi_set = nc.alloc_semaphore("hi_set")
    lo_set = nc.alloc_semaphore("lo_set")
    w_hi = nc.alloc_semaphore("w_hi")
    w_lo = nc.alloc_semaphore("w_lo")
    h_set = nc.alloc_semaphore("h_set")
    h_hi = nc.alloc_semaphore("h_hi")
    h_lo = nc.alloc_semaphore("h_lo")
    h_rowed = nc.alloc_semaphore("h_rowed")
    al_dotted = nc.alloc_semaphore("al_dotted")
    diag_set = nc.alloc_semaphore("diag_set")
    diag_used = nc.alloc_semaphore("diag_used")
    al_copied = nc.alloc_semaphore("al_copied")
    edges_floated = nc.alloc_semaphore("edges_floated")
    edges_turned = nc.alloc_semaphore("edges_turned")
    edgeT_set = nc.alloc_semaphore("edgeT_set")
    cand_set = nc.alloc_semaphore("cand_set")
    cand_turned = nc.alloc_semaphore("cand_turned")
    cmax_set = nc.alloc_semaphore("cmax_set")
    cmax_turned = nc.alloc_semaphore("cmax_turned")
    bounds_set = nc.alloc_semaphore("bounds_set")
    gate_turned = nc.alloc_semaphore("gate_turned")
    gate_hi = nc.alloc_semaphore("gate_hi")
    gate_lo = nc.alloc_semaphore("gate_lo")
    dve_step = nc.alloc_semaphore("dve_step")
    hot_ready = nc.alloc_semaphore("hot_ready")
    hot_free = nc.alloc_semaphore("hot_free")
    count_set = nc.alloc_semaphore("count_set")
    e_low_set = nc.alloc_semaphore("e_low_set")
    e_high_set = nc.alloc_semaphore("e_high_set")
    att_set = nc.alloc_semaphore("att_set")
    att_hi = nc.alloc_semaphore("att_hi")
    att_lo = nc.alloc_semaphore("att_lo")
    sum_set = nc.alloc_semaphore("sum_set")
    sum_read = nc.alloc_semaphore("sum_read")
    agg_set = nc.alloc_semaphore("agg_set")
    agg_free = nc.alloc_semaphore("agg_free")
    neg_set = nc.alloc_semaphore("neg_set")
    exp_set = nc.alloc_semaphore("exp_set")
    stats2_set = nc.alloc_semaphore("stats2_set")
    rstd2_set = nc.alloc_semaphore("rstd2_set")
    norm2_set = nc.alloc_semaphore("norm2_set")
    trans2_set = nc.alloc_semaphore("trans2_set")
    row_hi = nc.alloc_semaphore("row_hi")
    row_lo = nc.alloc_semaphore("row_lo")
    row_stored = nc.alloc_semaphore("row_stored")
    trans2_hi = nc.alloc_semaphore("trans2_hi")
    trans2_lo = nc.alloc_semaphore("trans2_lo")
    logits_set = nc.alloc_semaphore("logits_set")
    logit_exp = nc.alloc_semaphore("logit_exp")
    agg_done = nc.alloc_semaphore("agg_done")
    ln_chain = nc.alloc_semaphore("ln_chain")
    acc_chain = nc.alloc_semaphore("acc_chain")
    gate_loaded = nc.alloc_semaphore("gate_loaded")
    up_loaded = nc.alloc_semaphore("up_loaded")
    down_loaded = nc.alloc_semaphore("down_loaded")
    gu_hi = nc.alloc_semaphore("gu_hi")
    gu_lo = nc.alloc_semaphore("gu_lo")
    d_hi = nc.alloc_semaphore("d_hi")
    d_lo = nc.alloc_semaphore("d_lo")
    sel_set = nc.alloc_semaphore("sel_set")
    prefix_set = nc.alloc_semaphore("prefix_set")
    pairs_set = nc.alloc_semaphore("pairs_set")
    pairs_summed = nc.alloc_semaphore("pairs_summed")
    dests_set = nc.alloc_semaphore("dests_set")
    rows_loaded = nc.alloc_semaphore("rows_loaded")
    gathered = nc.alloc_semaphore("gathered")
    x_turned = nc.alloc_semaphore("x_turned")
    xT_hi_set = nc.alloc_semaphore("xT_hi_set")
    xT_lo_set = nc.alloc_semaphore("xT_lo_set")
    gu_done = nc.alloc_semaphore("gu_done")
    sig_set = nc.alloc_semaphore("sig_set")
    gated_set = nc.alloc_semaphore("gated_set")
    act_set = nc.alloc_semaphore("act_set")
    act_hi = nc.alloc_semaphore("act_hi")
    act_lo = nc.alloc_semaphore("act_lo")
    act_turned = nc.alloc_semaphore("act_turned")
    actT_set = nc.alloc_semaphore("actT_set")
    y_done = nc.alloc_semaphore("y_done")
    y_read = nc.alloc_semaphore("y_read")
    y_row_set = nc.alloc_semaphore("y_row_set")
    gather_picked = nc.alloc_semaphore("gather_picked")
    scatter_picked = nc.alloc_semaphore("scatter_picked")
    scattered = nc.alloc_semaphore("scattered")
    pool_passed = nc.alloc_semaphore("pool_passed")
    y_in_loaded0 = nc.alloc_semaphore("y_in_loaded0")
    y_in_loaded1 = nc.alloc_semaphore("y_in_loaded1")
    y_summed = nc.alloc_semaphore("y_summed")
    sum_chain = nc.alloc_semaphore("sum_chain")
    stored = nc.alloc_semaphore("stored")
    x_loaded = [nc.alloc_semaphore(f"x_loaded{t}") for t in range(T)]
    w_loaded = [nc.alloc_semaphore(f"w_loaded{b}") for b in range(2)]

    with nc.Block() as block:

        @block.sync
        def _(sp):
            sp.wait_ge(edges_padded, 1)
            for i, e in enumerate((src_in, dst_in)):
                sp.dma_start(edges_i[:, 2 * i, :], e[0:P * P].rearrange("(c e) -> c e", e=P)).then_inc(edges_loaded, 16)
                sp.dma_start(edges_i[0:FULL - P, 2 * i + 1, :],
                             e[P * P:FULL * P].rearrange("(c e) -> c e", e=P)).then_inc(edges_loaded, 16)
                if REST:
                    sp.dma_start(edges_i[FULL - P:FULL - P + 1, 2 * i + 1, 0:REST],
                                 e[FULL * P:NE].rearrange("(c e) -> c e", c=1)).then_inc(edges_loaded, 16)
            for t in range(T):
                if t == T - 1:
                    sp.wait_ge(x_tail_zeroed, 1)
                rows = P if t < T - 1 else TAIL
                sp.dma_start(xs[0:rows, t, :], x_in[t * P:t * P + rows, :]).then_inc(x_loaded[t], 16)
                if t == 1:
                    sp.dma_start(gate_rows[:, :], gate_in).then_inc(small_loaded, 16)
                    sp.dma_start(a_rows[:, :, :].rearrange("p a d -> p (a d)"),
                                 a_in.to_broadcast([P, 2 * D])).then_inc(small_loaded, 16)
                if t % 2 and t // 2 < K // 2:
                    q = t // 2
                    if q >= 2:
                        sp.wait_ge(w_hi, q - 1)
                        sp.wait_ge(w_lo, q - 1)
                    sp.dma_start(w_stage[:, q % 2, :, :],
                                 w_in[2 * q * P:(2 * q + 2) * P, :].rearrange("(k p) n -> p k n", p=P)).then_inc(w_loaded[q % 2], 16)
            matrices = ((gate_loaded, gu_hi, gu_lo), (up_loaded, gu_hi, gu_lo), (down_loaded, d_hi, d_lo))
            shared = (wgs_in, wus_in, wds_in)

            def as_blocks(w):
                return w.rearrange("(k p) n -> p k n", p=P)

            sp.wait_ge(att_lo, T)

            def rows_out(n):
                sp.wait_ge(row_lo, n + 1)
                sp.dma_start(x_rows[n * P:(n + 1) * P, :], x_row[:, :, :].rearrange("p a d -> p (a d)")).then_inc(row_stored, 16)

            for m, (loaded, _, _) in enumerate(matrices):
                if m >= 1:
                    sp.wait_ge(gu_hi, m)
                    sp.wait_ge(gu_lo, m)
                sp.dma_start(stage0[m][:, :, :], as_blocks(shared[m])).then_inc(loaded, 16)
                rows_out(2 * m)
                rows_out(2 * m + 1)
            for n in range(2 * MATS, T):
                rows_out(n)

            def first_rows(k):
                if k == 0:
                    sp.wait_ge(row_stored, 16 * T)
                    sp.wait_ge(trans2_set, T)
                else:
                    sp.wait_ge(x_turned, k)
                sp.dma_start(x_row[:, :, :].rearrange("p a d -> p (a d)"), x_rows[k * P:(k + 1) * P, :]).then_inc(rows_loaded, 16)

            def load_expert(q, mats):
                for m, (loaded, hi, lo) in enumerate(matrices):
                    if m == 0:
                        sp.wait_ge(d_hi, 1)
                        sp.wait_ge(d_lo, 1)
                    sp.wait_ge(hi, q if m == 2 else 2 * q)
                    sp.wait_ge(lo, q if m == 2 else 2 * q)
                    sp.dma_start(stage[m][:, :, :], as_blocks(mats[m])).then_inc(loaded, 16)

            first_rows(0)
            sp.wait_ge(agg_done, 1)
            load_expert(1, (wg_in[0], wu_in[0], wd_in[0]))
            for k in range(1, T0):
                first_rows(k)
            with sp.Fori(2, E + 1) as q:
                load_expert(q, [w[bass.ds(q - 1, 1)].rearrange("a h i -> (a h) i") for w in (wg_in, wu_in, wd_in)])
            load_expert(E + 1, shared)

            sp.wait_ge(dests_set, 1)
            tiles = sp.value_load(spans[0:1, E:E + 1], min_val=E * MIN_TILES, max_val=TE)

            def results_in(t):
                rows = P if t < T - 1 else TAIL
                if t >= 2:
                    sp.wait_ge(y_summed, t - 1)
                sp.dma_start(y_in[t % 2][0:rows, :, :].rearrange("p r d -> p (r d)"),
                             y_rows[t * P * TOPK:(t * P + rows) * TOPK, :].rearrange("(p r) d -> p (r d)", r=TOPK))\
                    .then_inc((y_in_loaded0, y_in_loaded1)[t % 2], 16)

            def store(t):
                rows = P if t < T - 1 else TAIL
                sp.dma_start(out[t * P:t * P + rows, :], xs[0:rows, t, :]).then_inc(stored, 16)

            sp.wait_ge(scattered, (tiles + 1) * 16)
            sp.wait_ge(d_lo, E + 2)
            sp.wait_ge(gu_lo, 2 * (E + 2))
            results_in(0)
            results_in(1)
            for t in range(T0 + 2, T):
                for i in (2 * (t - T0 - 2), 2 * (t - T0 - 2) + 1):
                    results_in(i + 2)
                    store(i) if i < T0 else None
            for t in range(2 * (T - T0 - 2) + 2, T):
                results_in(t)
            for t in range(T0):
                if t >= 2 * (T - T0 - 2):
                    sp.wait_ge(y_summed, t + 1)
                    store(t)
            for t in range(T0, T):
                sp.wait_ge(y_summed, t + 1)
                sp.wait_ge(y_read, t + 1)
                store(t)
            sp.wait_ge(stored, 16 * T)

        @block.gpsimd
        def _(pool):
            pool.dma_start(bias_row[:, :], bias_in.rearrange("(a e) -> a e", a=1).to_broadcast([P, E])).then_inc(scattered, 16)
            pool.memset(xs[96:P, T - 1, :], 0.0).then_inc(x_tail_zeroed, 1)
            pool.wait_ge(x_tail_zeroed, 1)
            pool.memset(edges_i[:, :, :], -1).then_inc(edges_padded, 1)
            pool.memset(ident[:, :], 0.0).then_inc(pool_step, 1)
            pool.wait_ge(pool_step, 1)
            pool.affine_select(out=ident[:, :], in_=ident[:, :], compare_op=ALU.not_equal, fill=1.0, base=0,
                               pattern=[[-1, P]], channel_multiplier=1).then_inc(consts_set, 1)
            pool.memset(ones[:, :], 1.0).then_inc(consts_set, 1)
            pool.memset(ones16w[:, :], 1.0).then_inc(consts_set, 1)
            pool.memset(zero16[:, :], 0.0).then_inc(consts_set, 1)
            pool.memset(mhalf[:, :], -0.5).then_inc(consts_set, 1)
            pool.wait_ge(consts_set, 5)
            pool.memset(before16[:, :], 1.0).then_inc(pool_step, 1)
            pool.wait_ge(pool_step, 2)
            pool.affine_select(out=before16[:, :], in_=before16[:, :], compare_op=ALU.is_gt, fill=0.0, base=0,
                               pattern=[[1, P]], channel_multiplier=-1).then_inc(consts_set, 1)
            pool.iota(token_i[:, :], [[P, T]], base=0, channel_multiplier=1).then_inc(consts_set, 1)
            pool.tensor_copy(ident16[:, :], ident[:, :]).then_inc(consts_set, 1)
            pool.wait_ge(consts_set, 8)
            pool.iota(iota_i[:, :], [[1, NP]], base=0, channel_multiplier=0).then_inc(iota_set, 1)
            pool.iota(pair_i[:, :], [[P, 2]], base=0, channel_multiplier=1).then_inc(iota_set, 1)
            pool.iota(first_i[:, :], [[P, T]], base=0, channel_multiplier=0).then_inc(iota_set, 1)

            pool_steps = [2]

            def chain(ins):
                pool_steps[0] += 1
                ins.then_inc(pool_step, 1)
                pool.wait_ge(pool_step, pool_steps[0])

            def rstd(n, stats_ready, ready):
                b = n % 2
                v, y, q, r = (rs[:, b, i:i + 1] for i in range(4))
                pool.wait_ge(stats_ready, n + 1)
                if n >= 2:
                    pool.wait_ge(norm_set if ready is rstd_set else norm2_set, n - 1)
                elif ready is rstd2_set:
                    pool.wait_ge(norm_set, T)
                chain(pool.tensor_scalar(v, mv[:, b, 1:2], LN_EPS, None, ALU.add))
                chain(pool.tensor_tensor(y, v, mhalf[:, :], ALU.pow))
                chain(pool.tensor_tensor(q, y, y, ALU.mult))
                chain(pool.tensor_tensor(q, q, v, ALU.mult))
                chain(pool.tensor_scalar(q, q, -0.5, 1.5, ALU.mult, ALU.add))
                pool.tensor_tensor(r, y, q, ALU.mult).then_inc(ready, 1)

            for n in range(T):
                rstd(n, stats_set, rstd_set)
            for n in range(T):
                rstd(n, stats2_set, rstd2_set)

            def gather(j):
                pool.wait_ge(x_turned, T0 + j)
                pool.sem_inc(pool_passed, 1)
                pool.tensor_copy(gather_now[:, :], gather_at[:, bass.ds(j, 1)].bitcast(mybir.dt.uint32)).then_inc(gather_picked, 1)
                pool.wait_ge(gather_picked, j + 1)
                pool.sem_inc(pool_passed, 1)
                pool.indirect_dma_start(out=x_row[:, :, :].rearrange("p a d -> p (a d)"), out_offset=None, in_=x_rows[:, :],
                                        in_offset=bass.IndirectOffsetOnAxis(ap=gather_now[:, :], axis=0)).then_inc(gathered, 16)

            def last_rows(t):
                pool.wait_ge(x_turned, tiles + t)
                pool.sem_inc(pool_passed, 1)
                pool.dma_start(x_row[:, :, :].rearrange("p a d -> p (a d)"), x_rows[t * P:(t + 1) * P, :]).then_inc(gathered, 16)

            def scatter(j, after):
                pool.wait_ge(y_row_set, after)
                pool.sem_inc(pool_passed, 1)
                pool.tensor_copy(scatter_now[:, :], scatter_at[:, bass.ds(j, 1)].bitcast(mybir.dt.uint32)).then_inc(scatter_picked, 1)
                pool.wait_ge(scatter_picked, after + 1)
                pool.sem_inc(pool_passed, 1)
                pool.indirect_dma_start(out=y_rows[:, :], out_offset=bass.IndirectOffsetOnAxis(ap=scatter_now[:, :], axis=0),
                                        in_=y_row[:, :], in_offset=None, bounds_check=NP * TOPK - 1,
                                        oob_is_err=False).then_inc(scattered, 16)

            pool.sem_inc(scatter_picked, 3)
            pool.sem_inc(y_row_set, 2)
            pool.wait_ge(dests_set, 1)
            tiles = pool.value_load(spans[0:1, E:E + 1], min_val=E * MIN_TILES, max_val=TE)
            for j in range(3):
                gather(j)
            with pool.Fori(3, tiles) as j:
                gather(j)
                scatter(nc.s_assert_within(pool.snap(j - 3), 0, KT - 1, skip_runtime_bounds_check_because="j is at least 3"), j)
            for j in range(T - T0):
                last_rows(T0 + j)
                if j < 3:
                    scatter(nc.s_assert_within(pool.snap(tiles - (3 - j)), 0, KT - 1,
                                               skip_runtime_bounds_check_because="there are at least E * MIN_TILES tiles"),
                            tiles + j)

        @block.scalar
        def _(act):
            act.wait_ge(edges_turned, 1)
            act.copy(edgeT[:, :, :].rearrange("p a c -> p (a c)"), prep[:, 0:4 * P]).then_inc(edgeT_set, 1)
            act.wait_ge(gate_turned, 1)
            act.activation(gateT[0][:, :, :].rearrange("p k e -> p (k e)"), prep[:, 0:K * E], ACT.Copy, scale=WS).then_inc(gate_hi, 1)

            def w_part(q):
                act.wait_ge(w_loaded[q % 2], 16 * (q // 2 + 1))
                act.activation(ws[0][:, 2 * q:2 * q + 2, :], w_stage[:, q % 2, :, :], ACT.Copy, scale=WS).then_inc(w_hi, 1)

            def turned_hi(n):
                act.wait_ge(trans_set, n + 1)
                act.copy(x1T[0][:, :, n * P:(n + 1) * P], trans[n % 2]).then_inc(hi_set, 1)

            def h_out(n):
                act.wait_ge(h_set, n + 1)
                if n == 0:
                    act.wait_ge(bounds_set, 1)
                act.activation(hs[0][:, n, :], h_acc[n % 2], ACT.Copy, scale=1 / WS).then_inc(h_hi, 1)
                if n >= 1:
                    act.wait_ge(al_dotted, n)
                else:
                    act.wait_ge(small_loaded, 32)
                act.activation(h_row[:, :], h_acc[n % 2], ACT.Copy, scale=1 / WS).then_inc(h_rowed, 1)

            for n in range(2):
                turned_hi(n)
                w_part(2 * n)
                w_part(2 * n + 1)
            for n in range(T):
                h_out(n)
                if n + 2 < T:
                    turned_hi(n + 2)
            act.wait_ge(diag_used, T)
            act.wait_ge(h_lo, T)
            act.wait_ge(w_lo, K // 2)
            act.copy(al_row[:, :], al_acc).then_inc(al_copied, 1)
            for j in range(T):
                act.wait_ge(al_copied, 1)
                if j >= 1:
                    act.wait_ge(att_set, j)
                else:
                    act.wait_ge(diag_set, T)
                act.activation(e_low[:, :], al_row[:, :], ACT.Exp, bias=nar[:, 0, j:j + 1], scale=-1.0).then_inc(e_low_set, 1)
                act.activation(e_high[:, :], al_row[:, :], ACT.Exp, bias=nar[:, 1, j:j + 1], scale=-SLOPE).then_inc(e_high_set, 1)
                act.wait_ge(att_set, j + 1)
                act.copy(att[0][:, j, :], att_row[:, :]).then_inc(att_hi, 1)

            def split_hi(q, m, sl, staged):
                act.wait_ge((gate_loaded, up_loaded, down_loaded)[m], 16 * (q + 1))
                act.activation(weights[sl][m][0][:, :, :], staged[m][:, :, :], ACT.Copy, scale=WS).then_inc(d_hi if m == 2 else gu_hi, 1)

            for n in range(T):
                act.wait_ge(neg_set, n + 1)
                act.activation(elu_neg[:, :], elu_neg[:, :], ACT.Exp).then_inc(exp_set, 1)
                act.wait_ge(norm2_set, n + 1)
                if n >= 1:
                    act.wait_ge(row_stored, 16 * n)
                    act.wait_ge(trans2_set, n)
                act.copy(x_row[:, 0, :], xn2[:, :]).then_inc(row_hi, 1)
                act.wait_ge(trans2_set, n + 1)
                if n >= 1:
                    act.wait_ge(logits_set, n)
                act.copy(xT[:, 0, :, :], trans2[0]).then_inc(trans2_hi, 1)
                if n in (1, 3, 5):
                    split_hi(0, n // 2, 0, stage0)
            act.wait_ge(logits_set, T)
            act.activation(score[:, :, :], logit_acc, ACT.Exp, scale=-1 / WS).then_inc(logit_exp, 1)

            def xT_hi(k):
                act.wait_ge(x_turned, k + 1)
                act.copy(xT[:, 0, :, :], xT_acc[0]).then_inc(xT_hi_set, 1)

            def ffn_tile(k, more=True, scatters=True, first_scatter=False):
                act.wait_ge(gu_done, k + 1)
                act.activation(sig[:, :], g_acc, ACT.Sigmoid, scale=1 / WS).then_inc(sig_set, 1)
                act.wait_ge(act_set, k + 1)
                act.copy(act_hl[:, 0, :], act_row[:, :]).then_inc(act_hi, 1)
                if more:
                    xT_hi(k + 1)
                if scatters:
                    act.wait_ge(y_done, k)
                    act.wait_ge(scattered, (k - T0) * 16)
                    act.activation(y_row[:, :], y_acc, ACT.Copy, scale=1 / WS).then_inc(y_row_set, 1)

            xT_hi(0)
            for k in range(T0):
                if k == T0 - 1:
                    act.wait_ge(dests_set, 1)
                    for m in range(MATS):
                        split_hi(1, m, 1, stage)
                ffn_tile(k, scatters=False)

            def expert(q, sl):
                begin = act.value_load(spans[0:1, bass.ds(q - 1, 1)], min_val=0, max_val=TE)
                end = act.value_load(spans[0:1, bass.ds(q, 1)], min_val=MIN_TILES, max_val=TE)
                split_hi(q + 1, 0, 1 - sl, stage)
                split_hi(q + 1, 1, 1 - sl, stage)
                with act.If(begin > 0):
                    ffn_tile(begin + T0)
                with act.Else():
                    ffn_tile(begin + T0, scatters=False)
                    act.wait_ge(y_done, T0)
                split_hi(q + 1, 2, 1 - sl, stage)
                ffn_tile(begin + T0 + 1)
                with act.Fori(begin + 2, end) as j:
                    ffn_tile(j + T0)

            act.wait_ge(dests_set, 1)
            with act.Fori(0, E // 2) as i:
                expert(i * 2 + 1, 1)
                expert(i * 2 + 2, 0)
            tiles = act.value_load(spans[0:1, E:E + 1], min_val=E * MIN_TILES, max_val=TE)
            for t in range(T0, T):
                ffn_tile(tiles + t, more=t < T - 1, scatters=t == T0)

        @block.vector
        def _(dve):
            steps = [0]

            def chain(ins):
                steps[0] += 1
                ins.then_inc(dve_step, 1)
                dve.wait_ge(dve_step, steps[0])

            def norm_stats(n, ready):
                b = n % 2
                dve.bn_stats(stats[:, b, 0, :], xs[:, n, 0:HALF])
                chain(dve.bn_stats(stats[:, b, 1, :], xs[:, n, HALF:D]))
                dve.bn_aggr(mv[:, b, :], stats[:, b, :, :].rearrange("p a s -> p (a s)")).then_inc(ready, 1)

            dve.wait_ge(iota_set, 3)
            dve.tensor_copy(nodes16[:, :], iota_i[:, :])
            dve.tensor_copy(first_f[:, 0, :], first_i[:, :])
            chain(dve.tensor_scalar(pair_i[:, :], pair_i[:, :], 1, None, ALU.arith_shift_right))
            chain(dve.tensor_copy(pair_f[:, :], pair_i[:, :]))
            dve.tensor_scalar(first_f[:, 1, :], first_f[:, 0, :], float(P - 1), None, ALU.add)
            dve.wait_ge(edges_loaded, 16 * (6 if REST else 4))
            dve.tensor_copy(edges_f[:, :, :], edges_i[:, :, :]).then_inc(edges_floated, 1)
            dve.wait_ge(edges_floated, 1)
            chain(dve.tensor_scalar(pads[:, :, :], edges_f[:, 2:4, :], 0.0, 4.0 * NP, ALU.is_lt, ALU.mult))
            chain(dve.tensor_tensor(pads[:, :, :], pads[:, :, :], edges_f[:, 2:4, :], ALU.add))
            dve.tensor_reduce(span[:, 0, :], pads[:, :, :], X, ALU.min)
            chain(dve.tensor_reduce(span[:, 1, :], edges_f[:, 2:4, :], X, ALU.max))
            for g in range(2):
                dve.tensor_scalar(need[:, 0, g, :], first_f[:, 1, :], span[:, 0, g:g + 1], None, ALU.is_ge)
                chain(dve.tensor_scalar(need[:, 1, g, :], first_f[:, 0, :], span[:, 1, g:g + 1], None, ALU.is_le))
            chain(dve.tensor_tensor(need[:, 0, :, :], need[:, 0, :, :], need[:, 1, :, :], ALU.mult))
            for g in range(2):
                dve.tensor_scalar(cand[:, 0, g, :], need[:, 0, g, :], pair_f[:, g:g + 1], None, ALU.mult)
                chain(dve.tensor_scalar(cand[:, 1, g, :], need[:, 0, g, :], float(P), None, ALU.mult))
            chain(dve.tensor_tensor(cand[:, 1, :, :], cand[:, 1, :, :], cand[:, 0, :, :], ALU.subtract))
            dve.tensor_tensor(cand[:, 0, :, :], cand[:, 0, :, :], need[:, 0, :, :], ALU.add).then_inc(cand_set, 1)
            dve.wait_ge(edgeT_set, 1)
            dve.wait_ge(cand_turned, 1)
            chain(dve.tensor_reduce(cmax[0:4 * T, :], prep[0:4 * T, 0:P], X, ALU.max))
            dve.tensor_scalar(diag[0:4 * T, 0:4 * T], ident[0:4 * T, 0:4 * T], cmax[0:4 * T, :], None, ALU.mult).then_inc(cmax_set, 1)
            dve.wait_ge(cmax_turned, 1)
            row = prep[0:1, 0:4 * T].rearrange("p (w g t) -> p w g t", w=2, g=2)
            chain(dve.tensor_copy(crow[:, :, :], row[:, :, 0, :]))
            chain(dve.tensor_tensor(crow[:, :, :], crow[:, :, :], row[:, :, 1, :], ALU.max))
            chain(dve.tensor_scalar(crow[:, 0, :], crow[:, 0, :], 1.0, None, ALU.max))
            chain(dve.tensor_scalar(crow[:, 1, :], crow[:, 1, :], -1.0, float(P), ALU.mult, ALU.add))
            chain(dve.tensor_scalar(lens[:, :], crow[:, 0, :], -1.0, None, ALU.add))
            chain(dve.tensor_tensor(crow[:, 1, :], crow[:, 1, :], lens[:, :], ALU.min))
            chain(dve.tensor_tensor(lens[:, :], crow[:, 0, :], crow[:, 1, :], ALU.subtract))
            chain(dve.memset(bounds_f[:, 0, 0:1], 0.0))
            for j in range(T):
                chain(dve.tensor_tensor(bounds_f[:, 1, j:j + 1], bounds_f[:, 0, j:j + 1], lens[:, j:j + 1], ALU.add))
                if j + 1 < T:
                    chain(dve.tensor_copy(bounds_f[:, 0, j + 1:j + 2], bounds_f[:, 1, j:j + 1]))
            chain(dve.tensor_tensor(bounds_f[:, 2, :], crow[:, 1, :], bounds_f[:, 0, :], ALU.subtract))
            chain(dve.tensor_scalar(bounds_f[:, 2, :], bounds_f[:, 2, :], float(P * T), None, ALU.add))
            dve.tensor_copy(bounds[:, :, :], bounds_f[:, :, :]).then_inc(bounds_set, 1)
            dve.wait_ge(gate_hi, 1)
            dve.scalar_tensor_tensor(out=gateT[1][:, :, :].rearrange("p k e -> p (k e)"), in0=prep[:, 0:K * E], scalar=WS,
                                     in1=gateT[0][:, :, :].rearrange("p k e -> p (k e)"), op0=ALU.mult,
                                     op1=ALU.subtract).then_inc(gate_lo, 1)

            def normalise(n):
                dve.wait_ge(rstd_set, n + 1)
                if n >= 2:
                    dve.wait_ge(trans_set, n - 1)
                b = n % 2
                dve.tensor_scalar(xn1[:, b, :], xs[:, n, :], mv[:, b, 0:1], rs[:, b, 3:4], ALU.subtract,
                                  ALU.mult).then_inc(norm_set, 1)

            def turned_lo(n):
                dve.wait_ge(hi_set, n + 1)
                dve.tensor_tensor(x1T[1][:, :, n * P:(n + 1) * P], trans[n % 2], x1T[0][:, :, n * P:(n + 1) * P],
                                  ALU.subtract).then_inc(lo_set, 1)

            def w_part(q):
                dve.wait_ge(w_hi, q + 1)
                dve.scalar_tensor_tensor(out=ws[1][:, 2 * q:2 * q + 2, :], in0=w_stage[:, q % 2, :, :], scalar=WS,
                                         in1=ws[0][:, 2 * q:2 * q + 2, :], op0=ALU.mult, op1=ALU.subtract).then_inc(w_lo, 1)

            def stats1(n):
                dve.wait_ge(x_loaded[n], 16)
                if n >= 2:
                    dve.wait_ge(norm_set, n - 1)
                norm_stats(n, stats_set)

            def h_out(n):
                dve.wait_ge(h_rowed, n + 1)
                dve.tensor_tensor(hs[1][:, n, :], h_row[:, :], hs[0][:, n, :], ALU.subtract).then_inc(h_lo, 1)
                if n >= 1:
                    dve.wait_ge(al_dotted, n)
                for i in range(2):
                    last = dve.tensor_tensor_reduce(dots[i][:, :], h_row[:, :], a_rows[:, i, :], 1.0, 0.0, ALU.mult, ALU.add,
                                                    alr[:, i, n:n + 1])
                last.then_inc(al_dotted, 1)

            dots = [elu_neg, elu_pos]
            stats1(0)
            stats1(1)
            for n in range(2):
                normalise(n)
                w_part(2 * n) if n == 0 else turned_lo(n)
                w_part(2 * n + 1) if n == 0 else w_part(2)
                turned_lo(0) if n == 0 else w_part(3)
            for n in range(T):
                if n + 2 < T:
                    stats1(n + 2)
                    normalise(n + 2)
                h_out(n)
                if n + 2 < T:
                    turned_lo(n + 2)

            dve.wait_ge(al_dotted, T)
            dve.tensor_scalar(nar[:, 0, :], alr[:, 1, :], -1.0, None, ALU.mult)
            dve.tensor_scalar(nar[:, 1, :], alr[:, 1, :], -SLOPE, None, ALU.mult)
            for n in range(T):
                if n >= 1:
                    dve.wait_ge(diag_used, n)
                dve.tensor_scalar(diag[:, :], ident[:, :], alr[:, 0, n:n + 1], None, ALU.mult).then_inc(diag_set, 1)

            def one_hots(j):
                begin = dve.value_load(bounds[0:1, 0, j:j + 1], min_val=0, max_val=P * T)
                end = dve.value_load(bounds[0:1, 1, j:j + 1], min_val=1, max_val=P * T)
                back = dve.value_load(bounds[0:1, 2, j:j + 1], min_val=0, max_val=P * T + P)
                with dve.Fori(begin, end) as q:
                    pair = nc.s_assert_within(
                        dve.snap(q + back - P * T), 0, P - 1,
                        skip_runtime_bounds_check_because="a tile's first and last pairs are pairs of chunks")
                    for b in range(2):
                        dve.wait_ge(hot_free, q * 2 + (b + 1))
                        dve.tensor_scalar(hot_src[:, b, :], nodes16[:, :], edge_src[:, bass.ds(pair * 2 + b, 1)], None, ALU.is_equal)
                        dve.tensor_scalar(hot_dst[:, b, :], nodes16[:, j * P:(j + 1) * P], edge_dst[:, bass.ds(pair * 2 + b, 1)],
                                          None, ALU.is_equal).then_inc(hot_ready, 1)

            def attention(j):
                dve.wait_ge(e_low_set, j + 1)
                dve.wait_ge(e_high_set, j + 1)
                dve.tensor_tensor(e_low[:, :], e_low[:, :], e_high[:, :], ALU.min).then_inc(acc_chain, 1)
                dve.wait_ge(acc_chain, j + 1)
                dve.wait_ge(count_set, j + 1)
                if j >= 1:
                    dve.wait_ge(att_hi, j)
                dve.scalar_tensor_tensor(out=att_row[:, :], in0=count_acc[j % 2], scalar=AS, in1=e_low[:, :], op0=ALU.mult,
                                         op1=ALU.mult).then_inc(att_set, 1)
                dve.wait_ge(att_set, j + 1)
                dve.wait_ge(att_hi, j + 1)
                dve.tensor_tensor(att[1][:, j, :], att_row[:, :], att[0][:, j, :], ALU.subtract).then_inc(att_lo, 1)

            edge_src = edgeT[:, 0:2, :].rearrange("p a c -> p (a c)")
            edge_dst = edgeT[:, 2:4, :].rearrange("p a c -> p (a c)")
            dve.wait_ge(bounds_set, 1)
            for j in range(T):
                one_hots(j)
                if j >= 1:
                    attention(j - 1)
            attention(T - 1)

            lns = [0]

            def link(ins):
                lns[0] += 1
                ins.then_inc(ln_chain, 1)
                dve.wait_ge(ln_chain, lns[0])

            def node_out(n):
                b = n % 2
                dve.wait_ge(sum_set, n + 1)
                dve.tensor_scalar(rsum[:, b, 0:1], sum_acc, AS * SUM_EPS, None, ALU.add).then_inc(sum_read, 1)
                dve.wait_ge(sum_read, n + 1)
                link(dve.reciprocal(rsum[:, b, 1:2], rsum[:, b, 0:1]))
                dve.wait_ge(agg_set, n + 1)
                dve.tensor_scalar(elu_neg[:, :], agg_acc[b], rsum[:, b, 1:2], 0.0, ALU.mult, ALU.min).then_inc(neg_set, 1)
                last = dve.tensor_scalar(elu_pos[:, :], agg_acc[b], rsum[:, b, 1:2], 0.0, ALU.mult, ALU.max)
                last.then_inc(agg_free, 1)
                dve.wait_ge(agg_free, n + 1)
                link(dve.tensor_tensor(elu_pos[:, :], elu_pos[:, :], xs[:, n, :], ALU.add))
                dve.wait_ge(exp_set, n + 1)
                link(dve.scalar_tensor_tensor(out=xs[:, n, :], in0=elu_neg[:, :], scalar=-1.0, in1=elu_pos[:, :], op0=ALU.add,
                                              op1=ALU.add))
                norm_stats(n, stats2_set)
                dve.wait_ge(rstd2_set, n + 1)
                if n >= 1:
                    dve.wait_ge(row_lo, n)
                dve.tensor_scalar(xn2[:, :], xs[:, n, :], mv[:, b, 0:1], rs[:, b, 3:4], ALU.subtract,
                                  ALU.mult).then_inc(norm2_set, 1)
                dve.wait_ge(row_hi, n + 1)
                dve.tensor_tensor(x_row[:, 1, :], xn2[:, :], x_row[:, 0, :], ALU.subtract).then_inc(row_lo, 1)
                dve.wait_ge(trans2_hi, n + 1)
                dve.tensor_copy(xT[:, 1, :, :], trans2[1]).then_inc(trans2_lo, 1)

            def split_lo(q, m, sl, staged):
                dve.wait_ge(d_hi if m == 2 else gu_hi, q + 1 if m == 2 else q * 2 + (m + 1))
                dve.scalar_tensor_tensor(out=weights[sl][m][1][:, :, :], in0=staged[m][:, :, :], scalar=WS,
                                         in1=weights[sl][m][0][:, :, :], op0=ALU.mult, op1=ALU.subtract)\
                    .then_inc(d_lo if m == 2 else gu_lo, 1)

            for n in range(T):
                node_out(n)
                if n in (1, 3, 5):
                    split_lo(0, n // 2, 0, stage0)

            def bc(ap, shape):
                return ap.to_broadcast(shape)

            def ranks(v, n, out_rank, ra, rb):
                mine = bc(v.unsqueeze(3), [P, T, n, n])
                other = bc(v.unsqueeze(2), [P, T, n, n])
                chain(dve.tensor_tensor(ra, other, mine, ALU.is_equal))
                chain(dve.tensor_tensor(ra, ra, bc(lower[:, 0:n, 0:n].unsqueeze(1), [P, T, n, n]), ALU.mult))
                chain(dve.tensor_tensor(rb, other, mine, ALU.is_gt))
                chain(dve.tensor_tensor(ra, ra, rb, ALU.add))
                chain(dve.tensor_reduce(out_rank, ra, X, ALU.add))

            dve.wait_ge(agg_done, 1)
            chain(dve.memset(lower[:, :, :], 0.0))
            for e in range(1, E):
                last = dve.memset(lower[:, e, 0:e], 1.0)
            chain(last)
            dve.wait_ge(consts_set, 8)
            chain(dve.tensor_copy(token[:, :], token_i[:, :]))
            chain(dve.tensor_scalar(valid[:, :], token[:, :], N - 0.5, None, ALU.is_lt))
            dve.wait_ge(scattered, 16)
            dve.wait_ge(logit_exp, 1)
            chain(dve.tensor_scalar(score[:, :, :], score[:, :, :], 1.0, None, ALU.add))
            chain(dve.reciprocal(score[:, :, :], score[:, :, :]))
            chain(dve.tensor_tensor(choice[:, :, :], score[:, :, :], bc(bias_row[:, :].unsqueeze(1), [P, T, E]), ALU.add))
            pairs = choice[:, :, :].rearrange("p t (g m) -> p t g m", m=EG)
            chain(dve.tensor_tensor(rg[:, :, :], pairs[:, :, :, 0], pairs[:, :, :, 1], ALU.add))
            nn = GROUPS * GROUPS
            ga = rank_a[:, :, :, :].rearrange("p t a b -> p (t a b)")[:, 0:T * nn].rearrange("p (t a b) -> p t a b", a=GROUPS, b=GROUPS)
            gb = rank_b[:, :, :, :].rearrange("p t a b -> p (t a b)")[:, 0:T * nn].rearrange("p (t a b) -> p t a b", a=GROUPS, b=GROUPS)
            ranks(rg[:, :, :], GROUPS, rg2[:, :, :], ga, gb)
            chain(dve.tensor_scalar(rg[:, :, :], rg2[:, :, :], TOP_GROUPS - 0.5, None, ALU.is_lt))
            chain(dve.tensor_tensor(pairs, pairs, bc(rg[:, :, :].unsqueeze(3), [P, T, GROUPS, EG]), ALU.mult))
            ranks(choice[:, :, :], E, r1[:, :, :], rank_a[:, :, :, :], rank_b[:, :, :, :])
            chain(dve.tensor_scalar(r2[:, :, :], r1[:, :, :], TOPK - 0.5, None, ALU.is_lt))
            chain(dve.tensor_tensor(sel[:, :, :], r2[:, :, :], bc(valid[:, :].unsqueeze(2), [P, T, E]), ALU.mult))
            dve.tensor_copy(sel16[:, :, :], sel[:, :, :]).then_inc(sel_set, 1)
            chain(dve.tensor_tensor(cw[:, :, :], r2[:, :, :], score[:, :, :], ALU.mult))
            chain(dve.tensor_reduce(rt[:, :], cw[:, :, :], X, ALU.add))
            chain(dve.tensor_scalar(rt[:, :], rt[:, :], 1e-20, None, ALU.add))
            chain(dve.reciprocal(rt2[:, :], rt[:, :]))
            chain(dve.tensor_scalar(rt2[:, :], rt2[:, :], ROUTED_SCALE, None, ALU.mult))
            chain(dve.tensor_tensor(cw[:, :, :], cw[:, :, :], bc(rt2[:, :].unsqueeze(2), [P, T, E]), ALU.mult))
            chain(dve.tensor_tensor(rank_a[:, :, :, :], bc(r2[:, :, :].unsqueeze(2), [P, T, E, E]),
                                    bc(lower[:, :, :].unsqueeze(1), [P, T, E, E]), ALU.mult))
            chain(dve.tensor_reduce(ranked[:, :, :], rank_a[:, :, :, :], X, ALU.add))

            def rank_weights():
                for i in range(TOPK):
                    chain(dve.scalar_tensor_tensor(out=choice[:, :, :], in0=ranked[:, :, :], scalar=float(i), in1=cw[:, :, :],
                                                   op0=ALU.is_equal, op1=ALU.mult))
                    chain(dve.tensor_reduce(rank_w[:, :, i], choice[:, :, :], X, ALU.add))
                chain(dve.tensor_scalar(r1[:, :, :], ranked[:, :, :], 1.0, None, ALU.add))

            def positions():
                dve.wait_ge(prefix_set, 1)
                prefix = route_acc[:, 0:PAIRS].rearrange("p (t e) -> p t e", e=E)
                total = route_acc[:, PAIRS:2 * PAIRS].rearrange("p (t e) -> p t e", e=E)
                chain(dve.memset(offs[:, 0, :], 0.0))
                for t in range(T):
                    chain(dve.tensor_tensor(offs[:, t + 1, :], offs[:, t, :], total[:, t, :], ALU.add))
                chain(dve.tensor_tensor(choice[:, :, :], prefix, offs[:, 0:T, :], ALU.add))
                chain(dve.tensor_copy(pos_i[:, :, :], choice[:, :, :]))
                dve.tensor_scalar(tile_i[:, :, :], pos_i[:, :, :], 7, None, ALU.arith_shift_right)
                chain(dve.tensor_scalar(slot_i[:, :, :], pos_i[:, :, :], P - 1, None, ALU.bitwise_and))
                dve.tensor_copy(kglob[:, :, :], tile_i[:, :, :])
                chain(dve.tensor_copy(slot[:, :, :], slot_i[:, :, :]))
                chain(dve.tensor_scalar(tiles_f[:, :], offs[:, T, :], float(P - 1), None, ALU.add))
                chain(dve.tensor_copy(tiles_i[:, :], tiles_f[:, :]))
                chain(dve.tensor_scalar(tiles_i[:, :], tiles_i[:, :], 7, None, ALU.arith_shift_right))
                chain(dve.tensor_copy(tiles_f[:, :], tiles_i[:, :]))
                chain(dve.tensor_scalar(tiles_f[:, :], tiles_f[:, :], float(MIN_TILES), None, ALU.max))
                chain(dve.memset(begin_f[:, 0:1], 0.0))
                for e in range(E):
                    chain(dve.tensor_tensor(begin_f[:, e + 1:e + 2], begin_f[:, e:e + 1], tiles_f[:, e:e + 1], ALU.add))
                chain(dve.tensor_copy(spans[:, :], begin_f[0:1, :]))
                chain(dve.tensor_tensor(kglob[:, :, :], kglob[:, :, :], bc(begin_f[:, 0:E].unsqueeze(1), [P, T, E]), ALU.add))
                chain(dve.scalar_tensor_tensor(out=slot[:, :, :], in0=slot[:, :, :], scalar=1.0, in1=sel[:, :, :], op0=ALU.add,
                                               op1=ALU.mult))
                chain(dve.tensor_scalar(slot[:, :, :], slot[:, :, :], -1.0, None, ALU.add))

            slot_c = slot[:, :, :].rearrange("p t e -> p (t e)")
            kglob_c = kglob[:, :, :].rearrange("p t e -> p (t e)")
            rank_c = r1[:, :, :].rearrange("p t e -> p (t e)")

            def pairs_hot(t0, t1):
                with dve.Fori(t0, t1) as t:
                    for e in range(E):
                        i = t * E + e
                        at_i = bass.ds(i, 1)
                        dve.tensor_scalar(hot_slot[:, at_i, :].rearrange("p a n -> p (a n)"), nodes16[:, 0:P], slot_c[:, at_i],
                                          None, ALU.is_equal)
                        dve.tensor_scalar(hot_tile[:, at_i, 0, :].rearrange("p a n -> p (a n)"), nodes16[:, 0:KT], kglob_c[:, at_i],
                                          token[:, bass.ds(t, 1)], ALU.is_equal, ALU.mult)
                        last = dve.tensor_scalar(hot_tile[:, at_i, 1, :].rearrange("p a n -> p (a n)"), nodes16[:, 0:KT],
                                                 kglob_c[:, at_i], rank_c[:, at_i], ALU.is_equal, ALU.mult)
                    last.then_inc(pairs_set, 1)

            def destinations():
                dve.wait_ge(pairs_summed, 1)
                tok, rk = route_acc[:, 0:KT], route_acc[:, KT:2 * KT]
                dve.tensor_copy(gather_at[:, :], tok)
                chain(dve.tensor_scalar(dest_a[:, :], rk, 0.5, 65536.0, ALU.is_lt, ALU.mult))
                chain(dve.scalar_tensor_tensor(out=dest_a[:, :], in0=rk, scalar=-1.0, in1=dest_a[:, :], op0=ALU.add, op1=ALU.add))
                chain(dve.scalar_tensor_tensor(out=dest_b[:, :], in0=tok, scalar=float(TOPK), in1=dest_a[:, :], op0=ALU.mult,
                                               op1=ALU.add))
                dve.tensor_copy(scatter_at[:, :], dest_b[:, :]).then_inc(dests_set, 1)

            def xT_lo(k):
                dve.wait_ge(x_turned, k + 1)
                dve.tensor_copy(xT[:, 1, :, :], xT_acc[1]).then_inc(xT_lo_set, 1)

            def ffn_tile(k, more=True, adds=None):
                dve.wait_ge(sig_set, k + 1)
                dve.scalar_tensor_tensor(out=gated[:, :], in0=g_acc, scalar=1 / WS, in1=sig[:, :], op0=ALU.mult,
                                         op1=ALU.mult).then_inc(gated_set, 1)
                dve.wait_ge(gated_set, k + 1)
                dve.scalar_tensor_tensor(out=act_row[:, :], in0=u_acc, scalar=1 / WS, in1=gated[:, :], op0=ALU.mult,
                                         op1=ALU.mult).then_inc(act_set, 1)
                if more:
                    xT_lo(k + 1)
                dve.wait_ge(act_hi, k + 1)
                dve.tensor_tensor(act_hl[:, 1, :], act_row[:, :], act_hl[:, 0, :], ALU.subtract).then_inc(act_lo, 1)
                if adds is not None:
                    dve.wait_ge(y_done, k)
                    dve.scalar_tensor_tensor(out=xs[:, adds, :], in0=y_acc, scalar=1 / WS, in1=xs[:, adds, :], op0=ALU.mult,
                                             op1=ALU.add).then_inc(y_read, 1)
                dve.wait_ge(act_turned, k + 1)
                dve.tensor_copy(actT[:, :, :, :], actT_acc).then_inc(actT_set, 1)

            xT_lo(0)
            rank_weights()
            ffn_tile(0)
            positions()
            ffn_tile(1, adds=0)
            pairs_hot(0, T // 2)
            ffn_tile(2, adds=1)
            pairs_hot(T // 2, T)
            ffn_tile(3, adds=2)
            destinations()
            dve.wait_ge(dests_set, 1)
            for m in range(MATS):
                split_lo(1, m, 1, stage)
            ffn_tile(4, adds=3)

            def expert(q, sl):
                begin = dve.value_load(spans[0:1, bass.ds(q - 1, 1)], min_val=0, max_val=TE)
                end = dve.value_load(spans[0:1, bass.ds(q, 1)], min_val=MIN_TILES, max_val=TE)
                split_lo(q + 1, 0, 1 - sl, stage)
                split_lo(q + 1, 1, 1 - sl, stage)
                with dve.If(begin > 0):
                    ffn_tile(begin + T0)
                with dve.Else():
                    ffn_tile(begin + T0, adds=T0 - 1)
                split_lo(q + 1, 2, 1 - sl, stage)
                ffn_tile(begin + T0 + 1)
                with dve.Fori(begin + 2, end) as j:
                    ffn_tile(j + T0)

            with dve.Fori(0, E // 2) as i:
                expert(i * 2 + 1, 1)
                expert(i * 2 + 2, 0)
            tiles = dve.value_load(spans[0:1, E:E + 1], min_val=E * MIN_TILES, max_val=TE)

            def add_results(t):
                rows = P if t < T - 1 else TAIL
                dve.wait_ge((y_in_loaded0, y_in_loaded1)[t % 2], 16 * (t // 2 + 1))
                if t < T - 1:
                    dve.wait_ge(y_read, t + 1)
                for i in range(TOPK):
                    last = dve.scalar_tensor_tensor(out=xs[0:rows, t, :], in0=y_in[t % 2][0:rows, i, :],
                                                    scalar=rank_w[0:rows, t, i:i + 1], in1=xs[0:rows, t, :], op0=ALU.mult,
                                                    op1=ALU.add)
                    if i < TOPK - 1:
                        last.then_inc(sum_chain, 1)
                        dve.wait_ge(sum_chain, (TOPK - 1) * t + i + 1)
                last.then_inc(y_summed, 1)

            ffn_tile(tiles + T0)
            ffn_tile(tiles + T0 + 1, adds=T0)
            for t in range(T0 + 2, T):
                add_results(2 * (t - T0 - 2))
                add_results(2 * (t - T0 - 2) + 1)
                ffn_tile(tiles + t, more=t < T - 1, adds=t - 1)
            for t in range(2 * (T - T0 - 2), T):
                add_results(t)
            dve.wait_ge(y_summed, T)
            dve.wait_ge(y_done, tiles + T)
            dve.scalar_tensor_tensor(out=xs[:, T - 1, :], in0=y_acc, scalar=1 / WS, in1=xs[:, T - 1, :], op0=ALU.mult,
                                     op1=ALU.add).then_inc(y_read, 1)

        @block.tensor
        def _(pe):
            pe.wait_ge(consts_set, 8)
            pe.wait_ge(edges_floated, 1)
            for i in range(4):
                last = pe.transpose(prep[:, i * P:(i + 1) * P], edges_f[:, i, :], ident[:, :])
            last.then_inc(edges_turned, 1)
            pe.wait_ge(edgeT_set, 1)
            pe.wait_ge(cand_set, 1)
            pe.transpose(prep[0:4 * T, 0:P], cand[:, :, :, :].rearrange("p a g t -> p (a g t)"), ident[:, :]).then_inc(cand_turned, 1)
            pe.wait_ge(cmax_set, 1)
            pe.matmul(prep[0:1, 0:4 * T], ones[0:4 * T, 0:1], diag[0:4 * T, 0:4 * T], start=True, stop=True).then_inc(cmax_turned, 1)
            pe.wait_ge(bounds_set, 1)
            pe.wait_ge(small_loaded, 32)
            for k in range(K):
                last = pe.transpose(prep[:, k * E:(k + 1) * E], gate_rows[:, k * P:(k + 1) * P], ident[0:E, 0:E])
            last.then_inc(gate_turned, 1)

            def turn(n):
                pe.wait_ge(norm_set, n + 1)
                if n >= 2:
                    pe.wait_ge(lo_set, n - 1)
                for k in range(K):
                    last = pe.transpose(trans[n % 2][:, k, :], xn1[:, n % 2, k * P:(k + 1) * P], ident[:, :])
                last.then_inc(trans_set, 1)

            def three_pass(out_ap, lhs, rhs, k, nk, cols, closes=True):
                for li, ri in ((0, 0), (0, 1), (1, 0)):
                    for c0, c1 in cols:
                        last = pe.matmul(out_ap[:, c0:c1], lhs(li), rhs(ri)[:, c0:c1], start=(k == 0 and li == ri),
                                         stop=(closes and k == nk - 1 and li == 1))
                return last

            HALVES = [(0, HALF), (HALF, D)]

            def h_product(n):
                pe.wait_ge(lo_set, n + 1)
                if n >= 2:
                    pe.wait_ge(h_rowed, n - 1)
                elif n == 0:
                    pe.wait_ge(gate_lo, 1)
                for k in range(K):
                    if n == 0 and k % 2 == 0:
                        pe.wait_ge(w_lo, k // 2 + 1)
                    last = three_pass(h_acc[n % 2], lambda i: x1T[i][:, k, n * P:(n + 1) * P], lambda i: ws[i][:, k, :], k, K, HALVES)
                last.then_inc(h_set, 1)

            turn(0)
            turn(1)
            for n in range(T):
                h_product(n)
                if n + 2 < T:
                    turn(n + 2)

            pe.wait_ge(lo_set, T)
            for n in range(T):
                pe.wait_ge(diag_set, n + 1)
                last = pe.matmul(al_acc[:, n * P:(n + 1) * P], ones[:, :], diag[:, :], start=True, stop=True)
                last.then_inc(diag_used, 1)

            def counts(j):
                acc = count_acc[j % 2]
                if j == 0:
                    pe.wait_ge(al_copied, 1)
                    pe.wait_ge(bounds_set, 1)
                elif j == 1:
                    pe.wait_ge(h_lo, T)
                    pe.wait_ge(h_rowed, T)
                else:
                    pe.wait_ge(att_set, j - 1)
                for c0, w in CH:
                    pe.matmul(acc[:, c0:c0 + 1], zero16[:, :], zero16[:, 0:1], start=True, stop=False, skip_group_check=True)
                begin = pe.value_load(bounds[0:1, 0, j:j + 1], min_val=0, max_val=P * T)
                end = pe.value_load(bounds[0:1, 1, j:j + 1], min_val=1, max_val=P * T)
                with pe.Fori(begin, end) as q:
                    for b in range(2):
                        pe.wait_ge(hot_ready, q * 2 + (b + 1))
                        for c0, w in CH:
                            last = pe.matmul(acc[:, c0:c0 + w], hot_dst[:, b, :], hot_src[:, b, c0:c0 + w], start=False,
                                             stop=False, skip_group_check=True)
                        last.then_inc(hot_free, 1)
                for c0, w in CH:
                    last = pe.matmul(acc[:, c0:c0 + 1], zero16[:, :], zero16[:, 0:1], start=False, stop=True, skip_group_check=True)
                last.then_inc(count_set, 1)

            pe.sem_inc(hot_free, 2)
            for j in range(T):
                counts(j)

            def aggregate(n):
                b = n % 2
                if n == 0:
                    pe.wait_ge(att_lo, T)
                if n >= 2:
                    pe.wait_ge(agg_free, n - 1)
                if n >= 1:
                    pe.wait_ge(sum_read, n)
                for j in range(T):
                    for i in range(2):
                        last = pe.matmul(sum_acc, att[i][:, j, n * P:(n + 1) * P], ones16, start=(j == 0 and i == 0),
                                         stop=(j == T - 1 and i == 1))
                last.then_inc(sum_set, 1)
                for j in range(T):
                    last = three_pass(agg_acc[b], lambda i: att[i][:, j, n * P:(n + 1) * P], lambda i: hs[i][:, j, :], j, T, HALVES)
                last.then_inc(agg_set, 1)

            def turn_rows(dst):
                for i in range(2):
                    for k in range(K):
                        last = pe.transpose(dst[i][:, k, :], x_row[:, i, k * P:(k + 1) * P], ident16[:, :])
                return last

            def turn2(n):
                pe.wait_ge(row_lo, n + 1)
                if n >= 1:
                    pe.wait_ge(trans2_lo, n)
                turn_rows(trans2).then_inc(trans2_set, 1)

            def logits(n):
                pe.wait_ge(trans2_lo, n + 1)
                for k in range(K):
                    for li, ri in ((0, 0), (0, 1), (1, 0)):
                        last = pe.matmul(logit_acc[:, n, :], xT[:, li, k, :], gateT[ri][:, k, :],
                                         start=(k == 0 and li == ri), stop=(k == K - 1 and li == 1))
                last.then_inc(logits_set, 1)

            for n in range(T):
                aggregate(n)
                if n == T - 1:
                    last = pe.matmul(bank[0:1, 5, 511:512], zero16[:, 0:1], zero16[:, 0:1], start=True, stop=True)
                    last.then_inc(agg_done, 1)
                if n >= 2:
                    logits(n - 2)
                if n >= 1:
                    turn2(n - 1)
            logits(T - 2)
            turn2(T - 1)
            logits(T - 1)

            def gate_up(k, sl):
                pe.wait_ge(xT_hi_set, k + 1)
                pe.wait_ge(xT_lo_set, k + 1)
                for b in range(K):
                    for li, ri in ((0, 0), (0, 1), (1, 0)):
                        for m, acc in enumerate((g_acc, u_acc)):
                            last = pe.matmul(acc, xT[:, li, b, :], weights[sl][m][ri][:, b, :], start=(b == 0 and li == ri),
                                             stop=(b == K - 1 and li == 1))
                last.then_inc(gu_done, 1)

            def turn_x(k):
                if isinstance(k, int) and k < T0:
                    pe.wait_ge(rows_loaded, (k + 1) * 16)
                else:
                    pe.wait_ge(gathered, (k - (T0 - 1)) * 16)
                turn_rows(xT_acc).then_inc(x_turned, 1)

            def down(k, sl, emptied, count):
                pe.wait_ge(actT_set, k + 1)
                if emptied is not None:
                    pe.wait_ge(emptied, count)
                for b in range(KI):
                    last = three_pass(y_acc, lambda i: actT[:, i, b, :], lambda i: weights[sl][2][i][:, b, :], b, KI, HALVES)
                last.then_inc(y_done, 1)

            def turn_act(k):
                pe.wait_ge(act_lo, k + 1)
                for i in range(2):
                    for b in range(KI):
                        last = pe.transpose(actT_acc[:, i, b, :], act_hl[:, i, b * P:(b + 1) * P], ident16[:, :])
                last.then_inc(act_turned, 1)

            pe.wait_ge(logit_exp, 1)
            turn_x(0)
            pe.wait_ge(gu_lo, 2)
            for k in range(T0):
                if k == 0:
                    pe.wait_ge(agg_free, T)
                gate_up(k, 0)
                if k >= 1:
                    turn_x(k + 1)
                    if k == 1:
                        pe.wait_ge(d_lo, 1)
                    down(k - 1, 0, y_read if k >= 2 else None, k - 1)
                else:
                    turn_x(1)
                turn_act(k)
                if k == 0:
                    pe.wait_ge(sel_set, 1)
                    flat = sel16[:, :, :].rearrange("p t e -> p (t e)")
                    pe.matmul(route_acc[:, 0:PAIRS], before16[:, :], flat, start=True, stop=True)
                    last = pe.matmul(route_acc[:, PAIRS:2 * PAIRS], ones16w[:, :], flat, start=True, stop=True)
                    last.then_inc(prefix_set, 1)
                if k == 3:
                    pe.wait_ge(pairs_set, T)
                    for i in range(PAIRS):
                        last = pe.matmul(route_acc[:, 0:2 * KT], hot_slot[:, i, :], hot_tile[:, i, :, :].rearrange("p a n -> p (a n)"),
                                         start=(i == 0), stop=(i == PAIRS - 1))
                    last.then_inc(pairs_summed, 1)

            def expert(q, sl):
                begin = pe.value_load(spans[0:1, bass.ds(q - 1, 1)], min_val=0, max_val=TE)
                end = pe.value_load(spans[0:1, bass.ds(q, 1)], min_val=MIN_TILES, max_val=TE)
                pe.wait_ge(gu_lo, q * 2 + 2)
                gate_up(begin + T0, sl)
                turn_x(begin + T0 + 1)
                with pe.If(begin > 0):
                    pe.wait_ge(y_row_set, begin + 1)
                with pe.Else():
                    pe.wait_ge(y_read, T0 - 1)
                down(begin + T0 - 1, 1 - sl, None, 0)
                turn_act(begin + T0)
                pe.wait_ge(d_lo, q + 1)
                for j in (begin + 1,):
                    gate_up(j + T0, sl)
                    turn_x(j + T0 + 1)
                    with pe.If(begin > 0):
                        pe.wait_ge(y_row_set, begin + 2)
                    with pe.Else():
                        pe.wait_ge(y_read, T0)
                    down(j + T0 - 1, sl, None, 0)
                    turn_act(j + T0)
                with pe.Fori(begin + 2, end) as j:
                    gate_up(j + T0, sl)
                    turn_x(j + T0 + 1)
                    down(j + T0 - 1, sl, y_row_set, j + 1)
                    turn_act(j + T0)

            pe.wait_ge(dests_set, 1)
            with pe.Fori(0, E // 2) as i:
                expert(i * 2 + 1, 1)
                expert(i * 2 + 2, 0)
            tiles = pe.value_load(spans[0:1, E:E + 1], min_val=E * MIN_TILES, max_val=TE)
            pe.wait_ge(gu_lo, 2 * (E + 2))
            for t in range(T0, T):
                gate_up(tiles + t, 1)
                if t < T - 1:
                    turn_x(tiles + t + 1)
                if t == T0:
                    down(tiles + t - 1, 0, y_row_set, tiles + 1)
                    pe.wait_ge(d_lo, E + 2)
                elif t == T0 + 1:
                    down(tiles + t - 1, 1, y_row_set, tiles + 2)
                else:
                    down(tiles + t - 1, 1, y_read, t - 1)
                turn_act(tiles + t)
            down(tiles + T - 1, 1, y_read, T - 1)


_INS = ["x", "src", "dst", "L0_gnn_W", "L0_gnn_a", "L0_ffn_gate_w", "L0_ffn_correction_bias", "L0_ffn_Wg", "L0_ffn_Wu",
        "L0_ffn_Wd", "L0_ffn_Wg_s", "L0_ffn_Wu_s", "L0_ffn_Wd_s"]


def kernel(**inputs):
    import numpy as np
    import concourse.bacc as bacc
    from concourse.bass_utils import run_bass_kernel_spmd

    nc = bacc.Bacc("TRN2", target_bir_lowering=False, num_devices=1, dynamic_dma_scratch_size=4096)
    arrays, args = {}, []
    for name in _INS:
        a = np.ascontiguousarray(inputs[name])
        arrays[f"in_{name}"] = a
        args.append(nc.dram_tensor(f"in_{name}", a.shape, mybir.dt.from_np(a.dtype), kind="ExternalInput").ap())
    shape = inputs["x"].shape
    args.append(nc.dram_tensor("out", shape, F32, kind="ExternalOutput").ap())
    build(nc, *args)
    r = run_bass_kernel_spmd(nc, [arrays], core_ids=[0])
    return r.results[0]["out"]
```

```python
import concourse.bass as bass
from concourse import mybir

F32 = mybir.dt.float32
F16 = mybir.dt.float16
I32 = mybir.dt.int32
ALU = mybir.AluOpType
ACT = mybir.ActivationFunctionType
X = mybir.AxisListType.X

P = 128
WS = 256.0
AS = 2.0
LN_EPS = 1e-5
SUM_EPS = 1e-5
SLOPE = 0.1
ROUTED_SCALE = 2.5
MIN_TILES = 3
TOPK = 4
GROUPS = 4
TOP_GROUPS = 2
PAIRS_STEP = 5
STEP = 2 * PAIRS_STEP


def build(nc, x_in, src_in, dst_in, w_in, a_in, gate_in, bias_in, wg_in, wu_in, wd_in,
          wgs_in, wus_in, wds_in, out):
    N, D = x_in.shape
    NE = src_in.shape[0]
    E, _, FI = wg_in.shape
    T = -(-N // P)
    NP = T * P
    TAIL = N - (T - 1) * P
    K = D // P
    KI = FI // P
    C = -(-NE // P)
    CB = C - P
    FULL = NE // P
    REST = NE - FULL * P
    HALF = 512
    EG = E // GROUPS
    assert T % 2 == 0 and 0 < CB <= P and D == 2 * HALF and K == 8 and FI == HALF and NP == 2 * HALF + 256
    CH = [(0, HALF), (HALF, HALF), (2 * HALF, NP - 2 * HALF)]
    T0 = T // 2
    ORDER = [T - 2, T - 1] + list(range(T - 2))
    TE = N * TOPK // P + E * MIN_TILES
    KT = 64
    assert TE <= KT and FI == HALF and T - T0 >= 3 and E % 2 == 0 and T == 10

    x_rows = nc.dram_tensor("x_rows", [NP, 2 * D], F16, kind="Internal").ap()
    y_rows = nc.dram_tensor("y_rows", [NP * TOPK, D], F32, kind="Internal").ap()

    base = nc.sbuf_base + (-nc.sbuf_base) % 64
    cursor = [base]

    def at(name, offset, shape, dt):
        return nc.alloc_sbuf_tensor_at(name, shape, dt, offset=offset)

    def region(nbytes):
        start = cursor[0]
        cursor[0] += nbytes + (-nbytes) % 32
        assert cursor[0] <= nc.sbuf_usable_end, (cursor[0], nc.sbuf_usable_end)
        return start

    R_X = region(T * D * 4)
    R_A = region(T * NP * 4)
    R_B = region(T * D * 4)
    R_C = region(T * D * 4)
    R_D = region(2 * K * FI * 4)
    R_T = region(12288)

    xs = at("xs", R_X, [P, T, D], F32)
    x1T = [at(f"x1T{i}", R_A + i * K * NP * 2, [P, K, NP], F16) for i in range(2)]
    xn1 = at("xn1", R_A + K * NP * 4, [P, 2, D], F32)
    att = [at(f"att{i}", R_A + i * T * NP * 2, [P, T, NP], F16) for i in range(2)]
    hs = [at(f"hs{i}", R_B + i * T * D * 2, [P, T, D], F16) for i in range(2)]
    ws = [at(f"ws{i}", R_C + i * K * D * 2, [P, K, D], F16) for i in range(2)]
    w_stage = at("w_stage", R_D, [P, 2, 2, D], F32)
    h_row = at("h_row", R_T + D * 4, [P, D], F32)
    a_rows = at("a_rows", R_D + 24576, [P, 2, D], F32)
    edge_w = at("edge_w", R_D, [P, 2, NP], F32)
    att_row = at("att_row", R_D + 2 * NP * 4, [P, 2, NP], F32)
    hot_src = at("hot_src", R_C, [P, STEP, NP], F16)
    hot_dst = at("hot_dst", R_C + STEP * NP * 2, [P, STEP, P], F16)
    al_row = at("al_row", R_C + STEP * (NP + P) * 2, [P, NP], F32)
    al_relu = at("al_relu", R_C + STEP * (NP + P) * 2 + NP * 4, [P, NP], F32)
    diags = at("diags", R_D + 2 * NP * 4, [P, T, P], F32)
    MAT = K * FI * 4
    MATS = 3
    YB = 3
    slot_at = [R_C, R_A]
    weights = [[[at(f"w{sl}{m}{i}", slot_at[sl] + m * MAT + i * MAT // 2, [P, KI if m == 2 else K, D if m == 2 else FI], F16)
                 for i in range(2)] for m in range(MATS)] for sl in range(2)]
    stage_at = [R_C + MATS * MAT, R_A + MATS * MAT, R_A + (MATS + 1) * MAT]
    stage = [at(f"stage{m}", stage_at[m], [P, KI if m == 2 else K, D if m == 2 else FI], F32) for m in range(MATS)]
    stage0 = [stage[0], stage[0], at("stage_first_down", stage_at[0], [P, KI, D], F32)]
    x_row = at("x_row", R_D + 24576, [P, 2, D], F16)
    xT = at("xT", R_D + 28672, [P, 2, K, P], F16)
    y_row = at("y_row", R_A + (MATS + 2) * MAT, [P, D], F32)
    y_in = [at(f"y_in{b}", stage_at[b], [P, TOPK - 1, D], F32) for b in range(YB)]
    y_first = at("y_first", R_A + 5 * MAT + 4096, [P, D], F32)
    act_hl = at("act_hl", R_T + 6144, [P, 2, FI], F16)
    actT = at("actT", R_T + 8192, [P, 2, KI, P], F16)
    elu_neg = at("elu_neg", R_T, [P, D], F32)
    elu_pos = at("elu_pos", R_T + 4096, [P, D], F32)
    xn2 = at("xn2", R_T + 8192, [P, D], F32)
    sig = at("sig", R_T, [P, HALF], F32)
    gated = at("gated", R_T + 2048, [P, HALF], F32)
    act_row = at("act_row", R_T + 4096, [P, HALF], F32)

    early_at = [R_T + 8192]
    late_at = [R_A + 5 * MAT + 4096]

    def early(name, shape, dt):
        n = mybir.dt.size(dt)
        for d in shape[1:]:
            n *= d
        n += -n % 32
        early_at[0] += n
        assert early_at[0] <= R_T + 12288
        return at(name, early_at[0] - n, shape, dt)

    def late(name, shape, dt):
        n = mybir.dt.size(dt)
        for d in shape[1:]:
            n *= d
        n += -n % 32
        late_at[0] += n
        assert late_at[0] <= R_C
        return at(name, late_at[0] - n, shape, dt)

    def small(name, shape, dt):
        n = 1
        for s in shape[1:]:
            n *= s
        return at(name, region(n * mybir.dt.size(dt)), shape, dt)

    ident = small("ident", [P, P], F32)
    ident16 = small("ident16", [P, P], F16)
    before16 = small("before16", [P, P], F16)
    ones = early("ones", [P, P], F32)
    ones16w = small("ones16", [P, P], F16)
    ones16 = ones16w[:, 0:1]
    zero16 = small("zero16", [P, P], F16)
    iota_i = at("iota_i", R_B, [P, NP], I32)
    nodes16 = small("nodes16", [P, NP], F16)
    edges_i = at("edges_i", R_B + 5120, [P, 4, P], I32)
    edges_f = at("edges_f", R_B + 8192, [P, 4, P], F32)
    STEPS = -(-P // PAIRS_STEP)
    LAST = STEPS * PAIRS_STEP
    LEAD = LAST * T
    edgeT = early("edgeT", [P, 2, 2 * LAST], F32)
    edge_src = edgeT[:, 0, :]
    edge_dst = edgeT[:, 1, :]
    step_over = at("step_over", R_B + 19456, [1, T, STEPS], F32)
    gate_rows = at("gate_rows", R_B + 12288, [E, D], F32)
    gateT = [small(f"gateT{i}", [P, K, E], F16) for i in range(2)]
    bias_row = small("bias_row", [P, E], F32)
    stats = small("stats", [P, 2, 2, 6], F32)
    mv = small("mv", [P, 2, 2], F32)
    rs = small("rs", [P, 2, 4], F32)
    mhalf = small("mhalf", [P, 1], F32)
    alr = early("alr", [P, 2, T], F32)
    nar = early("nar", [P, T], F32)
    diag = early("diag", [P, P], F32)
    sum_eps = small("sum_eps", [P, T], F32)
    rsum = small("rsum", [P, 2, 2], F32)
    span = small("span", [P, 2, 2], F32)
    pads = at("pads", R_B + 16384, [P, 2, P], F32)
    pair_i = small("pair_i", [P, 2], I32)
    pair_f = small("pair_f", [P, 2], F32)
    first_i = small("first_i", [P, T], I32)
    first_f = small("first_f", [P, 2, T], F32)
    need = at("need", R_B + 17408, [P, 2, 2, T], F32)
    cand = at("cand", R_B + 18432, [P, 2, 2, T], F32)
    cmax = small("cmax", [P, 1], F32)
    crow = small("crow", [1, 2, T], F32)
    lens = small("lens", [1, T], F32)
    bounds_f = small("bounds_f", [1, 3, T], F32)
    bounds = small("bounds", [1, 3, T], I32)
    PAIRS = T * E
    hot_slot = at("hot_slot", R_A, [P, PAIRS, P], F16)
    hot_tile = at("hot_tile", R_A + PAIRS * P * 2, [P, PAIRS, 2, KT], F16)
    r_at = [R_A + PAIRS * (P + 2 * KT) * 2]

    def routing(name, shape, dt=F32):
        n = 4
        for d in shape[1:]:
            n *= d
        n += -n % 32
        r_at[0] += n
        assert r_at[0] <= R_A + MATS * MAT
        return at(name, r_at[0] - n, shape, dt)

    rank_a = routing("rank_a", [P, T, E, E])
    rank_b = routing("rank_b", [P, T, E, E])
    lower = routing("lower", [P, E, E])
    choice, r1, r2, sel, cw, ranked, kglob, slot = (
        late(n, [P, T, E], F32) for n in ("choice", "r1", "r2", "sel", "cw", "ranked", "kglob", "slot"))
    pos_i = late("pos_i", [P, T, E], I32)
    tile_i = late("tile_i", [P, T, E], I32)
    slot_i = late("slot_i", [P, T, E], I32)
    offs = late("offs", [P, T + 1, E], F32)
    tiles_f = routing("tiles_f", [P, E])
    tiles_i = routing("tiles_i", [P, E], I32)
    begin_f = routing("begin_f", [P, E + 1])
    sel16 = routing("sel16", [P, T, E], F16)
    valid = routing("valid", [P, T])
    rg = routing("rg", [P, T, GROUPS])
    rg2 = routing("rg2", [P, T, GROUPS])
    rt = routing("rt", [P, T])
    rt2 = routing("rt2", [P, T])
    dest_a = routing("dest_a", [P, KT])
    dest_b = routing("dest_b", [P, KT])
    token_i = small("token_i", [P, T], I32)
    token = late("token", [P, T], F32)
    score = late("score", [P, T, E], F32)
    assert late_at[0] >= R_A + 5 * MAT + 4096 + D * 4
    rank_w = late("rank_w", [P, T, TOPK], F32)
    gather_at = late("gather_at", [P, KT], I32)
    scatter_at = late("scatter_at", [P, KT], I32)
    gather_now = small("gather_now", [P, 1], mybir.dt.uint32)
    scatter_now = small("scatter_now", [P, 1], mybir.dt.uint32)
    spans = small("spans", [1, E + 1], I32)

    bank = nc.alloc_psum_tensor("bank", [P, 8, HALF], F32)
    trans = [bank[:, 2 * b:2 * b + 2, :].rearrange("p a (k n) -> p (a k) n", n=P) for b in range(2)]
    h_acc = [bank[:, 4 + 2 * b:6 + 2 * b, :].rearrange("p a n -> p (a n)") for b in range(2)]
    count_acc = [bank[:, 3 * b:3 * b + 3, :].rearrange("p a n -> p (a n)")[:, 0:NP] for b in range(2)]
    al_acc = count_acc[1]
    prep = bank[:, 7, :]
    agg_acc = [bank[:, 2 * b:2 * b + 2, :].rearrange("p a n -> p (a n)") for b in range(2)]
    sum_acc = bank[:, 4, 0:1]
    logit_acc = bank[:, 5, 0:T * E].rearrange("p (t e) -> p t e", e=E)
    trans2 = [bank[:, 6 + i, :].bitcast(F16).rearrange("p (k n) -> p k n", n=P) for i in range(2)]
    g_acc, u_acc = bank[:, 0, :], bank[:, 1, :]
    y_acc = bank[:, 2:4, :].rearrange("p a n -> p (a n)")
    xT_acc = [bank[:, 4 + i, :].bitcast(F16).rearrange("p (k n) -> p k n", n=P) for i in range(2)]
    actT_acc = bank[:, 6, :].bitcast(F16).rearrange("p (i k n) -> p i k n", i=2, n=P)
    route_acc = bank[:, 7, :]

    x_tail_zeroed = nc.alloc_semaphore("x_tail_zeroed")
    edges_padded = nc.alloc_semaphore("edges_padded")
    small_loaded = nc.alloc_semaphore("small_loaded")
    edges_loaded = nc.alloc_semaphore("edges_loaded")
    consts_set = nc.alloc_semaphore("consts_set")
    iota_set = nc.alloc_semaphore("iota_set")
    pool_step = nc.alloc_semaphore("pool_step")
    stats_set = nc.alloc_semaphore("stats_set")
    rstd_set = nc.alloc_semaphore("rstd_set")
    norm_set = nc.alloc_semaphore("norm_set")
    trans_set = nc.alloc_semaphore("trans_set")
    hi_set = nc.alloc_semaphore("hi_set")
    lo_set = nc.alloc_semaphore("lo_set")
    w_hi = nc.alloc_semaphore("w_hi")
    w_lo = nc.alloc_semaphore("w_lo")
    h_set = nc.alloc_semaphore("h_set")
    h_hi = nc.alloc_semaphore("h_hi")
    h_lo = nc.alloc_semaphore("h_lo")
    h_rowed = nc.alloc_semaphore("h_rowed")
    half_dotted = nc.alloc_semaphore("half_dotted")
    al_dotted = nc.alloc_semaphore("al_dotted")
    diag_set = nc.alloc_semaphore("diag_set")
    eps_exp = nc.alloc_semaphore("eps_exp")
    nar_set = nc.alloc_semaphore("nar_set")
    al_rowed = nc.alloc_semaphore("al_rowed")
    al_copied = nc.alloc_semaphore("al_copied")
    edges_floated = nc.alloc_semaphore("edges_floated")
    edges_turned = nc.alloc_semaphore("edges_turned")
    edgeT_set = nc.alloc_semaphore("edgeT_set")
    cand_set = nc.alloc_semaphore("cand_set")
    cand_turned = nc.alloc_semaphore("cand_turned")
    cmax_set = nc.alloc_semaphore("cmax_set")
    crow_set = nc.alloc_semaphore("crow_set")
    cmax_turned = nc.alloc_semaphore("cmax_turned")
    bounds_set = nc.alloc_semaphore("bounds_set")
    gate_turned = nc.alloc_semaphore("gate_turned")
    gate_hi = nc.alloc_semaphore("gate_hi")
    gate_lo = nc.alloc_semaphore("gate_lo")
    dve_step = nc.alloc_semaphore("dve_step")
    hot_ready = nc.alloc_semaphore("hot_ready")
    hot_free = nc.alloc_semaphore("hot_free")
    count_set = nc.alloc_semaphore("count_set")
    z_relued = nc.alloc_semaphore("z_relued")
    z_summed = nc.alloc_semaphore("z_summed")
    weight_set = nc.alloc_semaphore("weight_set")
    att_set = nc.alloc_semaphore("att_set")
    att_hi = nc.alloc_semaphore("att_hi")
    att_lo = nc.alloc_semaphore("att_lo")
    sum_set = nc.alloc_semaphore("sum_set")
    sum_read = nc.alloc_semaphore("sum_read")
    agg_set = nc.alloc_semaphore("agg_set")
    agg_free = nc.alloc_semaphore("agg_free")
    neg_set = nc.alloc_semaphore("neg_set")
    exp_set = nc.alloc_semaphore("exp_set")
    stats2_set = nc.alloc_semaphore("stats2_set")
    rstd2_set = nc.alloc_semaphore("rstd2_set")
    norm2_set = nc.alloc_semaphore("norm2_set")
    trans2_set = nc.alloc_semaphore("trans2_set")
    row_hi = nc.alloc_semaphore("row_hi")
    row_lo = nc.alloc_semaphore("row_lo")
    row_stored = nc.alloc_semaphore("row_stored")
    trans2_hi = nc.alloc_semaphore("trans2_hi")
    trans2_lo = nc.alloc_semaphore("trans2_lo")
    logits_set = nc.alloc_semaphore("logits_set")
    logit_exp = nc.alloc_semaphore("logit_exp")
    agg_done = nc.alloc_semaphore("agg_done")
    ln_chain = nc.alloc_semaphore("ln_chain")
    gate_loaded = nc.alloc_semaphore("gate_loaded")
    up_loaded = nc.alloc_semaphore("up_loaded")
    down_loaded = nc.alloc_semaphore("down_loaded")
    gu_hi = nc.alloc_semaphore("gu_hi")
    gu_lo = nc.alloc_semaphore("gu_lo")
    d_hi = nc.alloc_semaphore("d_hi")
    d_lo = nc.alloc_semaphore("d_lo")
    sel_set = nc.alloc_semaphore("sel_set")
    prefix_set = nc.alloc_semaphore("prefix_set")
    tile_hot_set = nc.alloc_semaphore("tile_hot_set")
    tile_hot_read = nc.alloc_semaphore("tile_hot_read")
    tile_hot_scaled = nc.alloc_semaphore("tile_hot_scaled")
    slot_hot_set = nc.alloc_semaphore("slot_hot_set")
    pairs_summed = nc.alloc_semaphore("pairs_summed")
    dests_set = nc.alloc_semaphore("dests_set")
    rows_loaded = nc.alloc_semaphore("rows_loaded")
    gathered = nc.alloc_semaphore("gathered")
    x_turned = nc.alloc_semaphore("x_turned")
    xT_hi_set = nc.alloc_semaphore("xT_hi_set")
    xT_lo_set = nc.alloc_semaphore("xT_lo_set")
    gu_done = nc.alloc_semaphore("gu_done")
    sig_set = nc.alloc_semaphore("sig_set")
    gated_set = nc.alloc_semaphore("gated_set")
    act_set = nc.alloc_semaphore("act_set")
    act_hi = nc.alloc_semaphore("act_hi")
    act_lo = nc.alloc_semaphore("act_lo")
    act_turned = nc.alloc_semaphore("act_turned")
    actT_set = nc.alloc_semaphore("actT_set")
    y_done = nc.alloc_semaphore("y_done")
    y_read = nc.alloc_semaphore("y_read")
    y_row_set = nc.alloc_semaphore("y_row_set")
    gather_picked = nc.alloc_semaphore("gather_picked")
    scatter_picked = nc.alloc_semaphore("scatter_picked")
    scattered = nc.alloc_semaphore("scattered")
    pool_passed = nc.alloc_semaphore("pool_passed")
    first_loaded = nc.alloc_semaphore("first_loaded")
    first_added = nc.alloc_semaphore("first_added")
    y_in_loaded = [nc.alloc_semaphore(f"y_in_loaded{b}") for b in range(YB)]
    y_summed = nc.alloc_semaphore("y_summed")
    sum_chain = nc.alloc_semaphore("sum_chain")
    stored = nc.alloc_semaphore("stored")
    x_loaded = [nc.alloc_semaphore(f"x_loaded{t}") for t in range(T)]
    w_loaded = [nc.alloc_semaphore(f"w_loaded{b}") for b in range(2)]

    with nc.Block() as block:

        @block.sync
        def _(sp):
            def x_part(t):
                if t == T - 1:
                    sp.wait_ge(x_tail_zeroed, 1)
                rows = P if t < T - 1 else TAIL
                sp.dma_start(xs[0:rows, t, :], x_in[t * P:t * P + rows, :]).then_inc(x_loaded[t], 16)

            def w_part(q):
                if q >= 2:
                    sp.wait_ge(w_hi, q - 1)
                    sp.wait_ge(w_lo, q - 1)
                sp.dma_start(w_stage[:, q % 2, :, :],
                             w_in[2 * q * P:(2 * q + 2) * P, :].rearrange("(k p) n -> p k n", p=P)).then_inc(w_loaded[q % 2], 16)

            x_part(0)
            x_part(1)
            w_part(0)
            w_part(1)
            sp.wait_ge(edges_padded, 1)
            for i, e in enumerate((src_in, dst_in)):
                sp.dma_start(edges_i[:, 2 * i, :], e[0:P * P].rearrange("(c e) -> c e", e=P)).then_inc(edges_loaded, 16)
                sp.dma_start(edges_i[0:FULL - P, 2 * i + 1, :],
                             e[P * P:FULL * P].rearrange("(c e) -> c e", e=P)).then_inc(edges_loaded, 16)
                if REST:
                    sp.dma_start(edges_i[FULL - P:FULL - P + 1, 2 * i + 1, 0:REST],
                                 e[FULL * P:NE].rearrange("(c e) -> c e", c=1)).then_inc(edges_loaded, 16)
            sp.dma_start(gate_rows[:, :], gate_in).then_inc(small_loaded, 16)
            sp.dma_start(a_rows[:, :, :].rearrange("p a d -> p (a d)"), a_in.to_broadcast([P, 2 * D])).then_inc(small_loaded, 16)
            w_part(2)
            x_part(2)
            w_part(3)
            for t in range(3, T):
                x_part(t)
            matrices = ((gate_loaded, gu_hi, gu_lo), (up_loaded, gu_hi, gu_lo), (down_loaded, d_hi, d_lo))
            shared = (wgs_in, wus_in, wds_in)

            def as_blocks(w):
                return w.rearrange("(k p) n -> p k n", p=P)

            sp.wait_ge(att_lo, T)

            def rows_out(n):
                sp.wait_ge(row_lo, n + 1)
                sp.dma_start(x_rows[n * P:(n + 1) * P, :], x_row[:, :, :].rearrange("p a d -> p (a d)")).then_inc(row_stored, 16)

            for m, (loaded, _, _) in enumerate(matrices):
                if m >= 1:
                    sp.wait_ge(gu_hi, m)
                    sp.wait_ge(gu_lo, m)
                sp.dma_start(stage0[m][:, :, :], as_blocks(shared[m])).then_inc(loaded, 16)
                rows_out(2 * m)
                rows_out(2 * m + 1)
            for n in range(2 * MATS, T):
                rows_out(n)

            def first_rows(k):
                if k == 2:
                    sp.wait_ge(row_stored, 16 * T)
                    sp.wait_ge(trans2_set, T)
                else:
                    sp.wait_ge(x_turned, k)
                t = ORDER[k]
                sp.dma_start(x_row[:, :, :].rearrange("p a d -> p (a d)"), x_rows[t * P:(t + 1) * P, :]).then_inc(rows_loaded, 16)

            def first_in(i):
                if i >= 1:
                    sp.wait_ge(first_added, i)
                else:
                    sp.wait_ge(scattered, (below_first + 1) * 16)
                rows = P if i < T - 1 else TAIL
                sp.dma_start(y_first[0:rows, :], y_rows[i * P:i * P + rows, :]).then_inc(first_loaded, 16)

            def load_expert(q, mats):
                for m, (loaded, hi, lo) in enumerate(matrices):
                    if m == 0:
                        sp.wait_ge(d_hi, 1)
                        sp.wait_ge(d_lo, 1)
                    sp.wait_ge(hi, q if m == 2 else 2 * q)
                    sp.wait_ge(lo, q if m == 2 else 2 * q)
                    sp.dma_start(stage[m][:, :, :], as_blocks(mats[m])).then_inc(loaded, 16)

            first_rows(2)
            sp.wait_ge(agg_done, 1)
            load_expert(1, (wg_in[0], wu_in[0], wd_in[0]))
            for k in range(3, T0):
                first_rows(k)
            with sp.Fori(2, E) as q:
                load_expert(q, [w[bass.ds(q - 1, 1)].rearrange("a h i -> (a h) i") for w in (wg_in, wu_in, wd_in)])
            sp.wait_ge(dests_set, 1)
            below_first = sp.value_load(spans[0:1, E - TOPK + 1:E - TOPK + 2], min_val=E - TOPK, max_val=TE)
            load_expert(E, (wg_in[E - 1], wu_in[E - 1], wd_in[E - 1]))
            for i in range(3):
                first_in(i)
            load_expert(E + 1, shared)
            for i in range(3, T):
                first_in(i)

            tiles = sp.value_load(spans[0:1, E:E + 1], min_val=E * MIN_TILES, max_val=TE)

            def results_in(i):
                t = ORDER[i]
                rows = P if t < T - 1 else TAIL
                if i >= YB:
                    sp.wait_ge(y_summed, i - YB + 1)
                sp.dma_start(y_in[i % YB][0:rows, :, :],
                             y_rows[:, :].rearrange("(r p) d -> p r d", r=TOPK)[t * P:t * P + rows, 1:TOPK, :])\
                    .then_inc(y_in_loaded[i % YB], 16)

            def store(i):
                t = ORDER[i]
                rows = P if t < T - 1 else TAIL
                sp.dma_start(out[t * P:t * P + rows, :], xs[0:rows, t, :]).then_inc(stored, 16)

            sp.wait_ge(scattered, (tiles + 1) * 16)
            sp.wait_ge(d_lo, E + 2)
            sp.wait_ge(gu_lo, 2 * (E + 2))
            for i in range(YB):
                results_in(i)
            for i in range(T):
                if i + YB < T:
                    results_in(i + YB)
                else:
                    sp.wait_ge(y_summed, i + 1)
                store(i)
            sp.wait_ge(stored, 16 * T)

        @block.gpsimd
        def _(pool):
            pool.dma_start(bias_row[:, :], bias_in.rearrange("(a e) -> a e", a=1).to_broadcast([P, E])).then_inc(scattered, 16)
            pool.memset(xs[96:P, T - 1, :], 0.0).then_inc(x_tail_zeroed, 1)
            pool.wait_ge(x_tail_zeroed, 1)
            pool.memset(edges_i[:, :, :], -1).then_inc(edges_padded, 1)
            pool.memset(ident[:, :], 0.0).then_inc(pool_step, 1)
            pool.wait_ge(pool_step, 1)
            pool.affine_select(out=ident[:, :], in_=ident[:, :], compare_op=ALU.not_equal, fill=1.0, base=0,
                               pattern=[[-1, P]], channel_multiplier=1).then_inc(consts_set, 1)
            pool.memset(ones[:, :], 1.0).then_inc(consts_set, 1)
            pool.memset(ones16w[:, :], 1.0).then_inc(consts_set, 1)
            pool.memset(zero16[:, :], 0.0).then_inc(consts_set, 1)
            pool.memset(mhalf[:, :], -0.5).then_inc(consts_set, 1)
            pool.wait_ge(consts_set, 5)
            pool.memset(before16[:, :], 1.0).then_inc(pool_step, 1)
            pool.wait_ge(pool_step, 2)
            pool.affine_select(out=before16[:, :], in_=before16[:, :], compare_op=ALU.is_gt, fill=0.0, base=0,
                               pattern=[[1, P]], channel_multiplier=-1).then_inc(consts_set, 1)
            pool.iota(token_i[:, :], [[P, T]], base=0, channel_multiplier=1).then_inc(consts_set, 1)
            pool.tensor_copy(ident16[:, :], ident[:, :]).then_inc(consts_set, 1)
            pool.memset(edgeT[:, :, 2 * P:], -1.0).then_inc(consts_set, 1)
            pool.wait_ge(consts_set, 9)
            pool_steps = [2]

            def chain(ins):
                pool_steps[0] += 1
                ins.then_inc(pool_step, 1)
                pool.wait_ge(pool_step, pool_steps[0])

            def rstd(n, stats_ready, ready):
                b = n % 2
                v, y, q, r = (rs[:, b, i:i + 1] for i in range(4))
                pool.wait_ge(stats_ready, n + 1)
                if n >= 2:
                    pool.wait_ge(norm_set if ready is rstd_set else norm2_set, n - 1)
                elif ready is rstd2_set:
                    pool.wait_ge(norm_set, T)
                chain(pool.tensor_scalar(v, mv[:, b, 1:2], LN_EPS, None, ALU.add))
                chain(pool.tensor_tensor(y, v, mhalf[:, :], ALU.pow))
                chain(pool.tensor_tensor(q, y, y, ALU.mult))
                chain(pool.tensor_tensor(q, q, v, ALU.mult))
                chain(pool.tensor_scalar(q, q, -0.5, 1.5, ALU.mult, ALU.add))
                pool.tensor_tensor(r, y, q, ALU.mult).then_inc(ready, 1)

            rstd(0, stats_set, rstd_set)
            rstd(1, stats_set, rstd_set)
            pool.iota(iota_i[:, :], [[1, NP]], base=0, channel_multiplier=0).then_inc(iota_set, 1)
            pool.iota(pair_i[:, :], [[P, 2]], base=0, channel_multiplier=1).then_inc(iota_set, 1)
            pool.iota(first_i[:, :], [[P, T]], base=0, channel_multiplier=0).then_inc(iota_set, 1)
            for n in range(2, T):
                rstd(n, stats_set, rstd_set)
            def exponent(j):
                pool.wait_ge(z_relued, j + 1)
                pool.tensor_tensor(edge_w[:, j % 2, :], edge_w[:, j % 2, :], al_relu[:, :], ALU.subtract).then_inc(z_summed, 1)

            exponent(0)
            exponent(1)
            for j in range(T):
                pool.wait_ge(att_hi, j + 1)
                pool.tensor_tensor(att[1][:, j, :], att_row[:, j % 2, :], att[0][:, j, :], ALU.subtract).then_inc(att_lo, 1)
                if j + 2 < T:
                    exponent(j + 2)
            for n in range(T):
                rstd(n, stats2_set, rstd2_set)

            pool.wait_ge(tile_hot_set, 1)
            by_tile = hot_tile[:, :, :, :].rearrange("p (t e) a n -> p t e a n", e=E)
            pool.tensor_tensor(by_tile[:, :, :, 0, :], by_tile[:, :, :, 1, :],
                               token[:, :].unsqueeze(2).unsqueeze(3).to_broadcast([P, T, E, KT]), ALU.mult).then_inc(tile_hot_read, 1)
            pool.wait_ge(tile_hot_read, 1)
            pool.tensor_tensor(hot_tile[:, :, 1, :], hot_tile[:, :, 1, :],
                               r1[:, :, :].rearrange("p t e -> p (t e)").unsqueeze(2).to_broadcast([P, PAIRS, KT]),
                               ALU.mult).then_inc(tile_hot_scaled, 1)

            def gather(j):
                pool.wait_ge(x_turned, T0 + j)
                pool.sem_inc(pool_passed, 1)
                pool.tensor_copy(gather_now[:, :], gather_at[:, bass.ds(j, 1)].bitcast(mybir.dt.uint32)).then_inc(gather_picked, 1)
                pool.wait_ge(gather_picked, j + 1)
                pool.sem_inc(pool_passed, 1)
                pool.indirect_dma_start(out=x_row[:, :, :].rearrange("p a d -> p (a d)"), out_offset=None, in_=x_rows[:, :],
                                        in_offset=bass.IndirectOffsetOnAxis(ap=gather_now[:, :], axis=0)).then_inc(gathered, 16)

            def last_rows(t):
                pool.wait_ge(x_turned, tiles + t)
                pool.sem_inc(pool_passed, 1)
                pool.dma_start(x_row[:, :, :].rearrange("p a d -> p (a d)"), x_rows[ORDER[t] * P:(ORDER[t] + 1) * P, :]).then_inc(gathered, 16)

            def scatter(j, after):
                pool.wait_ge(y_row_set, after)
                pool.sem_inc(pool_passed, 1)
                pool.tensor_copy(scatter_now[:, :], scatter_at[:, bass.ds(j, 1)].bitcast(mybir.dt.uint32)).then_inc(scatter_picked, 1)
                pool.wait_ge(scatter_picked, after + 1)
                pool.sem_inc(pool_passed, 1)
                pool.indirect_dma_start(out=y_rows[:, :], out_offset=bass.IndirectOffsetOnAxis(ap=scatter_now[:, :], axis=0),
                                        in_=y_row[:, :], in_offset=None, bounds_check=NP * TOPK - 1,
                                        oob_is_err=False).then_inc(scattered, 16)

            pool.sem_inc(scatter_picked, 3)
            pool.sem_inc(y_row_set, 2)
            pool.wait_ge(dests_set, 1)
            tiles = pool.value_load(spans[0:1, E:E + 1], min_val=E * MIN_TILES, max_val=TE)
            for j in range(3):
                gather(j)
            with pool.Fori(3, tiles) as j:
                gather(j)
                scatter(nc.s_assert_within(pool.snap(j - 3), 0, KT - 1, skip_runtime_bounds_check_because="j is at least 3"), j)
            for j in range(T - T0):
                last_rows(T0 + j)
                if j < 3:
                    scatter(nc.s_assert_within(pool.snap(tiles - (3 - j)), 0, KT - 1,
                                               skip_runtime_bounds_check_because="there are at least E * MIN_TILES tiles"),
                            tiles + j)

        @block.scalar
        def _(act):
            def w_part(q):
                act.wait_ge(w_loaded[q % 2], 16 * (q // 2 + 1))
                act.activation(ws[0][:, 2 * q:2 * q + 2, :], w_stage[:, q % 2, :, :], ACT.Copy, scale=WS).then_inc(w_hi, 1)

            def turned_hi(n):
                act.wait_ge(trans_set, n + 1)
                act.copy(x1T[0][:, :, n * P:(n + 1) * P], trans[n % 2]).then_inc(hi_set, 1)

            def h_out(n):
                act.wait_ge(h_set, n + 1)
                if n == 0:
                    act.wait_ge(bounds_set, 1)
                act.activation(hs[0][:, n, :], h_acc[n % 2], ACT.Copy, scale=1 / WS).then_inc(h_hi, 1)
                if n >= 1:
                    act.wait_ge(al_dotted, n)
                else:
                    act.wait_ge(small_loaded, 32)
                act.activation(h_row[:, :], h_acc[n % 2], ACT.Copy, scale=1 / WS).then_inc(h_rowed, 1)

            w_part(0)
            turned_hi(0)
            w_part(1)
            turned_hi(1)
            act.wait_ge(edges_turned, 1)
            act.copy(edgeT[:, :, 0:2 * P], prep[:, 0:4 * P].rearrange("p (a c) -> p a c", a=2)).then_inc(edgeT_set, 1)
            w_part(2)
            w_part(3)
            act.wait_ge(gate_turned, 1)
            act.activation(gateT[0][:, :, :].rearrange("p k e -> p (k e)"), prep[:, 0:K * E], ACT.Copy, scale=WS).then_inc(gate_hi, 1)
            for n in range(T):
                h_out(n)
                if n + 2 < T:
                    turned_hi(n + 2)
            def z_relu(j):
                if j >= 2:
                    act.wait_ge(att_set, j - 1)
                act.activation(edge_w[:, j % 2, :], al_row[:, :], ACT.Relu, bias=alr[:, 1, j:j + 1], scale=1.0).then_inc(z_relued, 1)

            def edge_weight(j):
                act.wait_ge(z_summed, j + 1)
                act.activation(edge_w[:, j % 2, :], edge_w[:, j % 2, :], ACT.Exp, bias=nar[:, j:j + 1],
                               scale=-(1.0 - SLOPE)).then_inc(weight_set, 1)

            def row_hi_part(j):
                act.wait_ge(att_set, j + 1)
                act.copy(att[0][:, j, :], att_row[:, j % 2, :]).then_inc(att_hi, 1)

            act.wait_ge(al_rowed, 1)
            act.activation(al_relu[:, :], al_acc, ACT.Relu).then_inc(al_copied, 1)
            act.copy(al_row[:, :], al_acc).then_inc(al_copied, 1)
            act.wait_ge(al_copied, 2)
            act.wait_ge(nar_set, 1)
            z_relu(0)
            act.activation(sum_eps[:, :], sum_eps[:, :], ACT.Exp).then_inc(eps_exp, 1)
            edge_weight(0)
            z_relu(1)
            for j in range(1, T):
                row_hi_part(j - 1)
                edge_weight(j)
                if j + 1 < T:
                    z_relu(j + 1)
            row_hi_part(T - 1)

            def split_hi(q, m, sl, staged):
                act.wait_ge((gate_loaded, up_loaded, down_loaded)[m], 16 * (q + 1))
                act.activation(weights[sl][m][0][:, :, :], staged[m][:, :, :], ACT.Copy, scale=WS).then_inc(d_hi if m == 2 else gu_hi, 1)

            def turned2_hi(n):
                act.wait_ge(trans2_set, n + 1)
                if n >= 1:
                    act.wait_ge(logits_set, n)
                act.copy(xT[:, 0, :, :], trans2[0]).then_inc(trans2_hi, 1)

            for n in range(T):
                act.wait_ge(neg_set, n + 1)
                act.activation(elu_neg[:, :], elu_neg[:, :], ACT.Exp).then_inc(exp_set, 1)
                if n >= 1:
                    turned2_hi(n - 1)
                act.wait_ge(norm2_set, n + 1)
                if n >= 1:
                    act.wait_ge(row_stored, 16 * n)
                act.copy(x_row[:, 0, :], xn2[:, :]).then_inc(row_hi, 1)
                if n in (1, 3, 5):
                    split_hi(0, n // 2, 0, stage0)
            def xT_hi(k):
                act.wait_ge(x_turned, k + 1)
                act.copy(xT[:, 0, :, :], xT_acc[0]).then_inc(xT_hi_set, 1)

            def gate_act(k):
                act.wait_ge(gu_done, k + 1)
                act.activation(sig[:, :], g_acc, ACT.Sigmoid, scale=1 / WS).then_inc(sig_set, 1)

            def act_hi_part(k):
                act.wait_ge(act_set, k + 1)
                act.copy(act_hl[:, 0, :], act_row[:, :]).then_inc(act_hi, 1)

            def ffn_tile(k, more=True, scatters=True):
                gate_act(k)
                act_hi_part(k)
                if more:
                    xT_hi(k + 1)
                if scatters:
                    act.wait_ge(y_done, k)
                    act.wait_ge(scattered, (k - T0) * 16)
                    act.activation(y_row[:, :], y_acc, ACT.Copy, scale=1 / WS).then_inc(y_row_set, 1)

            gate_act(0)
            act.wait_ge(gu_done, 1)
            turned2_hi(T - 1)
            act.sem_inc(xT_hi_set, 2)
            act_hi_part(0)
            act.wait_ge(logits_set, T)
            act.activation(score[:, :, :], logit_acc, ACT.Exp, scale=-1 / WS).then_inc(logit_exp, 1)
            for k in range(1, T0):
                if k == T0 - 1:
                    act.wait_ge(dests_set, 1)
                    split_hi(1, 0, 1, stage)
                    split_hi(1, 1, 1, stage)
                ffn_tile(k, scatters=False)
            split_hi(1, 2, 1, stage)

            def expert(q, sl):
                begin = act.value_load(spans[0:1, bass.ds(q - 1, 1)], min_val=0, max_val=TE)
                end = act.value_load(spans[0:1, bass.ds(q, 1)], min_val=MIN_TILES, max_val=TE)
                with act.If(begin > 0):
                    ffn_tile(begin + T0)
                with act.Else():
                    ffn_tile(begin + T0, scatters=False)
                    act.wait_ge(y_done, T0)
                split_hi(q + 1, 0, 1 - sl, stage)
                split_hi(q + 1, 1, 1 - sl, stage)
                ffn_tile(begin + T0 + 1)
                split_hi(q + 1, 2, 1 - sl, stage)
                with act.Fori(begin + 2, end) as j:
                    ffn_tile(j + T0)

            act.wait_ge(dests_set, 1)
            with act.Fori(0, E // 2) as i:
                expert(i * 2 + 1, 1)
                expert(i * 2 + 2, 0)
            tiles = act.value_load(spans[0:1, E:E + 1], min_val=E * MIN_TILES, max_val=TE)
            for t in range(T0, T):
                ffn_tile(tiles + t, more=t < T - 1, scatters=t == T0)

        @block.vector
        def _(dve):
            steps = [0]

            def chain(ins):
                steps[0] += 1
                ins.then_inc(dve_step, 1)
                dve.wait_ge(dve_step, steps[0])

            def norm_stats(n, ready):
                b = n % 2
                dve.bn_stats(stats[:, b, 0, :], xs[:, n, 0:HALF])
                chain(dve.bn_stats(stats[:, b, 1, :], xs[:, n, HALF:D]))
                dve.bn_aggr(mv[:, b, :], stats[:, b, :, :].rearrange("p a s -> p (a s)")).then_inc(ready, 1)

            def edges_needed():
                dve.wait_ge(iota_set, 3)
                dve.tensor_copy(nodes16[:, :], iota_i[:, :])
                dve.tensor_copy(first_f[:, 0, :], first_i[:, :])
                chain(dve.tensor_scalar(pair_i[:, :], pair_i[:, :], 1, None, ALU.arith_shift_right))
                chain(dve.tensor_copy(pair_f[:, :], pair_i[:, :]))
                dve.tensor_scalar(first_f[:, 1, :], first_f[:, 0, :], float(P - 1), None, ALU.add)
                dve.wait_ge(edges_loaded, 16 * (6 if REST else 4))
                dve.tensor_copy(edges_f[:, :, :], edges_i[:, :, :]).then_inc(edges_floated, 1)
                dve.wait_ge(edges_floated, 1)
                chain(dve.tensor_scalar(pads[:, :, :], edges_f[:, 2:4, :], 0.0, 4.0 * NP, ALU.is_lt, ALU.mult))
                chain(dve.tensor_tensor(pads[:, :, :], pads[:, :, :], edges_f[:, 2:4, :], ALU.add))
                dve.tensor_reduce(span[:, 0, :], pads[:, :, :], X, ALU.min)
                chain(dve.tensor_reduce(span[:, 1, :], edges_f[:, 2:4, :], X, ALU.max))
                for g in range(2):
                    dve.tensor_scalar(need[:, 0, g, :], first_f[:, 1, :], span[:, 0, g:g + 1], None, ALU.is_ge)
                    chain(dve.tensor_scalar(need[:, 1, g, :], first_f[:, 0, :], span[:, 1, g:g + 1], None, ALU.is_le))
                chain(dve.tensor_tensor(need[:, 0, :, :], need[:, 0, :, :], need[:, 1, :, :], ALU.mult))
                for g in range(2):
                    dve.tensor_scalar(cand[:, 0, g, :], need[:, 0, g, :], pair_f[:, g:g + 1], None, ALU.mult)
                    chain(dve.tensor_scalar(cand[:, 1, g, :], need[:, 0, g, :], float(P), None, ALU.mult))
                chain(dve.tensor_tensor(cand[:, 1, :, :], cand[:, 1, :, :], cand[:, 0, :, :], ALU.subtract))
                dve.tensor_tensor(cand[:, 0, :, :], cand[:, 0, :, :], need[:, 0, :, :], ALU.add).then_inc(cand_set, 1)

            def edges_range():
                dve.wait_ge(edgeT_set, 1)
                dve.wait_ge(cand_turned, 1)
                chain(dve.tensor_reduce(cmax[0:4 * T, :], prep[0:4 * T, 0:P], X, ALU.max))
                dve.tensor_scalar(diag[0:4 * T, 0:4 * T], ident[0:4 * T, 0:4 * T], cmax[0:4 * T, :], None, ALU.mult).then_inc(cmax_set, 1)
                dve.wait_ge(cmax_turned, 1)
                row = prep[0:1, 0:4 * T].rearrange("p (w g t) -> p w g t", w=2, g=2)
                chain(dve.tensor_copy(crow[:, :, :], row[:, :, 0, :]))
                dve.tensor_tensor(crow[:, :, :], crow[:, :, :], row[:, :, 1, :], ALU.max).then_inc(crow_set, 1)
                dve.wait_ge(crow_set, 1)

            def edges_steps():
                chain(dve.tensor_scalar(crow[:, 0, :], crow[:, 0, :], 1.0, None, ALU.max))
                chain(dve.tensor_scalar(crow[:, 1, :], crow[:, 1, :], -1.0, float(P), ALU.mult, ALU.add))
                chain(dve.tensor_scalar(lens[:, :], crow[:, 0, :], -1.0, None, ALU.add))
                chain(dve.tensor_tensor(crow[:, 1, :], crow[:, 1, :], lens[:, :], ALU.min))
                chain(dve.tensor_tensor(lens[:, :], crow[:, 0, :], crow[:, 1, :], ALU.subtract))
                chain(dve.tensor_tensor(step_over[:, :, :], lens[:, :].unsqueeze(2).to_broadcast([1, T, STEPS]),
                                        nodes16[0:1, 0:LAST].rearrange("p (s n) -> p s n", n=PAIRS_STEP)[:, :, 0].unsqueeze(1)
                                        .to_broadcast([1, T, STEPS]), ALU.is_gt))
                chain(dve.tensor_reduce(lens[:, :], step_over[:, :, :], X, ALU.add))
                chain(dve.tensor_scalar(crow[:, 0, :], lens[:, :], -float(PAIRS_STEP), float(LAST), ALU.mult, ALU.add))
                chain(dve.tensor_tensor(crow[:, 1, :], crow[:, 1, :], crow[:, 0, :], ALU.min))
                chain(dve.memset(bounds_f[:, 0, 0:1], 0.0))
                for j in range(T):
                    chain(dve.tensor_tensor(bounds_f[:, 1, j:j + 1], bounds_f[:, 0, j:j + 1], lens[:, j:j + 1], ALU.add))
                    if j + 1 < T:
                        chain(dve.tensor_copy(bounds_f[:, 0, j + 1:j + 2], bounds_f[:, 1, j:j + 1]))
                chain(dve.scalar_tensor_tensor(out=bounds_f[:, 2, :], in0=bounds_f[:, 0, :], scalar=-float(PAIRS_STEP), in1=crow[:, 1, :],
                                               op0=ALU.mult, op1=ALU.add))
                chain(dve.tensor_scalar(bounds_f[:, 2, :], bounds_f[:, 2, :], float(LEAD), None, ALU.add))
                dve.tensor_copy(bounds[:, :, :], bounds_f[:, :, :]).then_inc(bounds_set, 1)

            def gate_low():
                dve.wait_ge(gate_hi, 1)
                dve.scalar_tensor_tensor(out=gateT[1][:, :, :].rearrange("p k e -> p (k e)"), in0=prep[:, 0:K * E], scalar=WS,
                                         in1=gateT[0][:, :, :].rearrange("p k e -> p (k e)"), op0=ALU.mult,
                                         op1=ALU.subtract).then_inc(gate_lo, 1)

            def normalise(n):
                dve.wait_ge(rstd_set, n + 1)
                if n >= 2:
                    dve.wait_ge(trans_set, n - 1)
                b = n % 2
                dve.tensor_scalar(xn1[:, b, :], xs[:, n, :], mv[:, b, 0:1], rs[:, b, 3:4], ALU.subtract,
                                  ALU.mult).then_inc(norm_set, 1)

            def turned_lo(n):
                dve.wait_ge(hi_set, n + 1)
                dve.tensor_tensor(x1T[1][:, :, n * P:(n + 1) * P], trans[n % 2], x1T[0][:, :, n * P:(n + 1) * P],
                                  ALU.subtract).then_inc(lo_set, 1)

            def w_part(q):
                dve.wait_ge(w_hi, q + 1)
                dve.scalar_tensor_tensor(out=ws[1][:, 2 * q:2 * q + 2, :], in0=w_stage[:, q % 2, :, :], scalar=WS,
                                         in1=ws[0][:, 2 * q:2 * q + 2, :], op0=ALU.mult, op1=ALU.subtract).then_inc(w_lo, 1)

            def stats1(n):
                dve.wait_ge(x_loaded[n], 16)
                if n >= 2:
                    dve.wait_ge(norm_set, n - 1)
                norm_stats(n, stats_set)

            def h_out(n):
                dve.wait_ge(h_rowed, n + 1)
                dve.tensor_tensor(hs[1][:, n, :], h_row[:, :], hs[0][:, n, :], ALU.subtract).then_inc(h_lo, 1)
                if n >= 1:
                    dve.wait_ge(al_dotted, n)
                dve.tensor_tensor_reduce(elu_neg[:, :], h_row[:, :], a_rows[:, 0, :], 1.0, 0.0, ALU.mult, ALU.add,
                                         alr[:, 0, n:n + 1]).then_inc(half_dotted, 1)
                dve.wait_ge(half_dotted, n + 1)
                dve.tensor_tensor_reduce(elu_neg[:, :], h_row[:, :], a_rows[:, 1, :], 1.0, 0.0, ALU.mult, ALU.add,
                                         alr[:, 1, n:n + 1]).then_inc(al_dotted, 1)

            stats1(0)
            stats1(1)
            normalise(0)
            normalise(1)
            w_part(0)
            turned_lo(0)
            w_part(1)
            edges_needed()
            turned_lo(1)
            w_part(2)
            edges_range()
            w_part(3)
            stats1(2)
            normalise(2)
            gate_low()
            edges_steps()
            dve.wait_ge(bounds_set, 1)
            dve_ends, backs = [], []
            for n in range(T):
                if n + 3 < T:
                    stats1(n + 3)
                    normalise(n + 3)
                h_out(n)
                dve_ends.append(dve.value_load(bounds[0:1, 1, n:n + 1], min_val=1, max_val=STEPS * T))
                backs.append(dve.value_load(bounds[0:1, 2, n:n + 1], min_val=0, max_val=LEAD + LAST))
                if n + 2 < T:
                    turned_lo(n + 2)

            def one_hots(j):
                begin, end, back = 0 if j == 0 else dve_ends[j - 1], dve_ends[j], backs[j]
                with dve.Fori(begin, end) as q:
                    pair = nc.s_assert_within(
                        dve.snap(q * PAIRS_STEP + back - LEAD), 0, LAST - PAIRS_STEP,
                        skip_runtime_bounds_check_because="a tile's pairs are pairs of chunks")
                    for b in range(STEP):
                        dve.wait_ge(hot_free, q * STEP + (b + 1))
                        dve.tensor_scalar(hot_src[:, b, :], nodes16[:, :],
                                          edge_src[:, bass.ds(pair * 2 + b, 1)], None, ALU.is_equal)
                        dve.tensor_scalar(hot_dst[:, b, :], nodes16[:, j * P:(j + 1) * P],
                                          edge_dst[:, bass.ds(pair * 2 + b, 1)], None, ALU.is_equal).then_inc(hot_ready, 1)

            def attention(j):
                b = j % 2
                dve.wait_ge(weight_set, j + 1)
                dve.wait_ge(count_set, j + 1)
                if j >= 2:
                    dve.wait_ge(att_lo, j - 1)
                dve.scalar_tensor_tensor(out=att_row[:, b, :], in0=count_acc[b], scalar=AS, in1=edge_w[:, b, :], op0=ALU.mult,
                                         op1=ALU.mult).then_inc(att_set, 1)

            dve.wait_ge(bounds_set, 1)
            for j in range(T):
                one_hots(j)
                if j == 0:
                    dve.wait_ge(al_dotted, T)
                    dve.tensor_tensor(diags[:, :, :], ident[:, :].unsqueeze(1).to_broadcast([P, T, P]),
                                      alr[:, 0, :].unsqueeze(2).to_broadcast([P, T, P]), ALU.mult).then_inc(diag_set, 1)
                    chain(dve.scalar_tensor_tensor(out=sum_eps[:, :], in0=alr[:, 0, :], scalar=SLOPE, in1=alr[:, 0, :],
                                                   op0=ALU.mult, op1=ALU.max))
                    chain(dve.tensor_scalar(sum_eps[:, :], sum_eps[:, :], 80.0, None, ALU.min))
                    dve.tensor_scalar(nar[:, :], alr[:, 1, :], -SLOPE, None, ALU.mult).then_inc(nar_set, 1)
                else:
                    attention(j - 1)
            attention(T - 1)

            lns = [0]

            def link(ins):
                lns[0] += 1
                ins.then_inc(ln_chain, 1)
                dve.wait_ge(ln_chain, lns[0])

            def turned2_lo(n):
                dve.wait_ge(trans2_hi, n + 1)
                dve.tensor_copy(xT[:, 1, :, :], trans2[1]).then_inc(trans2_lo, 1)

            def node_out(n):
                b = n % 2
                dve.wait_ge(sum_set, n + 1)
                dve.tensor_scalar(rsum[:, b, 0:1], sum_acc, sum_eps[:, n:n + 1], None, ALU.add).then_inc(sum_read, 1)
                dve.wait_ge(sum_read, n + 1)
                link(dve.reciprocal(rsum[:, b, 1:2], rsum[:, b, 0:1]))
                dve.wait_ge(agg_set, n + 1)
                dve.tensor_scalar(elu_neg[:, :], agg_acc[b], rsum[:, b, 1:2], 0.0, ALU.mult, ALU.min).then_inc(neg_set, 1)
                last = dve.tensor_scalar(elu_pos[:, :], agg_acc[b], rsum[:, b, 1:2], 0.0, ALU.mult, ALU.max)
                last.then_inc(agg_free, 1)
                dve.wait_ge(agg_free, n + 1)
                link(dve.tensor_tensor(elu_pos[:, :], elu_pos[:, :], xs[:, n, :], ALU.add))
                dve.wait_ge(exp_set, n + 1)
                if n == T - 1:
                    turned2_lo(n - 1)
                link(dve.scalar_tensor_tensor(out=xs[:, n, :], in0=elu_neg[:, :], scalar=-1.0, in1=elu_pos[:, :], op0=ALU.add,
                                              op1=ALU.add))
                norm_stats(n, stats2_set)
                if 1 <= n < T - 1:
                    turned2_lo(n - 1)
                if n in (2, 4, 6):
                    split_lo(0, (n - 1) // 2, 0, stage0)
                dve.wait_ge(rstd2_set, n + 1)
                if n >= 1:
                    dve.wait_ge(row_lo, n)
                dve.tensor_scalar(xn2[:, :], xs[:, n, :], mv[:, b, 0:1], rs[:, b, 3:4], ALU.subtract,
                                  ALU.mult).then_inc(norm2_set, 1)
                dve.wait_ge(row_hi, n + 1)
                dve.tensor_tensor(x_row[:, 1, :], xn2[:, :], x_row[:, 0, :], ALU.subtract).then_inc(row_lo, 1)

            def split_lo(q, m, sl, staged):
                dve.wait_ge(d_hi if m == 2 else gu_hi, q + 1 if m == 2 else q * 2 + (m + 1))
                dve.scalar_tensor_tensor(out=weights[sl][m][1][:, :, :], in0=staged[m][:, :, :], scalar=WS,
                                         in1=weights[sl][m][0][:, :, :], op0=ALU.mult, op1=ALU.subtract)\
                    .then_inc(d_lo if m == 2 else gu_lo, 1)

            def gate_times_up(k):
                dve.wait_ge(sig_set, k + 1)
                dve.scalar_tensor_tensor(out=gated[:, :], in0=g_acc, scalar=1 / WS, in1=sig[:, :], op0=ALU.mult,
                                         op1=ALU.mult).then_inc(gated_set, 1)
                dve.wait_ge(gated_set, k + 1)
                dve.scalar_tensor_tensor(out=act_row[:, :], in0=u_acc, scalar=1 / WS, in1=gated[:, :], op0=ALU.mult,
                                         op1=ALU.mult).then_inc(act_set, 1)

            def act_lo_part(k):
                dve.wait_ge(act_hi, k + 1)
                dve.tensor_tensor(act_hl[:, 1, :], act_row[:, :], act_hl[:, 0, :], ALU.subtract).then_inc(act_lo, 1)

            def turned_act(k):
                dve.wait_ge(act_turned, k + 1)
                dve.tensor_copy(actT[:, :, :, :], actT_acc).then_inc(actT_set, 1)

            dve.wait_ge(eps_exp, 1)
            link(dve.tensor_scalar(sum_eps[:, :], sum_eps[:, :], AS * SUM_EPS, None, ALU.mult))
            for n in range(T):
                node_out(n)
            gate_times_up(0)
            turned2_lo(T - 1)
            dve.sem_inc(xT_lo_set, 2)
            act_lo_part(0)
            turned_act(0)

            def bc(ap, shape):
                return ap.to_broadcast(shape)

            def ranks(v, n, out_rank, ra, rb):
                mine = bc(v.unsqueeze(3), [P, T, n, n])
                other = bc(v.unsqueeze(2), [P, T, n, n])
                chain(dve.tensor_tensor(ra, other, mine, ALU.is_equal))
                chain(dve.tensor_tensor(ra, ra, bc(lower[:, 0:n, 0:n].unsqueeze(1), [P, T, n, n]), ALU.mult))
                chain(dve.tensor_tensor(rb, other, mine, ALU.is_gt))
                chain(dve.tensor_tensor(ra, ra, rb, ALU.add))
                chain(dve.tensor_reduce(out_rank, ra, X, ALU.add))

            dve.wait_ge(agg_done, 1)
            chain(dve.memset(lower[:, :, :], 0.0))
            for e in range(1, E):
                last = dve.memset(lower[:, e, 0:e], 1.0)
            chain(last)
            dve.wait_ge(consts_set, 9)
            chain(dve.tensor_copy(token[:, :], token_i[:, :]))
            chain(dve.tensor_scalar(valid[:, :], token[:, :], N - 0.5, None, ALU.is_lt))
            dve.wait_ge(scattered, 16)
            dve.wait_ge(logit_exp, 1)
            chain(dve.tensor_scalar(score[:, :, :], score[:, :, :], 1.0, None, ALU.add))
            chain(dve.reciprocal(score[:, :, :], score[:, :, :]))
            chain(dve.tensor_tensor(choice[:, :, :], score[:, :, :], bc(bias_row[:, :].unsqueeze(1), [P, T, E]), ALU.add))
            pairs = choice[:, :, :].rearrange("p t (g m) -> p t g m", m=EG)
            chain(dve.tensor_tensor(rg[:, :, :], pairs[:, :, :, 0], pairs[:, :, :, 1], ALU.add))
            nn = GROUPS * GROUPS
            ga = rank_a[:, :, :, :].rearrange("p t a b -> p (t a b)")[:, 0:T * nn].rearrange("p (t a b) -> p t a b", a=GROUPS, b=GROUPS)
            gb = rank_b[:, :, :, :].rearrange("p t a b -> p (t a b)")[:, 0:T * nn].rearrange("p (t a b) -> p t a b", a=GROUPS, b=GROUPS)
            ranks(rg[:, :, :], GROUPS, rg2[:, :, :], ga, gb)
            chain(dve.tensor_scalar(rg[:, :, :], rg2[:, :, :], TOP_GROUPS - 0.5, None, ALU.is_lt))
            chain(dve.tensor_tensor(pairs, pairs, bc(rg[:, :, :].unsqueeze(3), [P, T, GROUPS, EG]), ALU.mult))
            ranks(choice[:, :, :], E, r1[:, :, :], rank_a[:, :, :, :], rank_b[:, :, :, :])
            chain(dve.tensor_scalar(r2[:, :, :], r1[:, :, :], TOPK - 0.5, None, ALU.is_lt))
            chain(dve.tensor_tensor(sel[:, :, :], r2[:, :, :], bc(valid[:, :].unsqueeze(2), [P, T, E]), ALU.mult))
            dve.tensor_copy(sel16[:, :, :], sel[:, :, :]).then_inc(sel_set, 1)
            chain(dve.tensor_tensor(cw[:, :, :], r2[:, :, :], score[:, :, :], ALU.mult))
            chain(dve.tensor_reduce(rt[:, :], cw[:, :, :], X, ALU.add))
            chain(dve.tensor_scalar(rt[:, :], rt[:, :], 1e-20, None, ALU.add))
            chain(dve.reciprocal(rt2[:, :], rt[:, :]))
            chain(dve.tensor_scalar(rt2[:, :], rt2[:, :], ROUTED_SCALE, None, ALU.mult))
            chain(dve.tensor_tensor(cw[:, :, :], cw[:, :, :], bc(rt2[:, :].unsqueeze(2), [P, T, E]), ALU.mult))
            chain(dve.tensor_tensor(rank_a[:, :, :, :], bc(r2[:, :, :].unsqueeze(2), [P, T, E, E]),
                                    bc(lower[:, :, :].unsqueeze(1), [P, T, E, E]), ALU.mult))
            chain(dve.tensor_reduce(ranked[:, :, :], rank_a[:, :, :, :], X, ALU.add))

            def rank_weights():
                for i in range(TOPK):
                    chain(dve.scalar_tensor_tensor(out=choice[:, :, :], in0=ranked[:, :, :], scalar=float(i), in1=cw[:, :, :],
                                                   op0=ALU.is_equal, op1=ALU.mult))
                    chain(dve.tensor_reduce(rank_w[:, :, i], choice[:, :, :], X, ALU.add))

            def positions():
                chain(dve.tensor_scalar(r1[:, :, :], ranked[:, :, :], 1.0, None, ALU.add))
                dve.wait_ge(prefix_set, 1)
                prefix = route_acc[:, 0:PAIRS].rearrange("p (t e) -> p t e", e=E)
                total = route_acc[:, PAIRS:2 * PAIRS].rearrange("p (t e) -> p t e", e=E)
                chain(dve.memset(offs[:, 0, :], 0.0))
                for t in range(T):
                    chain(dve.tensor_tensor(offs[:, t + 1, :], offs[:, t, :], total[:, t, :], ALU.add))
                chain(dve.tensor_tensor(choice[:, :, :], prefix, offs[:, 0:T, :], ALU.add))
                chain(dve.tensor_copy(pos_i[:, :, :], choice[:, :, :]))
                dve.tensor_scalar(tile_i[:, :, :], pos_i[:, :, :], 7, None, ALU.arith_shift_right)
                chain(dve.tensor_scalar(slot_i[:, :, :], pos_i[:, :, :], P - 1, None, ALU.bitwise_and))
                dve.tensor_copy(kglob[:, :, :], tile_i[:, :, :])
                chain(dve.tensor_copy(slot[:, :, :], slot_i[:, :, :]))
                chain(dve.tensor_scalar(tiles_f[:, :], offs[:, T, :], float(P - 1), None, ALU.add))
                chain(dve.tensor_copy(tiles_i[:, :], tiles_f[:, :]))
                chain(dve.tensor_scalar(tiles_i[:, :], tiles_i[:, :], 7, None, ALU.arith_shift_right))
                chain(dve.tensor_copy(tiles_f[:, :], tiles_i[:, :]))
                chain(dve.tensor_scalar(tiles_f[:, :], tiles_f[:, :], float(MIN_TILES), None, ALU.max))
                chain(dve.memset(begin_f[:, 0:1], 0.0))
                for e in range(E):
                    chain(dve.tensor_tensor(begin_f[:, e + 1:e + 2], begin_f[:, e:e + 1], tiles_f[:, e:e + 1], ALU.add))
                chain(dve.tensor_copy(spans[:, :], begin_f[0:1, :]))
                chain(dve.tensor_tensor(kglob[:, :, :], kglob[:, :, :], bc(begin_f[:, 0:E].unsqueeze(1), [P, T, E]), ALU.add))
                chain(dve.scalar_tensor_tensor(out=slot[:, :, :], in0=slot[:, :, :], scalar=1.0, in1=sel[:, :, :], op0=ALU.add,
                                               op1=ALU.mult))
                chain(dve.tensor_scalar(slot[:, :, :], slot[:, :, :], -1.0, None, ALU.add))

            slot_c = slot[:, :, :].rearrange("p t e -> p (t e)")
            kglob_c = kglob[:, :, :].rearrange("p t e -> p (t e)")

            def tile_hots():
                dve.tensor_tensor(hot_tile[:, :, 1, :], bc(nodes16[:, 0:KT].unsqueeze(1), [P, PAIRS, KT]),
                                  bc(kglob_c[:, :].unsqueeze(2), [P, PAIRS, KT]), ALU.is_equal).then_inc(tile_hot_set, 1)

            def slot_hots():
                dve.tensor_tensor(hot_slot[:, :, :], bc(nodes16[:, 0:P].unsqueeze(1), [P, PAIRS, P]),
                                  bc(slot_c[:, :].unsqueeze(2), [P, PAIRS, P]), ALU.is_equal).then_inc(slot_hot_set, 1)

            def destinations():
                dve.wait_ge(pairs_summed, 1)
                tok, rk = route_acc[:, 0:KT], route_acc[:, KT:2 * KT]
                dve.tensor_copy(gather_at[:, :], tok)
                chain(dve.tensor_scalar(dest_a[:, :], rk, 0.5, 65536.0, ALU.is_lt, ALU.mult))
                chain(dve.scalar_tensor_tensor(out=dest_a[:, :], in0=rk, scalar=float(NP), in1=dest_a[:, :], op0=ALU.mult,
                                               op1=ALU.add))
                chain(dve.scalar_tensor_tensor(out=dest_b[:, :], in0=dest_a[:, :], scalar=float(-NP), in1=tok, op0=ALU.add,
                                               op1=ALU.add))
                dve.tensor_copy(scatter_at[:, :], dest_b[:, :]).then_inc(dests_set, 1)

            def xT_lo(k):
                dve.wait_ge(x_turned, k + 1)
                dve.tensor_copy(xT[:, 1, :, :], xT_acc[1]).then_inc(xT_lo_set, 1)

            def ffn_tile(k, more=True, adds=None):
                gate_times_up(k)
                if more:
                    xT_lo(k + 1)
                act_lo_part(k)
                if adds is not None:
                    dve.wait_ge(y_done, k)
                    dve.scalar_tensor_tensor(out=xs[:, adds, :], in0=y_acc, scalar=1 / WS, in1=xs[:, adds, :], op0=ALU.mult,
                                             op1=ALU.add).then_inc(y_read, 1)
                turned_act(k)

            ffn_tile(1, adds=ORDER[0])
            positions()
            tile_hots()
            ffn_tile(2, adds=ORDER[1])
            slot_hots()
            ffn_tile(3, adds=ORDER[2])
            destinations()
            dve.wait_ge(dests_set, 1)
            split_lo(1, 0, 1, stage)
            split_lo(1, 1, 1, stage)
            ffn_tile(4, more=False, adds=ORDER[3])
            xT_lo(5)
            split_lo(1, 2, 1, stage)
            rank_weights()

            def add_first(i):
                rows = P if i < T - 1 else TAIL
                dve.wait_ge(first_loaded, 16 * (i + 1))
                dve.scalar_tensor_tensor(out=xs[0:rows, i, :], in0=y_first[0:rows, :], scalar=rank_w[0:rows, i, 0:1],
                                         in1=xs[0:rows, i, :], op0=ALU.mult, op1=ALU.add).then_inc(first_added, 1)

            def expert(q, sl, adds=(None,) * 4):
                begin = dve.value_load(spans[0:1, bass.ds(q - 1, 1)], min_val=0, max_val=TE)
                end = dve.value_load(spans[0:1, bass.ds(q, 1)], min_val=MIN_TILES, max_val=TE)
                with dve.If(begin > 0):
                    ffn_tile(begin + T0)
                with dve.Else():
                    ffn_tile(begin + T0, adds=ORDER[T0 - 1])
                for m in range(2):
                    if adds[m] is not None:
                        add_first(adds[m])
                    split_lo(q + 1, m, 1 - sl, stage)
                ffn_tile(begin + T0 + 1)
                if adds[2] is not None:
                    add_first(adds[2])
                split_lo(q + 1, 2, 1 - sl, stage)
                if adds[3] is not None:
                    add_first(adds[3])
                with dve.Fori(begin + 2, end) as j:
                    ffn_tile(j + T0)

            with dve.Fori(0, E // 2 - 2) as i:
                expert(i * 2 + 1, 1)
                expert(i * 2 + 2, 0)
            expert(E - 3, 1)
            dve.wait_ge(y_read, T0)
            expert(E - 2, 0)
            expert(E - 1, 1, (0, 1, None, None))
            expert(E, 0, (2, 3, 4, 5))
            tiles = dve.value_load(spans[0:1, E:E + 1], min_val=E * MIN_TILES, max_val=TE)

            def add_results(n):
                t = ORDER[n]
                rows = P if t < T - 1 else TAIL
                dve.wait_ge(y_in_loaded[n % YB], 16 * (n // YB + 1))
                dve.wait_ge(y_read, n + 1)
                for i in range(1, TOPK):
                    last = dve.scalar_tensor_tensor(out=xs[0:rows, t, :], in0=y_in[n % YB][0:rows, i - 1, :],
                                                    scalar=rank_w[0:rows, t, i:i + 1], in1=xs[0:rows, t, :], op0=ALU.mult,
                                                    op1=ALU.add)
                    if i < TOPK - 1:
                        last.then_inc(sum_chain, 1)
                        dve.wait_ge(sum_chain, (TOPK - 2) * n + i)
                last.then_inc(y_summed, 1)

            ffn_tile(tiles + T0)
            for i in range(6, 8):
                add_first(i)
            ffn_tile(tiles + T0 + 1, adds=ORDER[T0])
            for i in range(8, T):
                add_first(i)
            dve.wait_ge(first_added, T)
            added = 0
            for t in range(T0 + 2, T):
                for _ in range(1 if t == T0 + 2 else 3):
                    add_results(added)
                    added += 1
                ffn_tile(tiles + t, more=t < T - 1, adds=ORDER[t - 1])
            for n in range(added, T - 1):
                add_results(n)
            dve.wait_ge(y_done, tiles + T)
            dve.scalar_tensor_tensor(out=xs[:, ORDER[T - 1], :], in0=y_acc, scalar=1 / WS, in1=xs[:, ORDER[T - 1], :],
                                     op0=ALU.mult, op1=ALU.add).then_inc(y_read, 1)
            add_results(T - 1)

        @block.tensor
        def _(pe):
            pe.wait_ge(consts_set, 9)

            def turn_edges():
                pe.wait_ge(edges_floated, 1)
                for i in range(4):
                    last = pe.transpose(prep[:, i * P:(i + 1) * P], edges_f[:, i, :], ident[:, :])
                last.then_inc(edges_turned, 1)
                pe.wait_ge(edgeT_set, 1)
                pe.wait_ge(cand_set, 1)
                pe.transpose(prep[0:4 * T, 0:P], cand[:, :, :, :].rearrange("p a g t -> p (a g t)"), ident[:, :]).then_inc(cand_turned, 1)
                pe.wait_ge(cmax_set, 1)
                pe.matmul(prep[0:1, 0:4 * T], ones[0:4 * T, 0:1], diag[0:4 * T, 0:4 * T], start=True, stop=True).then_inc(cmax_turned, 1)

            def turn_gate():
                pe.wait_ge(crow_set, 1)
                pe.wait_ge(small_loaded, 32)
                for k in range(K):
                    last = pe.transpose(prep[:, k * E:(k + 1) * E], gate_rows[:, k * P:(k + 1) * P], ident[0:E, 0:E])
                last.then_inc(gate_turned, 1)

            def turn(n):
                pe.wait_ge(norm_set, n + 1)
                if n >= 2:
                    pe.wait_ge(lo_set, n - 1)
                for k in range(K):
                    last = pe.transpose(trans[n % 2][:, k, :], xn1[:, n % 2, k * P:(k + 1) * P], ident[:, :])
                last.then_inc(trans_set, 1)

            def three_pass(out_ap, lhs, rhs, k, nk, cols, closes=True):
                for li, ri in ((0, 0), (0, 1), (1, 0)):
                    for c0, c1 in cols:
                        last = pe.matmul(out_ap[:, c0:c1], lhs(li), rhs(ri)[:, c0:c1], start=(k == 0 and li == ri),
                                         stop=(closes and k == nk - 1 and li == 1))
                return last

            HALVES = [(0, HALF), (HALF, D)]

            def h_product(n):
                pe.wait_ge(lo_set, n + 1)
                if n >= 2:
                    pe.wait_ge(h_rowed, n - 1)
                elif n == 1:
                    pe.wait_ge(gate_lo, 1)
                for k in range(K):
                    if n == 0 and k == K // 2:
                        turn_edges()
                    if n == 0 and k == K - 2:
                        turn_gate()
                    if n == 0 and k % 2 == 0:
                        pe.wait_ge(w_lo, k // 2 + 1)
                    last = three_pass(h_acc[n % 2], lambda i: x1T[i][:, k, n * P:(n + 1) * P], lambda i: ws[i][:, k, :], k, K, HALVES)
                last.then_inc(h_set, 1)

            ends = []

            def load_ends(count):
                for j in range(len(ends), len(ends) + count):
                    ends.append(pe.value_load(bounds[0:1, 1, j:j + 1], min_val=1, max_val=STEPS * T))

            turn(0)
            turn(1)
            for n in range(T):
                h_product(n)
                if n == 1:
                    pe.wait_ge(bounds_set, 1)
                    load_ends(T // 2)
                if n + 2 < T:
                    turn(n + 2)

            def counts(j):
                acc = count_acc[j % 2]
                if j == 0:
                    pe.wait_ge(lo_set, T)
                    pe.wait_ge(bounds_set, 1)
                elif j == 1:
                    pe.wait_ge(al_copied, 2)
                else:
                    pe.wait_ge(att_set, j - 1)
                for c0, w in CH:
                    pe.matmul(acc[:, c0:c0 + 1], zero16[:, :], zero16[:, 0:1], start=True, stop=False, skip_group_check=True)
                begin, end = 0 if j == 0 else ends[j - 1], ends[j]
                with pe.Fori(begin, end) as q:
                    for b in range(STEP):
                        pe.wait_ge(hot_ready, q * STEP + (b + 1))
                        for c0, w in CH:
                            last = pe.matmul(acc[:, c0:c0 + w], hot_dst[:, b, :],
                                             hot_src[:, b, c0:c0 + w], start=False,
                                             stop=False, skip_group_check=True)
                        last.then_inc(hot_free, 1)
                for c0, w in CH:
                    last = pe.matmul(acc[:, c0:c0 + 1], zero16[:, :], zero16[:, 0:1], start=False, stop=True, skip_group_check=True)
                last.then_inc(count_set, 1)

            pe.sem_inc(hot_free, STEP)
            for j in range(T):
                counts(j)
                if j == 0:
                    load_ends(T - T // 2)
                    pe.wait_ge(diag_set, 1)
                    pe.wait_ge(h_rowed, T)
                    for c0, w in CH:
                        last = pe.matmul(al_acc[:, c0:c0 + w], ones[:, :],
                                         diags[:, :, :].rearrange("p t n -> p (t n)")[:, c0:c0 + w], start=True, stop=True)
                    last.then_inc(al_rowed, 1)

            def row_sums(n):
                for j in range(T):
                    for i in range(2):
                        last = pe.matmul(sum_acc, att[i][:, j, n * P:(n + 1) * P], ones16, start=(j == 0 and i == 0),
                                         stop=(j == T - 1 and i == 1))
                last.then_inc(sum_set, 1)

            def aggregate(n):
                b = n % 2
                if n == 0:
                    pe.wait_ge(att_set, T - 1)
                if n >= 2:
                    pe.wait_ge(agg_free, n - 1)
                for j in range(T):
                    if n == 0:
                        pe.wait_ge(att_lo, j + 1)
                    if j == T // 2 and n >= 2:
                        turn2(n - 2)
                    if j == T // 2 and n >= 1:
                        pe.wait_ge(sum_read, n)
                        row_sums(n)
                    last = three_pass(agg_acc[b], lambda i: att[i][:, j, n * P:(n + 1) * P], lambda i: hs[i][:, j, :], j, T, HALVES)
                last.then_inc(agg_set, 1)
                if n == 0:
                    row_sums(n)

            def turn_rows(dst):
                for i in range(2):
                    for k in range(K):
                        last = pe.transpose(dst[i][:, k, :], x_row[:, i, k * P:(k + 1) * P], ident16[:, :])
                return last

            def turn2(n):
                pe.wait_ge(row_lo, n + 1)
                if n >= 1:
                    pe.wait_ge(trans2_lo, n)
                turn_rows(trans2).then_inc(trans2_set, 1)

            def logits(n):
                pe.wait_ge(trans2_lo, n + 1)
                for k in range(K):
                    for li, ri in ((0, 0), (0, 1), (1, 0)):
                        last = pe.matmul(logit_acc[:, n, :], xT[:, li, k, :], gateT[ri][:, k, :],
                                         start=(k == 0 and li == ri), stop=(k == K - 1 and li == 1))
                last.then_inc(logits_set, 1)

            for n in range(T):
                aggregate(n)
                if n == T - 1:
                    last = pe.matmul(bank[0:1, 5, 511:512], zero16[:, 0:1], zero16[:, 0:1], start=True, stop=True)
                    last.then_inc(agg_done, 1)
                if n >= 2:
                    logits(n - 2)
            turn2(T - 2)
            logits(T - 2)

            def gate_up(k, sl):
                if isinstance(k, int) and k < 2:
                    pe.wait_ge(trans2_lo, T - 1 + k)
                else:
                    pe.wait_ge(xT_hi_set, k + 1)
                    pe.wait_ge(xT_lo_set, k + 1)
                for b in range(K):
                    for li, ri in ((0, 0), (0, 1), (1, 0)):
                        for m, acc in enumerate((g_acc, u_acc)):
                            last = pe.matmul(acc, xT[:, li, b, :], weights[sl][m][ri][:, b, :], start=(b == 0 and li == ri),
                                             stop=(b == K - 1 and li == 1))
                last.then_inc(gu_done, 1)

            def turn_x(k):
                if isinstance(k, int) and k < T0:
                    pe.wait_ge(rows_loaded, (k - 1) * 16)
                else:
                    pe.wait_ge(gathered, (k - (T0 - 1)) * 16)
                turn_rows(xT_acc).then_inc(x_turned, 1)

            def down(k, sl, emptied, count):
                pe.wait_ge(actT_set, k + 1)
                if emptied is not None:
                    pe.wait_ge(emptied, count)
                for b in range(KI):
                    last = three_pass(y_acc, lambda i: actT[:, i, b, :], lambda i: weights[sl][2][i][:, b, :], b, KI, HALVES)
                last.then_inc(y_done, 1)

            def turn_act(k):
                pe.wait_ge(act_lo, k + 1)
                for i in range(2):
                    for b in range(KI):
                        last = pe.transpose(actT_acc[:, i, b, :], act_hl[:, i, b * P:(b + 1) * P], ident16[:, :])
                last.then_inc(act_turned, 1)

            pe.wait_ge(gu_lo, 2)
            pe.wait_ge(agg_free, T - 1)
            gate_up(0, 0)
            turn2(T - 1)
            pe.sem_inc(x_turned, 2)
            logits(T - 1)
            pe.wait_ge(trans2_hi, T)
            turn_act(0)
            pe.wait_ge(d_lo, 1)
            pe.wait_ge(agg_free, T)
            for k in range(1, T0):
                gate_up(k, 0)
                if k == 1:
                    pe.wait_ge(logit_exp, 1)
                if k < T0 - 1:
                    turn_x(k + 1)
                down(k - 1, 0, y_read if k >= 2 else None, k - 1)
                turn_act(k)
                if k == T0 - 1:
                    turn_x(k + 1)
                if k == 1:
                    pe.wait_ge(sel_set, 1)
                    flat = sel16[:, :, :].rearrange("p t e -> p (t e)")
                    pe.matmul(route_acc[:, 0:PAIRS], before16[:, :], flat, start=True, stop=True)
                    last = pe.matmul(route_acc[:, PAIRS:2 * PAIRS], ones16w[:, :], flat, start=True, stop=True)
                    last.then_inc(prefix_set, 1)
                if k == 3:
                    pe.wait_ge(tile_hot_scaled, 1)
                    pe.wait_ge(slot_hot_set, 1)
                    for i in range(PAIRS):
                        last = pe.matmul(route_acc[:, 0:2 * KT], hot_slot[:, i, :], hot_tile[:, i, :, :].rearrange("p a n -> p (a n)"),
                                         start=(i == 0), stop=(i == PAIRS - 1))
                    last.then_inc(pairs_summed, 1)

            def expert(q, sl):
                begin = pe.value_load(spans[0:1, bass.ds(q - 1, 1)], min_val=0, max_val=TE)
                end = pe.value_load(spans[0:1, bass.ds(q, 1)], min_val=MIN_TILES, max_val=TE)
                pe.wait_ge(gu_lo, q * 2 + 2)
                gate_up(begin + T0, sl)
                turn_x(begin + T0 + 1)
                with pe.If(begin > 0):
                    pe.wait_ge(y_row_set, begin + 1)
                with pe.Else():
                    pe.wait_ge(y_read, T0 - 1)
                down(begin + T0 - 1, 1 - sl, None, 0)
                turn_act(begin + T0)
                pe.wait_ge(d_lo, q + 1)
                for j in (begin + 1,):
                    gate_up(j + T0, sl)
                    turn_x(j + T0 + 1)
                    with pe.If(begin > 0):
                        pe.wait_ge(y_row_set, begin + 2)
                    with pe.Else():
                        pe.wait_ge(y_read, T0)
                    down(j + T0 - 1, sl, None, 0)
                    turn_act(j + T0)
                with pe.Fori(begin + 2, end) as j:
                    gate_up(j + T0, sl)
                    turn_x(j + T0 + 1)
                    down(j + T0 - 1, sl, y_row_set, j + 1)
                    turn_act(j + T0)

            pe.wait_ge(dests_set, 1)
            with pe.Fori(0, E // 2) as i:
                expert(i * 2 + 1, 1)
                expert(i * 2 + 2, 0)
            tiles = pe.value_load(spans[0:1, E:E + 1], min_val=E * MIN_TILES, max_val=TE)
            pe.wait_ge(gu_lo, 2 * (E + 2))
            for t in range(T0, T):
                gate_up(tiles + t, 1)
                if t < T - 1:
                    turn_x(tiles + t + 1)
                if t == T0:
                    down(tiles + t - 1, 0, y_row_set, tiles + 1)
                    pe.wait_ge(d_lo, E + 2)
                elif t == T0 + 1:
                    down(tiles + t - 1, 1, y_row_set, tiles + 2)
                else:
                    down(tiles + t - 1, 1, y_read, t - 1)
                turn_act(tiles + t)
            down(tiles + T - 1, 1, y_read, T - 1)


_INS = ["x", "src", "dst", "L0_gnn_W", "L0_gnn_a", "L0_ffn_gate_w", "L0_ffn_correction_bias", "L0_ffn_Wg", "L0_ffn_Wu",
        "L0_ffn_Wd", "L0_ffn_Wg_s", "L0_ffn_Wu_s", "L0_ffn_Wd_s"]


def kernel(**inputs):
    import numpy as np
    import concourse.bacc as bacc
    from concourse.bass_utils import run_bass_kernel_spmd

    nc = bacc.Bacc("TRN2", target_bir_lowering=False, num_devices=1, dynamic_dma_scratch_size=4096)
    arrays, args = {}, []
    for name in _INS:
        a = np.ascontiguousarray(inputs[name])
        arrays[f"in_{name}"] = a
        args.append(nc.dram_tensor(f"in_{name}", a.shape, mybir.dt.from_np(a.dtype), kind="ExternalInput").ap())
    shape = inputs["x"].shape
    args.append(nc.dram_tensor("out", shape, F32, kind="ExternalOutput").ap())
    build(nc, *args)
    r = run_bass_kernel_spmd(nc, [arrays], core_ids=[0])
    return r.results[0]["out"]
```
